# Optimizing a Trainium2 kernel written in Bass

```python
import numpy as np
import jax
import jax.numpy as jnp

def _softmax(x, axis=-1):
    return jax.nn.softmax(x, axis=axis)

def _gelu(x):
    return jax.nn.gelu(x, approximate=True)

def _silu(x):
    return jax.nn.silu(x)

def _sigmoid(x):
    return jax.nn.sigmoid(x)

def _layernorm(x, axis=-1, eps=1e-05):
    m = jnp.mean(x, axis=axis, keepdims=True)
    v = jnp.var(x, axis=axis, keepdims=True)
    return (x - m) / jnp.sqrt(v + eps)

def _scatter_add(tgt, idx, src, axis=0):
    return tgt.at[idx].add(src)

def _segment_sum(src, seg, n):
    return jax.ops.segment_sum(src, seg, n)
kernel_name = 'mk_vit_tower_cls_d2_tok_img1024_r4_02f7ba'

def setup_inputs(seed: int=0):
    np.random.seed(seed)
    _w = jnp.asarray

    def _rec_inputs():
        import jax
        import jax.numpy as jnp
        _rk = jax.random.key(seed)
        x = -0.000222058 + 0.999998 * jax.random.normal(jax.random.fold_in(_rk, 1), (64, 64, 64, 3), jnp.float32)
        cls_tok = 0.02 * jax.random.normal(jax.random.fold_in(_rk, 5), (1, 1, 256), jnp.float32)
        return (x, cls_tok)
    x, cls_tok = _rec_inputs()

    def _L0_tok_setup():
        import jax, jax.numpy as jnp
        import numpy as np
        PATCH = 16
        CHANNELS = 3
        HIDDEN = 256
        key = jax.random.key(seed)
        k1, k2 = jax.random.split(key)
        inputs = jax.random.normal(k1, (32, 128, 128, 3), dtype=jnp.float32)
        fan_in = CHANNELS * PATCH * PATCH
        W = jax.random.normal(k2, (fan_in, HIDDEN), dtype=jnp.float32) / np.sqrt(fan_in)
        return {'inputs': inputs, 'W': W}
    _L0_tok_all = _L0_tok_setup()
    _L0_tok_in = {k: v for k, v in _L0_tok_all.items() if k in ('W',)}
    del _L0_tok_all

    def _L0_attn_setup():
        import jax, jax.numpy as jnp
        import numpy as np
        INPUT_DIM = 256
        D_MODEL = 256
        NUM_HEADS = 16
        D_HEAD = D_MODEL // NUM_HEADS
        key = jax.random.key(seed)
        k_x, k_qkv, k_out = jax.random.split(key, 3)
        x = jax.random.normal(k_x, (4, 512, INPUT_DIM), dtype=jnp.float32)
        lim_qkv = float(np.sqrt(6.0 / (INPUT_DIM + 3 * D_MODEL)))
        W_qkv = jax.random.uniform(k_qkv, (3 * D_MODEL, INPUT_DIM), minval=-lim_qkv, maxval=lim_qkv, dtype=jnp.float32)
        b_qkv = jnp.zeros((3 * D_MODEL,), dtype=jnp.float32)
        lim_out = float(np.sqrt(6.0 / (D_MODEL + D_MODEL)))
        W_out = jax.random.uniform(k_out, (D_MODEL, D_MODEL), minval=-lim_out, maxval=lim_out, dtype=jnp.float32)
        b_out = jnp.zeros((D_MODEL,), dtype=jnp.float32)
        return {'x': x, 'W_qkv': W_qkv, 'b_qkv': b_qkv, 'W_out': W_out, 'b_out': b_out}
    _L0_attn_all = _L0_attn_setup()
    _L0_attn_in = {k: v for k, v in _L0_attn_all.items() if k in ('W_qkv', 'b_qkv', 'W_out', 'b_out')}
    del _L0_attn_all

    def _L0_ffn_setup():
        import jax, jax.numpy as jnp
        import numpy as np
        NUM_HEADS = 16
        TOP_K = 2
        ROPE_BASE = 10000.0
        LN_EPS = 1e-05

        def _rope_sin_cos(S, D, dtype):
            inv_freq = 1.0 / ROPE_BASE ** (jnp.arange(0, D, 2, dtype=jnp.float32) / D)
            freqs = jnp.arange(S, dtype=jnp.float32)[:, None] * inv_freq[None, :]
            sin = jnp.sin(freqs).astype(dtype)[None, :, None, :]
            cos = jnp.cos(freqs).astype(dtype)[None, :, None, :]
            return (sin, cos)

        def _apply_rope(x, sin, cos):
            x1, x2 = (x[..., 0::2], x[..., 1::2])
            r1 = x1 * cos - x2 * sin
            r2 = x1 * sin + x2 * cos
            return jnp.stack([r1, r2], axis=-1).reshape(x.shape)

        def _layer_norm(x, w, b):
            mu = jnp.mean(x, axis=-1, keepdims=True)
            var = jnp.mean(jnp.square(x - mu), axis=-1, keepdims=True)
            return (x - mu) * jax.lax.rsqrt(var + LN_EPS) * w + b
        key = jax.random.key(seed)
        ks = jax.random.split(key, 8)
        B, S, E, NE = (2, 512, 256, 8)
        s = 0.02
        return {'x': jax.random.normal(ks[0], (B, S, E), dtype=jnp.float32), 'in_proj_w': jax.random.normal(ks[1], (3 * E, E), dtype=jnp.float32) * s, 'in_proj_b': jnp.zeros((3 * E,), dtype=jnp.float32), 'out_proj_w': jax.random.normal(ks[2], (E, E), dtype=jnp.float32) * s, 'out_proj_b': jnp.zeros((E,), dtype=jnp.float32), 'gate_w': jax.random.normal(ks[3], (NE, E), dtype=jnp.float32) * s, 'gate_b': jnp.zeros((NE,), dtype=jnp.float32), 'expert_w': jax.random.normal(ks[4], (NE, E, E), dtype=jnp.float32) * s, 'expert_b': jnp.zeros((NE, E), dtype=jnp.float32), 'ln1_w': jnp.ones((E,), dtype=jnp.float32), 'ln1_b': jnp.zeros((E,), dtype=jnp.float32), 'ln2_w': jnp.ones((E,), dtype=jnp.float32), 'ln2_b': jnp.zeros((E,), dtype=jnp.float32)}
    _L0_ffn_all = _L0_ffn_setup()
    _L0_ffn_in = {k: v for k, v in _L0_ffn_all.items() if k in ('in_proj_w', 'in_proj_b', 'out_proj_w', 'out_proj_b', 'gate_w', 'gate_b', 'expert_w', 'expert_b', 'ln1_w', 'ln1_b', 'ln2_w', 'ln2_b')}
    del _L0_ffn_all

    def _L1_attn_setup():
        import jax, jax.numpy as jnp
        import numpy as np
        import math
        NUM_HEADS = 4
        NUM_MEM = 4
        TOPK = 2
        CAPACITY = 0.5
        GATE_NORM = 16.0
        EPS = 1e-05
        B, S, D = (4, 512, 256)
        DK, DV = (128, 256)
        HDK, HDV = (DK // NUM_HEADS, DV // NUM_HEADS)
        LOW = 16

        def _transform(x, routing_mask, sel):
            b, s0, d = x.shape
            k = sel.shape[2]
            xr = jnp.repeat(x, k, axis=1)
            s = s0 * k
            mem_flat = sel.reshape(b, -1).reshape(-1)
            batch_idx = jnp.repeat(jnp.arange(b), s)
            combined = batch_idx * NUM_MEM + mem_flat
            sorted_idx = jnp.argsort(combined)
            x_sorted = xr.reshape(b * s, d)[sorted_idx]
            counts = routing_mask.sum(1)
            offset = jnp.cumsum(counts, axis=1)
            flat_off = (offset + jnp.arange(b)[:, None] * s).reshape(-1)
            cap_len = math.ceil(s0 * CAPACITY)
            prev = jnp.concatenate([jnp.zeros((1,), flat_off.dtype), flat_off[:-1]])
            idx = jnp.arange(cap_len)[None, :] + prev[:, None]
            trunc = idx + counts.reshape(-1)[:, None] - cap_len
            mask = (trunc < flat_off[:, None]) & (trunc >= 0) & (trunc >= prev[:, None])
            trunc = jnp.where(mask, trunc, 0)
            gathered = x_sorted[trunc.reshape(-1)]
            tx = gathered.reshape(b * NUM_MEM, cap_len, d) * mask[..., None]
            tx = tx.reshape(b, NUM_MEM, cap_len, d).transpose(1, 0, 2, 3)
            return (tx, trunc, sorted_idx, mask)

        def _reconstruct(ty, trunc, sorted_idx, rw, mask, b, s0):
            M, _, cap, H, dv = ty.shape
            g = ty.transpose(1, 0, 2, 3, 4).reshape(b * M * cap, H, dv)
            g = g * mask.reshape(-1)[:, None, None]
            res = jnp.zeros((b * s0 * TOPK, H, dv), ty.dtype).at[trunc.reshape(-1)].add(g)
            inv = jnp.argsort(sorted_idx)
            out = res[inv].reshape(b, s0, TOPK, H, dv)
            return (out * rw[..., None, None]).sum(2)

        def _gla(q, k, v, gk):

            def step(Smat, inp):
                qt, kt, vt, gt = inp
                Smat = Smat * jnp.exp(gt)[..., None] + kt[..., None] * vt[..., None, :]
                o = jnp.einsum('...k,...kv->...v', qt, Smat)
                return (Smat, o)
            S0 = jnp.zeros(q.shape[1:-1] + (q.shape[-1], v.shape[-1]), q.dtype)
            _, o = jax.lax.scan(step, S0, (q, k, v, gk))
            return o

        def _forward(x, w_gate, w_q, w_k, w_v, w_gk1, w_gk2, b_gk, w_ks, w_vs, w_gk1s, w_gk2s, b_gks, w_g, w_o, norm_w):
            b, s0, d = x.shape
            scale = HDK ** (-0.5)
            probs = jax.nn.softmax(x @ w_gate, -1)
            rw, sel = jax.lax.top_k(probs, TOPK)
            rw = rw / rw.sum(-1, keepdims=True)
            routing_mask = jax.nn.one_hot(sel, NUM_MEM, dtype=jnp.int32).sum(2)
            tx, trunc, sorted_idx, mask = _transform(x, routing_mask, sel)
            cap = tx.shape[2]
            q = jnp.einsum('mbtd,dk->mbtk', tx, w_q).reshape(NUM_MEM, b, cap, NUM_HEADS, HDK) * scale
            k = jnp.einsum('mbtd,mdk->mbtk', tx, w_k).reshape(NUM_MEM, b, cap, NUM_HEADS, HDK)
            v = jnp.einsum('mbtd,mdk->mbtk', tx, w_v).reshape(NUM_MEM, b, cap, NUM_HEADS, HDV)
            gk = jnp.einsum('mbtr,mrk->mbtk', jnp.einsum('mbtd,mdr->mbtr', tx, w_gk1), w_gk2) + b_gk[:, None, None, :]
            gk = (jax.nn.log_sigmoid(gk) / GATE_NORM).reshape(NUM_MEM, b, cap, NUM_HEADS, HDK)
            to_t = lambda a: jnp.moveaxis(a, 2, 0)
            o_mem = jnp.moveaxis(_gla(to_t(q), to_t(k), to_t(v), to_t(gk)), 0, 2)
            o_rout = _reconstruct(o_mem, trunc, sorted_idx, rw, mask, b, s0)
            qs = (x @ w_q).reshape(b, s0, NUM_HEADS, HDK) * scale
            ks = (x @ w_ks).reshape(b, s0, NUM_HEADS, HDK)
            vs = (x @ w_vs).reshape(b, s0, NUM_HEADS, HDV)
            gks = (jax.nn.log_sigmoid(x @ w_gk1s @ w_gk2s + b_gks) / GATE_NORM).reshape(b, s0, NUM_HEADS, HDK)
            tt = lambda a: jnp.moveaxis(a, 1, 0)
            o_sh = jnp.moveaxis(_gla(tt(qs), tt(ks), tt(vs), tt(gks)), 0, 1)
            o = o_rout + o_sh
            g = (x @ w_g).reshape(b, s0, NUM_HEADS, HDV)
            o = o * jax.lax.rsqrt(jnp.mean(o * o, -1, keepdims=True) + EPS) * norm_w
            o = o * (g * jax.nn.sigmoid(g))
            return o.reshape(b, s0, DV) @ w_o
        key = jax.random.key(seed)
        ks = jax.random.split(key, 17)
        n = lambda i, shp: 0.02 * jax.random.normal(ks[i], shp, dtype=jnp.float32)
        return {'x': jax.random.normal(ks[0], (B, S, D), dtype=jnp.float32), 'w_gate': n(1, (D, NUM_MEM)), 'w_q': n(2, (D, DK)), 'w_k': n(3, (NUM_MEM, D, DK)), 'w_v': n(4, (NUM_MEM, D, DV)), 'w_gk1': n(5, (NUM_MEM, D, LOW)), 'w_gk2': n(6, (NUM_MEM, LOW, DK)), 'b_gk': n(7, (NUM_MEM, DK)), 'w_ks': n(8, (D, DK)), 'w_vs': n(9, (D, DV)), 'w_gk1s': n(10, (D, LOW)), 'w_gk2s': n(11, (LOW, DK)), 'b_gks': n(12, (DK,)), 'w_g': n(13, (D, DV)), 'w_o': n(14, (DV, D)), 'norm_w': jnp.ones((HDV,), dtype=jnp.float32)}
    _L1_attn_all = _L1_attn_setup()
    _L1_attn_in = {k: v for k, v in _L1_attn_all.items() if k in ('w_gate', 'w_q', 'w_k', 'w_v', 'w_gk1', 'w_gk2', 'b_gk', 'w_ks', 'w_vs', 'w_gk1s', 'w_gk2s', 'b_gks', 'w_g', 'w_o', 'norm_w')}
    del _L1_attn_all

    def _L1_ffn_setup():
        import jax, jax.numpy as jnp
        import numpy as np
        TOP_K = 2
        EPS = 1e-20
        key = jax.random.key(seed)
        ks = jax.random.split(key, 8)
        B, S, H, E, D = (4, 512, 256, 8, 512)
        s = 0.02
        return {'x': jax.random.normal(ks[0], (B, S, H), dtype=jnp.float32), 'Wr': jax.random.normal(ks[1], (H, E), dtype=jnp.float32) * s, 'Wg': jax.random.normal(ks[2], (E, H, D), dtype=jnp.float32) * s, 'Wu': jax.random.normal(ks[3], (E, H, D), dtype=jnp.float32) * s, 'Wd': jax.random.normal(ks[4], (E, D, H), dtype=jnp.float32) * s, 'Sg': jax.random.normal(ks[5], (H, D), dtype=jnp.float32) * s, 'Su': jax.random.normal(ks[6], (H, D), dtype=jnp.float32) * s, 'Sd': jax.random.normal(ks[7], (D, H), dtype=jnp.float32) * s}
    _L1_ffn_all = _L1_ffn_setup()
    _L1_ffn_in = {k: v for k, v in _L1_ffn_all.items() if k in ('Wr', 'Wg', 'Wu', 'Wd', 'Sg', 'Su', 'Sd')}
    del _L1_ffn_all
    return {'x': x, 'cls_tok': cls_tok, 'L0_tok_W': _L0_tok_in['W'], 'L0_attn_W_qkv': _L0_attn_in['W_qkv'], 'L0_attn_b_qkv': _L0_attn_in['b_qkv'], 'L0_attn_W_out': _L0_attn_in['W_out'], 'L0_attn_b_out': _L0_attn_in['b_out'], 'L0_ffn_in_proj_w': _L0_ffn_in['in_proj_w'], 'L0_ffn_in_proj_b': _L0_ffn_in['in_proj_b'], 'L0_ffn_out_proj_w': _L0_ffn_in['out_proj_w'], 'L0_ffn_out_proj_b': _L0_ffn_in['out_proj_b'], 'L0_ffn_gate_w': _L0_ffn_in['gate_w'], 'L0_ffn_gate_b': _L0_ffn_in['gate_b'], 'L0_ffn_expert_w': _L0_ffn_in['expert_w'], 'L0_ffn_expert_b': _L0_ffn_in['expert_b'], 'L0_ffn_ln1_w': _L0_ffn_in['ln1_w'], 'L0_ffn_ln1_b': _L0_ffn_in['ln1_b'], 'L0_ffn_ln2_w': _L0_ffn_in['ln2_w'], 'L0_ffn_ln2_b': _L0_ffn_in['ln2_b'], 'L1_attn_w_gate': _L1_attn_in['w_gate'], 'L1_attn_w_q': _L1_attn_in['w_q'], 'L1_attn_w_k': _L1_attn_in['w_k'], 'L1_attn_w_v': _L1_attn_in['w_v'], 'L1_attn_w_gk1': _L1_attn_in['w_gk1'], 'L1_attn_w_gk2': _L1_attn_in['w_gk2'], 'L1_attn_b_gk': _L1_attn_in['b_gk'], 'L1_attn_w_ks': _L1_attn_in['w_ks'], 'L1_attn_w_vs': _L1_attn_in['w_vs'], 'L1_attn_w_gk1s': _L1_attn_in['w_gk1s'], 'L1_attn_w_gk2s': _L1_attn_in['w_gk2s'], 'L1_attn_b_gks': _L1_attn_in['b_gks'], 'L1_attn_w_g': _L1_attn_in['w_g'], 'L1_attn_w_o': _L1_attn_in['w_o'], 'L1_attn_norm_w': _L1_attn_in['norm_w'], 'L1_ffn_Wr': _L1_ffn_in['Wr'], 'L1_ffn_Wg': _L1_ffn_in['Wg'], 'L1_ffn_Wu': _L1_ffn_in['Wu'], 'L1_ffn_Wd': _L1_ffn_in['Wd'], 'L1_ffn_Sg': _L1_ffn_in['Sg'], 'L1_ffn_Su': _L1_ffn_in['Su'], 'L1_ffn_Sd': _L1_ffn_in['Sd']}

def reference(x, cls_tok, L0_tok_W, L0_attn_W_qkv, L0_attn_b_qkv, L0_attn_W_out, L0_attn_b_out, L0_ffn_in_proj_w, L0_ffn_in_proj_b, L0_ffn_out_proj_w, L0_ffn_out_proj_b, L0_ffn_gate_w, L0_ffn_gate_b, L0_ffn_expert_w, L0_ffn_expert_b, L0_ffn_ln1_w, L0_ffn_ln1_b, L0_ffn_ln2_w, L0_ffn_ln2_b, L1_attn_w_gate, L1_attn_w_q, L1_attn_w_k, L1_attn_w_v, L1_attn_w_gk1, L1_attn_w_gk2, L1_attn_b_gk, L1_attn_w_ks, L1_attn_w_vs, L1_attn_w_gk1s, L1_attn_w_gk2s, L1_attn_b_gks, L1_attn_w_g, L1_attn_w_o, L1_attn_norm_w, L1_ffn_Wr, L1_ffn_Wg, L1_ffn_Wu, L1_ffn_Wd, L1_ffn_Sg, L1_ffn_Su, L1_ffn_Sd):
    import jax
    import jax.numpy as jnp

    def _L0_tok_ref(inputs, W):
        import jax, jax.numpy as jnp
        import numpy as np
        PATCH = 16
        CHANNELS = 3
        HIDDEN = 256
        if inputs.shape[1] == CHANNELS and inputs.shape[-1] != CHANNELS:
            inputs = jnp.transpose(inputs, (0, 2, 3, 1))
        b, h, w, c = inputs.shape
        p = PATCH
        patches = inputs.reshape(b, h // p, p, w // p, p, c)
        patches = jnp.transpose(patches, (0, 1, 3, 2, 4, 5))
        patches = patches.reshape(b, -1, p * p * c)
        return jnp.einsum('bnf,fh->bnh', patches, W)

    def _L0_attn_ref(x, W_qkv, b_qkv, W_out, b_out):
        import jax, jax.numpy as jnp
        import numpy as np
        INPUT_DIM = 256
        D_MODEL = 256
        NUM_HEADS = 16
        D_HEAD = D_MODEL // NUM_HEADS
        B, S, _ = x.shape
        qkv = jnp.einsum('bsi,oi->bso', x, W_qkv) + b_qkv
        qkv = qkv.reshape(B, S, NUM_HEADS, 3 * D_HEAD).transpose(0, 2, 1, 3)
        q, k, v = jnp.split(qkv, 3, axis=-1)
        scale = 1.0 / jnp.sqrt(jnp.asarray(D_HEAD, dtype=x.dtype))
        logits = jnp.einsum('bhqd,bhkd->bhqk', q, k) * scale
        attn = jax.nn.softmax(logits, axis=-1)
        values = jnp.einsum('bhqk,bhkd->bhqd', attn, v)
        values = values.transpose(0, 2, 1, 3).reshape(B, S, D_MODEL)
        out = jnp.einsum('bsd,od->bso', values, W_out) + b_out
        return out

    def _L0_ffn_ref(x, in_proj_w, in_proj_b, out_proj_w, out_proj_b, gate_w, gate_b, expert_w, expert_b, ln1_w, ln1_b, ln2_w, ln2_b):
        import jax, jax.numpy as jnp
        import numpy as np
        NUM_HEADS = 16
        TOP_K = 2
        ROPE_BASE = 10000.0
        LN_EPS = 1e-05

        def _rope_sin_cos(S, D, dtype):
            inv_freq = 1.0 / ROPE_BASE ** (jnp.arange(0, D, 2, dtype=jnp.float32) / D)
            freqs = jnp.arange(S, dtype=jnp.float32)[:, None] * inv_freq[None, :]
            sin = jnp.sin(freqs).astype(dtype)[None, :, None, :]
            cos = jnp.cos(freqs).astype(dtype)[None, :, None, :]
            return (sin, cos)

        def _apply_rope(x, sin, cos):
            x1, x2 = (x[..., 0::2], x[..., 1::2])
            r1 = x1 * cos - x2 * sin
            r2 = x1 * sin + x2 * cos
            return jnp.stack([r1, r2], axis=-1).reshape(x.shape)

        def _layer_norm(x, w, b):
            mu = jnp.mean(x, axis=-1, keepdims=True)
            var = jnp.mean(jnp.square(x - mu), axis=-1, keepdims=True)
            return (x - mu) * jax.lax.rsqrt(var + LN_EPS) * w + b
        B, S, E = x.shape
        H = NUM_HEADS
        D = E // H
        xh = x.reshape(B, S, H, D)
        sin, cos = _rope_sin_cos(S, D, x.dtype)
        q_in = _apply_rope(xh, sin, cos).reshape(B, S, E)
        k_in = q_in
        v_in = x
        Wq, Wk, Wv = jnp.split(in_proj_w, 3, axis=0)
        bq, bk, bv = jnp.split(in_proj_b, 3, axis=0)
        q = (q_in @ Wq.T + bq).reshape(B, S, H, D)
        k = (k_in @ Wk.T + bk).reshape(B, S, H, D)
        v = (v_in @ Wv.T + bv).reshape(B, S, H, D)
        scale = 1.0 / jnp.sqrt(jnp.asarray(D, dtype=x.dtype))
        scores = jnp.einsum('bqhd,bkhd->bhqk', q, k) * scale
        causal = jnp.tril(jnp.ones((S, S), dtype=bool))
        scores = jnp.where(causal[None, None], scores, jnp.asarray(-jnp.inf, dtype=scores.dtype))
        attn = jax.nn.softmax(scores, axis=-1)
        ctx = jnp.einsum('bhqk,bkhd->bqhd', attn, v).reshape(B, S, E)
        attn_out = ctx @ out_proj_w.T + out_proj_b
        x1 = _layer_norm(x + attn_out, ln1_w, ln1_b)
        gates = jax.nn.softmax(x1 @ gate_w.T + gate_b, axis=-1)
        _, top_idx = jax.lax.top_k(gates, TOP_K)
        top_gates = jnp.take_along_axis(gates, top_idx, axis=-1)
        expert_outputs = jnp.einsum('bsd,efd->bsef', x1, expert_w) + expert_b[None, None]
        sel = jnp.take_along_axis(expert_outputs, top_idx[..., None], axis=2)
        moe_out = jnp.sum(sel * top_gates[..., None], axis=2)
        return _layer_norm(x1 + moe_out, ln2_w, ln2_b)

    def _L1_attn_ref(x, w_gate, w_q, w_k, w_v, w_gk1, w_gk2, b_gk, w_ks, w_vs, w_gk1s, w_gk2s, b_gks, w_g, w_o, norm_w):
        import jax, jax.numpy as jnp
        import numpy as np
        import math
        NUM_HEADS = 4
        NUM_MEM = 4
        TOPK = 2
        CAPACITY = 0.5
        GATE_NORM = 16.0
        EPS = 1e-05
        B, S, D = (4, 512, 256)
        DK, DV = (128, 256)
        HDK, HDV = (DK // NUM_HEADS, DV // NUM_HEADS)
        LOW = 16

        def _transform(x, routing_mask, sel):
            b, s0, d = x.shape
            k = sel.shape[2]
            xr = jnp.repeat(x, k, axis=1)
            s = s0 * k
            mem_flat = sel.reshape(b, -1).reshape(-1)
            batch_idx = jnp.repeat(jnp.arange(b), s)
            combined = batch_idx * NUM_MEM + mem_flat
            sorted_idx = jnp.argsort(combined)
            x_sorted = xr.reshape(b * s, d)[sorted_idx]
            counts = routing_mask.sum(1)
            offset = jnp.cumsum(counts, axis=1)
            flat_off = (offset + jnp.arange(b)[:, None] * s).reshape(-1)
            cap_len = math.ceil(s0 * CAPACITY)
            prev = jnp.concatenate([jnp.zeros((1,), flat_off.dtype), flat_off[:-1]])
            idx = jnp.arange(cap_len)[None, :] + prev[:, None]
            trunc = idx + counts.reshape(-1)[:, None] - cap_len
            mask = (trunc < flat_off[:, None]) & (trunc >= 0) & (trunc >= prev[:, None])
            trunc = jnp.where(mask, trunc, 0)
            gathered = x_sorted[trunc.reshape(-1)]
            tx = gathered.reshape(b * NUM_MEM, cap_len, d) * mask[..., None]
            tx = tx.reshape(b, NUM_MEM, cap_len, d).transpose(1, 0, 2, 3)
            return (tx, trunc, sorted_idx, mask)

        def _reconstruct(ty, trunc, sorted_idx, rw, mask, b, s0):
            M, _, cap, H, dv = ty.shape
            g = ty.transpose(1, 0, 2, 3, 4).reshape(b * M * cap, H, dv)
            g = g * mask.reshape(-1)[:, None, None]
            res = jnp.zeros((b * s0 * TOPK, H, dv), ty.dtype).at[trunc.reshape(-1)].add(g)
            inv = jnp.argsort(sorted_idx)
            out = res[inv].reshape(b, s0, TOPK, H, dv)
            return (out * rw[..., None, None]).sum(2)

        def _gla(q, k, v, gk):

            def step(Smat, inp):
                qt, kt, vt, gt = inp
                Smat = Smat * jnp.exp(gt)[..., None] + kt[..., None] * vt[..., None, :]
                o = jnp.einsum('...k,...kv->...v', qt, Smat)
                return (Smat, o)
            S0 = jnp.zeros(q.shape[1:-1] + (q.shape[-1], v.shape[-1]), q.dtype)
            _, o = jax.lax.scan(step, S0, (q, k, v, gk))
            return o

        def _forward(x, w_gate, w_q, w_k, w_v, w_gk1, w_gk2, b_gk, w_ks, w_vs, w_gk1s, w_gk2s, b_gks, w_g, w_o, norm_w):
            b, s0, d = x.shape
            scale = HDK ** (-0.5)
            probs = jax.nn.softmax(x @ w_gate, -1)
            rw, sel = jax.lax.top_k(probs, TOPK)
            rw = rw / rw.sum(-1, keepdims=True)
            routing_mask = jax.nn.one_hot(sel, NUM_MEM, dtype=jnp.int32).sum(2)
            tx, trunc, sorted_idx, mask = _transform(x, routing_mask, sel)
            cap = tx.shape[2]
            q = jnp.einsum('mbtd,dk->mbtk', tx, w_q).reshape(NUM_MEM, b, cap, NUM_HEADS, HDK) * scale
            k = jnp.einsum('mbtd,mdk->mbtk', tx, w_k).reshape(NUM_MEM, b, cap, NUM_HEADS, HDK)
            v = jnp.einsum('mbtd,mdk->mbtk', tx, w_v).reshape(NUM_MEM, b, cap, NUM_HEADS, HDV)
            gk = jnp.einsum('mbtr,mrk->mbtk', jnp.einsum('mbtd,mdr->mbtr', tx, w_gk1), w_gk2) + b_gk[:, None, None, :]
            gk = (jax.nn.log_sigmoid(gk) / GATE_NORM).reshape(NUM_MEM, b, cap, NUM_HEADS, HDK)
            to_t = lambda a: jnp.moveaxis(a, 2, 0)
            o_mem = jnp.moveaxis(_gla(to_t(q), to_t(k), to_t(v), to_t(gk)), 0, 2)
            o_rout = _reconstruct(o_mem, trunc, sorted_idx, rw, mask, b, s0)
            qs = (x @ w_q).reshape(b, s0, NUM_HEADS, HDK) * scale
            ks = (x @ w_ks).reshape(b, s0, NUM_HEADS, HDK)
            vs = (x @ w_vs).reshape(b, s0, NUM_HEADS, HDV)
            gks = (jax.nn.log_sigmoid(x @ w_gk1s @ w_gk2s + b_gks) / GATE_NORM).reshape(b, s0, NUM_HEADS, HDK)
            tt = lambda a: jnp.moveaxis(a, 1, 0)
            o_sh = jnp.moveaxis(_gla(tt(qs), tt(ks), tt(vs), tt(gks)), 0, 1)
            o = o_rout + o_sh
            g = (x @ w_g).reshape(b, s0, NUM_HEADS, HDV)
            o = o * jax.lax.rsqrt(jnp.mean(o * o, -1, keepdims=True) + EPS) * norm_w
            o = o * (g * jax.nn.sigmoid(g))
            return o.reshape(b, s0, DV) @ w_o
        return _forward(x, w_gate, w_q, w_k, w_v, w_gk1, w_gk2, b_gk, w_ks, w_vs, w_gk1s, w_gk2s, b_gks, w_g, w_o, norm_w)

    def _L1_ffn_ref(x, Wr, Wg, Wu, Wd, Sg, Su, Sd):
        import jax, jax.numpy as jnp
        import numpy as np
        TOP_K = 2
        EPS = 1e-20
        B, S, H = x.shape
        T = B * S
        xt = x.reshape(T, H)
        scores = jax.nn.softmax(xt @ Wr, axis=-1)
        topk_w, topk_idx = jax.lax.top_k(scores, TOP_K)
        topk_w = topk_w / (topk_w.sum(axis=-1, keepdims=True) + EPS)
        g = jax.nn.silu(jnp.einsum('th,ehd->etd', xt, Wg))
        u = jnp.einsum('th,ehd->etd', xt, Wu)
        out_all = jnp.einsum('etd,edh->eth', g * u, Wd)
        tok = jnp.arange(T)[:, None]
        gathered = out_all[topk_idx, tok, :]
        out = jnp.sum(gathered * topk_w[..., None], axis=1).reshape(B, S, H)
        shared = jax.nn.silu(x @ Sg) * (x @ Su) @ Sd
        return out + shared
    h = _L0_tok_ref(x, L0_tok_W)
    h = jnp.concatenate([jnp.broadcast_to(cls_tok, (h.shape[0], 1, h.shape[2])), h], axis=1)
    h = h + _L0_attn_ref(_layernorm(h, axis=-1), L0_attn_W_qkv, L0_attn_b_qkv, L0_attn_W_out, L0_attn_b_out)
    h = h + _L0_ffn_ref(_layernorm(h, axis=-1), L0_ffn_in_proj_w, L0_ffn_in_proj_b, L0_ffn_out_proj_w, L0_ffn_out_proj_b, L0_ffn_gate_w, L0_ffn_gate_b, L0_ffn_expert_w, L0_ffn_expert_b, L0_ffn_ln1_w, L0_ffn_ln1_b, L0_ffn_ln2_w, L0_ffn_ln2_b)
    h = h + _L1_attn_ref(_layernorm(h, axis=-1), L1_attn_w_gate, L1_attn_w_q, L1_attn_w_k, L1_attn_w_v, L1_attn_w_gk1, L1_attn_w_gk2, L1_attn_b_gk, L1_attn_w_ks, L1_attn_w_vs, L1_attn_w_gk1s, L1_attn_w_gk2s, L1_attn_b_gks, L1_attn_w_g, L1_attn_w_o, L1_attn_norm_w)
    h = h + _L1_ffn_ref(_layernorm(h, axis=-1), L1_ffn_Wr, L1_ffn_Wg, L1_ffn_Wu, L1_ffn_Wd, L1_ffn_Sg, L1_ffn_Su, L1_ffn_Sd)
    return h

_drawn_inputs = setup_inputs


def setup_inputs(seed=0):
    import zlib

    import numpy as np

    out = dict(_drawn_inputs(seed))
    spreads = {'L0_attn_b_qkv': (0.0, 0.1),
     'L0_attn_b_out': (0.0, 0.1),
     'L0_ffn_in_proj_b': (0.0, 0.446),
     'L0_ffn_out_proj_b': (0.0, 0.1),
     'L0_ffn_gate_b': (0.0, 0.328),
     'L0_ffn_expert_b': (0.0, 0.634),
     'L0_ffn_ln1_w': (1.0, 0.2),
     'L0_ffn_ln1_b': (0.0, 0.1),
     'L0_ffn_ln2_w': (1.0, 0.2),
     'L0_ffn_ln2_b': (0.0, 0.1),
     'L1_attn_norm_w': (1.0, 0.6)}
    factors = {'L1_attn_w_gate': 4.946,
     'L1_attn_w_k': 4.283,
     'L1_attn_w_v': 4.331,
     'L1_attn_w_gk1': 8.0,
     'L1_attn_w_gk2': 38.804,
     'L1_attn_b_gk': 132.554,
     'L1_attn_w_gk1s': 173.938,
     'L1_attn_w_gk2s': 200.0,
     'L1_attn_b_gks': 200.0,
     'L1_ffn_Wr': 7.865,
     'L1_ffn_Wg': 6.855,
     'L1_ffn_Wu': 6.808,
     'L1_ffn_Wd': 6.795,
     'L1_ffn_Sg': 4.888,
     'L1_ffn_Su': 4.809,
     'L1_ffn_Sd': 4.815}
    for name, (base, spread) in spreads.items():
        noise = np.random.default_rng([zlib.crc32(name.encode()), seed]).standard_normal(out[name].shape)
        drawn = base * np.exp(spread * noise) if base else spread * noise
        out[name] = jnp.asarray(drawn.astype(out[name].dtype))
    for name, factor in factors.items():
        out[name] = (out[name] * factor).astype(out[name].dtype)
    return out
```

```python
from contextlib import ExitStack

import concourse.bass as bass
from concourse import mybir

F32 = mybir.dt.float32
BF16 = mybir.dt.bfloat16
U32 = mybir.dt.uint32
ALU = mybir.AluOpType
ACT = mybir.ActivationFunctionType
AX = mybir.AxisListType

B, PATCHES, S = 64, 16, 17
E = 256
KC = E // 128
FEAT = 768
FC = FEAT // 128
SEQS = 7
TOK = SEQS * S
GROUPS = -(-B // SEQS)
PAIRS = GROUPS // 2
H0, D0 = 16, 16
NE0 = 8
H1, DK, DV = 4, 32, 64
MEM, CAP, LOW = 4, 9, 16
SLOT = 64
PAIRM = MEM // 2
NE1, FF = 8, 512
EPS = 1e-5
FAR = -1e30
GATE_NORM = 16.0
QSCALE1 = float(DK) ** -0.5
DM = MEM * CAP * SLOT
DALL = DM + S * TOK

TILES = (2 * B * S + NE1 * 127) // 128
FULL = -(-B * S // 128)
EW = 2 * KC * FF + (FF // 128) * E
PACKS = {
    "tok": [("ident", 128), ("w_tok", FC * E), ("cls", E), ("is_cls", TOK)],
    "l0": [("wqk0", KC * 2 * E), ("wv0", KC * E), ("wo0", KC * E), ("bqk0", 4), ("bv0", E), ("bo0", E),
           ("headmask", 8),
           ("wqk1", KC * 2 * E), ("wv1", KC * E), ("wo1", KC * E), ("bqk1", 4), ("bv1", E), ("bo1", E),
           ("rope_cos", E), ("rope_sin", 128)],
    "l0f": [("w_gate0", KC * NE0), ("b_gate0", NE0), ("w_exp0", KC * NE0 * E), ("b_exp0", E),
            ("ln1_w", E), ("ln1_b", E), ("ln2_w", E), ("ln2_b", E), ("iota8", NE0)],
    "l1": [("w_gate1", KC * MEM), ("w_g", KC * E), ("wq", KC * 128), ("wks", KC * 128), ("wvs", KC * E),
           ("wgk1s", KC * LOW), ("wgk2s", 128), ("wk", KC * MEM * 128), ("wv", KC * MEM * E),
           ("wgk1", KC * MEM * LOW), ("wgk2", MEM * 128), ("bgk", MEM + 1), ("w_o", KC * E),
           ("norm_w", E), ("upto", TOK), ("same", TOK), ("seq9", 1), ("iota64", SLOT), ("keep", MEM * SLOT + TOK),
           ("hsel", H1), ("bmask9", SEQS), ("bmask17", SEQS),
           ("w_r", KC * NE1), ("sg", KC * FF), ("su", KC * FF), ("sd", (FF // 128) * E)],
}
PACKS["route"] = [("turner", 128), ("tri", TOK), ("ones", TOK), ("eight", NE1), ("valid", GROUPS), ("step_g", NE1 * GROUPS), ("step_e", NE1),
                  ("fills", FULL), ("tile_no", TILES)]
WIDTH = {k: sum(w for _, w in v) for k, v in PACKS.items()}


def view(ap, off, *dims):
    return bass.AP(ap.tensor, ap.offset + off, [list(ap.ap[0])] + [list(d) for d in dims])


class Steps:

    def __init__(self, eng, sem):
        self.eng, self.sem = eng, sem
        self.n, self.last = 0, {0: 0, 1: 0}

    def mark(self, ins, u):
        ins.then_inc(self.sem, 1)
        self.n += 1
        self.last[u] = self.n

    def wait(self, u):
        self.eng.wait_ge(self.sem, self.last[u])

    def end(self):
        self.eng.wait_ge(self.sem, self.n)
        self.eng.sem_clear(self.sem)



def tower_kernel(nc, xp_d, packs_d, masks_d, experts_d, x_d, xs_d, y_d, out_d):
    with ExitStack() as ctx, ExitStack() as phase1:
        def keep(name, shape, dt=F32):
            return ctx.enter_context(nc.sbuf_tensor(name, shape, dt))

        def sb(name, shape, dt=F32):
            return phase1.enter_context(nc.sbuf_tensor(name, shape, dt))

        def sem(name):
            return ctx.enter_context(nc.semaphore(name))

        PS = [ctx.enter_context(nc.psum_tensor(f"ps{u}", [128, 4, 512], F32)) for u in (0, 1)]
        pack = {"route": keep("pack_route", [128, WIDTH["route"]])}
        h_all = keep("h_all", [128, GROUPS, E])
        picked = keep("picked", [128, GROUPS * 4])
        pack |= {k: sb(f"pack_{k}", [128, w]) for k, w in WIDTH.items() if k != "route"}
        C = {}
        for k, parts in PACKS.items():
            at = 0
            for name, w in parts:
                C[name] = pack[k][:, at:at + w]
                at += w
        masks = sb("masks", [128, 2 * TOK + 128], BF16)
        identb = masks[:, 2 * TOK:]
        zeros = sb("zeros", [128, E])
        Dp = sb("pair_exponents", [128, DALL])
        half = sb("half", [128, 5])

        def two(name, shape, dt=F32):
            return [sb(f"{name}{u}", shape, dt) for u in (0, 1)]

        xp = two("patches", [128, FC * TOK])
        h = two("h", [128, E])
        xn = two("xn", [128, E])
        xa = two("xa", [128, E])
        hb = two("hb", [128, E])
        xT = two("xT", [128, 4 * TOK])
        vS = two("v_ones", [128, H0 * (D0 + 1)])
        cT = two("cT", [128, TOK])
        qS, kS = two("q_shared", [128, TOK]), two("k_shared", [128, TOK])
        vsh = two("v_shared", [128, E])
        gs = two("silu_g", [128, E])
        ohT = two("combineT", [128, PAIRM * TOK])
        qP = two("q_mem", [128, MEM * CAP * SEQS])
        kM = two("k_mem", [128, MEM * SLOT])
        vM = two("v_mem", [128, PAIRM * E])
        Gc = two("decay_sums", [128, MEM * SLOT + TOK])
        AbM = two("a_mem", [128, PAIRM * H1 * 128])
        st, mv, ve, rstd = two("st", [128, 6]), two("mv", [128, 2]), two("ve", [128, 1]), two("rstd", [128, 1])
        lg, d8, pr, pr4, mx8 = (two(n, [128, 8]) for n in ("lg", "d8", "pr", "pr4", "mx8"))
        ix = two("ix", [128, 8], U32)
        ixf = two("ixf", [128, 2])
        mxs, ssum, rsum = two("mxs", [128, 1]), two("ssum", [128, 1]), two("rsum", [128, 1])
        mxh = two("mxh", [128, H0])
        rden = two("rden", [128, H0])
        c0, c1, cw = two("c0", [128, 8]), two("c1", [128, 8]), two("cw", [128, 8])
        p12, rp = two("p12", [128, 1]), two("rp", [128, 1])
        rt, w2, t9, s1, vd, code = (two(n, [128, 4]) for n in ("rt", "w2", "t9", "s1", "vd", "code"))
        ms, mse, rs4 = (two(n, [128, 4]) for n in ("ms", "mse", "rs4"))
        U = two("area", [128, DALL])
        SC = H0 * TOK
        dA = [U[u][:, 0:SC] for u in (0, 1)]
        kPT = [U[u][:, SC:2 * SC] for u in (0, 1)]
        qT = [U[u][:, 2 * SC:2 * SC + 2 * TOK] for u in (0, 1)]
        kT = [U[u][:, 2 * SC + 2 * TOK:2 * SC + 4 * TOK] for u in (0, 1)]
        o = [U[u][:, 2 * SC:2 * SC + E] for u in (0, 1)]
        rr = [U[u][:, SC:SC + E] for u in (0, 1)]
        rq = [U[u][:, SC + E:SC + 2 * E] for u in (0, 1)]
        acc = [U[u][:, 0:E] for u in (0, 1)]
        NZ = MEM * SLOT + TOK
        xg = [U[u][:, 0:512] for u in (0, 1)]
        z1M = [U[u][:, 512:768] for u in (0, 1)]
        z1S = [U[u][:, 768:768 + TOK] for u in (0, 1)]
        OH = [U[u][:, 1024:1280] for u in (0, 1)]
        OHw = [U[u][:, 1280:1536] for u in (0, 1)]
        zz = [U[u][:, 1536:1536 + NZ] for u in (0, 1)]
        az = [U[u][:, 1536 + NZ:1536 + 2 * NZ] for u in (0, 1)]
        lgz = [U[u][:, 1536 + 2 * NZ:1536 + 3 * NZ] for u in (0, 1)]
        egs = [U[u][:, 3000:3256] for u in (0, 1)]
        AbS = [U[u][:, 0:H1 * TOK] for u in (0, 1)]
        oM = [U[u][:, 512:1024] for u in (0, 1)]
        oS = [U[u][:, 1024:1280] for u in (0, 1)]
        sq = [U[u][:, 1280:1536] for u in (0, 1)]
        eg = [U[u][:, 1536:2048] for u in (0, 1)]
        hm = [U[u][:, 2048:2560] for u in (0, 1)]
        hmT = [U[u][:, 2560:2560 + 4 * TOK] for u in (0, 1)]

        x_landed = [sem(f"x_landed{u}") for u in (0, 1)]
        tok_used = [sem(f"tok_used{u}") for u in (0, 1)]
        done = [sem(f"done{u}") for u in (0, 1)]
        landed = {k: sem(f"landed_{k}") for k in [*PACKS, "masks"]}
        out_stored = sem("out_stored")
        x_stored = [sem(f"x_stored{u}") for u in (0, 1)]
        cleared = sem("rows_cleared")
        dve_step, act_step, pool_step, pool_ready = sem("dve_step"), sem("act_step"), sem("pool_step"), sem("pool_ready")
        (stats, rstd_ready, norm, turned, turn_copied, qkv, qk_copied, km_ready, v_copied, scores, shifted,
         exped, p_turned, pt_act, pt_dve, av, attended, res_ready, projected, gate, logits, softmaxed,
         roped, experts, exp_read, c_ready, c_turned, c_copied, bias_ready, affine, g_prod, sh_prod, vs_prod,
         sh_copied, g_exped, routed, counted, onehot, weighted, gathered, xg_copied, oh_turned, oh_copied,
         z1_prod, z1_copied, qm_prod, qm_copied, vm_prod, z2_prod, zabs, lned, exponents, dexped, mem_prod,
         sh_pairs, a_prod, a_spread, om_prod, om_copied, o_prod, gated, gw_ready, up_prod, ff_exped, inner_ready,
         inner_turned, inner_copied, rms_ms, rms_ready, xf_norm) = (sem(n) for n in (
            "stats", "rstd_ready", "norm", "turned", "turn_copied", "qkv", "qk_copied", "km_ready", "v_copied",
            "scores", "shifted", "exped", "p_turned", "pt_act", "pt_dve", "av", "attended", "res_ready",
            "projected", "gate", "logits", "softmaxed", "roped", "experts", "exp_read", "c_ready", "c_turned",
            "c_copied", "bias_ready", "affine", "g_prod", "sh_prod", "vs_prod", "sh_copied", "g_exped", "routed",
            "counted", "onehot", "weighted", "gathered", "xg_copied", "oh_turned", "oh_copied", "z1_prod",
            "z1_copied", "qm_prod", "qm_copied", "vm_prod", "z2_prod", "zabs", "lned", "exponents", "dexped",
            "mem_prod", "sh_pairs", "a_prod", "a_spread", "om_prod", "om_copied", "o_prod", "gated", "gw_ready",
            "up_prod", "ff_exped", "inner_ready", "inner_turned", "inner_copied", "rms_ms", "rms_ready", "xf_norm"))

        def nth(i, k, per_group, u):
            return i * (2 * per_group) + 2 * k + u + 1

        LN, TURN = 6, 8
        UU = (0, 1)
        block_ctx = ExitStack()
        block = block_ctx.enter_context(nc.Block())

        @block.sync
        def _(sp):
            sp.dma_start(pack["tok"][:], packs_d["tok"]).then_inc(landed["tok"], 16)
            for u in UU:
                sp.dma_start(xp[u][:], xp_d[u]).then_inc(x_landed[u], 16)
            sp.dma_start(masks[:], masks_d).then_inc(landed["masks"], 16)
            for k in ("l0", "l0f", "l1", "route"):
                sp.dma_start(pack[k][:], packs_d[k]).then_inc(landed[k], 16)
            sp.wait_ge(pool_ready, 1)
            for j in range(TILES):
                sp.dma_start(xs_d[j * 128:(j + 1) * 128, :], zeros[:]).then_inc(cleared, 16)

            def store_inputs(i):
                for u in UU:
                    sp.wait_ge(norm, nth(i, 5, LN, u))
                    sp.dma_start(x_d[bass.ds((2 * i + u) * TOK, TOK), :], xn[u][:TOK, :]).then_inc(x_stored[u], 16)

            with sp.Fori(0, PAIRS - 1) as i:
                for u in UU:
                    sp.wait_ge(tok_used[u], i + 1)
                    sp.dma_start(xp[u][:], xp_d[bass.ds(2 * i + 2 + u, 1)].rearrange("o p f -> (o p) f")).then_inc(x_landed[u], 16)
                store_inputs(i)
            store_inputs(PAIRS - 1)
            for u in UU:
                sp.wait_ge(x_stored[u], (PAIRS + 1) * 16)
            sp.wait_ge(cleared, TILES * 16)

        @block.tensor
        def _(pe):
            mm, tp = nc.tensor.matmul, nc.tensor.transpose
            pe.wait_ge(landed["tok"], 16)
            with pe.Fori(0, PAIRS) as i:
                def turn(k, src, n):
                    for u in UU:
                        for c in range(n):
                            s = src(u, c)
                            last = tp(PS[u][:, 3, c * TOK:(c + 1) * TOK], s, C["ident"][:TOK, :TOK])
                        last.then_inc(turned, 1)

                for u in UU:
                    pe.wait_ge(x_landed[u], (i + 1) * 16)
                    pe.wait_ge(done[u], i + 1)
                    mm(PS[u][:TOK, 0, 0:E], C["is_cls"][0:1, :], C["cls"][0:1, :], start=True, stop=False)
                    for c in range(FC):
                        last = mm(PS[u][:TOK, 0, 0:E], xp[u][:, c * TOK:(c + 1) * TOK], C["w_tok"][:, c * E:(c + 1) * E],
                                  start=False, stop=(c == FC - 1))
                    last.then_inc(tok_used[u], 1)

                for k in (0, 1):
                    if k == 0:
                        for u in UU:
                            pe.wait_ge(norm, nth(i, 0, LN, u))
                            tp(PS[u][:, 3, 0:TOK], xn[u][:TOK, 0:128], C["ident"][:TOK, :TOK])
                            tp(PS[u][:, 3, TOK:2 * TOK], xn[u][:TOK, 128:256], C["ident"][:TOK, :TOK]).then_inc(turned, 1)
                        pe.wait_ge(landed["l0"], 16)
                        pe.wait_ge(landed["masks"], 16)
                    else:
                        for u in UU:
                            pe.wait_ge(norm, nth(i, 1, LN, u))
                            pe.wait_ge(roped, nth(i, 0, 1, u))
                            for c in range(4):
                                s = (xa[u] if c < 2 else rr[u])[:TOK, (c % 2) * 128:(c % 2 + 1) * 128]
                                last = tp(PS[u][:, 3, c * TOK:(c + 1) * TOK], s, C["ident"][:TOK, :TOK])
                            last.then_inc(turned, 1)
                    for u in UU:
                        pe.wait_ge(turn_copied, nth(i, 2 * k, TURN, u))
                        qk_at = 2 * k
                        for j in range(4):
                            for c in range(KC):
                                w = C[f"wqk{k}"][:, c * 2 * E + j * 128:c * 2 * E + (j + 1) * 128]
                                mm(PS[u][:, j // 2, (j % 2) * TOK:(j % 2 + 1) * TOK], w,
                                   xT[u][:, (qk_at + c) * TOK:(qk_at + c + 1) * TOK], start=(c == 0), stop=(c == KC - 1))
                        for c in range(KC):
                            last = mm(PS[u][:TOK, 2, 0:E], xT[u][:, c * TOK:(c + 1) * TOK],
                                      C[f"wv{k}"][:, c * E:(c + 1) * E], start=(c == 0), stop=(c == KC - 1))
                        last.then_inc(qkv, 1)
                    for u in UU:
                        pe.wait_ge(km_ready, nth(i, k, 2, u))
                        pe.wait_ge(v_copied, nth(i, k, 2, u))
                        for b in range(4):
                            mm(view(PS[u][:TOK, b, :], 0, [TOK, 4], [1, TOK]), identb[:TOK, :TOK],
                               view(masks[:TOK], k * TOK, [0, 4], [1, TOK]), start=True, stop=False)
                            last = mm(PS[u][:TOK, b, 0:4 * TOK], qT[u][:, (b // 2) * TOK:(b // 2 + 1) * TOK],
                                      kPT[u][:, b * 4 * TOK:(b + 1) * 4 * TOK], start=False, stop=True)
                        last.then_inc(scores, 1)
                    for u in UU:
                        pe.wait_ge(exped, nth(i, k, 2, u))
                        for hd in range(H0):
                            last = tp(PS[u][:TOK, hd // 4, (hd % 4) * TOK:(hd % 4 + 1) * TOK],
                                      dA[u][:TOK, hd * TOK:(hd + 1) * TOK], C["ident"][:TOK, :TOK])
                            if hd % 8 == 7:
                                last.then_inc(p_turned, 1)
                    for u in UU:
                        pe.wait_ge(pt_act, nth(i, k, 2, u))
                        pe.wait_ge(pt_dve, nth(i, k, 2, u))
                        W = D0 + 1
                        for hd in range(H0):
                            last = mm(PS[u][:TOK, 0, hd * W:(hd + 1) * W], kPT[u][:TOK, hd * TOK:(hd + 1) * TOK],
                                      vS[u][:TOK, hd * W:(hd + 1) * W], start=True, stop=True)
                        last.then_inc(av, 1)
                    for u in UU:
                        pe.wait_ge(attended, nth(i, k, 2, u))
                        for c in range(KC):
                            last = tp(PS[u][:, 3, c * TOK:(c + 1) * TOK], o[u][:TOK, c * 128:(c + 1) * 128], C["ident"][:TOK, :TOK])
                        last.then_inc(turned, 1)
                    for u in UU:
                        pe.wait_ge(turn_copied, nth(i, 2 * k + 1, TURN, u))
                        for c in range(KC):
                            last = mm(PS[u][:TOK, 1, 0:E], xT[u][:, c * TOK:(c + 1) * TOK],
                                      C[f"wo{k}"][:, c * E:(c + 1) * E], start=(c == 0), stop=(c == KC - 1))
                        last.then_inc(projected, 1)

                pe.wait_ge(landed["l0f"], 16)
                for u in UU:
                    pe.wait_ge(affine, nth(i, 0, 2, u))
                    for c in range(KC):
                        last = tp(PS[u][:, 3, c * TOK:(c + 1) * TOK], xa[u][:TOK, c * 128:(c + 1) * 128], C["ident"][:TOK, :TOK])
                    last.then_inc(turned, 1)
                for u in UU:
                    pe.wait_ge(turn_copied, nth(i, 4, TURN, u))
                    for c in range(KC):
                        last = mm(PS[u][:TOK, 0, 0:NE0], xT[u][:, c * TOK:(c + 1) * TOK],
                                  C["w_gate0"][:, c * NE0:(c + 1) * NE0], start=(c == 0), stop=(c == KC - 1))
                    last.then_inc(gate, 1)
                for j in range(4):
                    for u in UU:
                        if j == 3:
                            pe.wait_ge(exp_read, nth(i, 0, 4, u))
                        for c in range(KC):
                            last = mm(PS[u][:TOK, 1 + j % 3, :], xT[u][:, c * TOK:(c + 1) * TOK],
                                      C["w_exp0"][:, c * NE0 * E + j * 512:c * NE0 * E + (j + 1) * 512],
                                      start=(c == 0), stop=(c == KC - 1))
                        last.then_inc(experts, 1)
                for u in UU:
                    pe.wait_ge(c_ready, nth(i, 0, 1, u))
                    tp(PS[u][:NE0, 0, 128:128 + TOK], cw[u][:TOK, :], C["ident"][:TOK, :TOK]).then_inc(c_turned, 1)
                for u in UU:
                    pe.wait_ge(c_copied, nth(i, 0, 1, u))
                    mm(PS[u][:TOK, 0, 256:512], cT[u][:NE0, :], C["b_exp0"][:NE0, :], start=True, stop=True).then_inc(bias_ready, 1)

                pe.wait_ge(landed["l1"], 16)
                for u in UU:
                    pe.wait_ge(norm, nth(i, 4, LN, u))
                    for c in range(KC):
                        last = tp(PS[u][:, 3, c * TOK:(c + 1) * TOK], xn[u][:TOK, c * 128:(c + 1) * 128], C["ident"][:TOK, :TOK])
                    last.then_inc(turned, 1)
                for u in UU:
                    pe.wait_ge(turn_copied, nth(i, 5, TURN, u))
                    x0 = [xT[u][:, c * TOK:(c + 1) * TOK] for c in range(KC)]
                    for c in range(KC):
                        last = mm(PS[u][:TOK, 0, 0:MEM], x0[c], C["w_gate1"][:, c * MEM:(c + 1) * MEM], start=(c == 0), stop=(c == KC - 1))
                    last.then_inc(gate, 1)
                    for c in range(KC):
                        last = mm(PS[u][:TOK, 1, 0:E], x0[c], C["w_g"][:, c * E:(c + 1) * E], start=(c == 0), stop=(c == KC - 1))
                    last.then_inc(g_prod, 1)
                    for n, (w, m) in enumerate((("wq", 128), ("wks", 128), ("wgk1s", LOW))):
                        for c in range(KC):
                            last = mm(PS[u][:m, 2, n * TOK:(n + 1) * TOK], C[w][:, c * m:(c + 1) * m], x0[c], start=(c == 0), stop=(c == KC - 1))
                    last.then_inc(sh_prod, 1)
                    for c in range(KC):
                        last = mm(PS[u][:TOK, 3, 0:E], x0[c], C["wvs"][:, c * E:(c + 1) * E], start=(c == 0), stop=(c == KC - 1))
                    last.then_inc(vs_prod, 1)
                for u in UU:
                    pe.wait_ge(routed, nth(i, 0, 1, u))
                    mm(PS[u][:TOK, 0, 8:8 + MEM], C["upto"][:TOK, :], rt[u][:TOK, :], start=True, stop=True)
                    mm(PS[u][:TOK, 0, 12:12 + MEM], C["same"][:TOK, :], rt[u][:TOK, :], start=True, stop=True).then_inc(counted, 1)
                for u in UU:
                    pe.wait_ge(onehot, nth(i, 0, 1, u))
                    for c in range(KC):
                        last = mm(PS[u][:, 1, c * 256:(c + 1) * 256], xn[u][:TOK, c * 128:(c + 1) * 128], OH[u][:TOK, :], start=True, stop=True)
                    last.then_inc(gathered, 1)
                for u in UU:
                    pe.wait_ge(weighted, nth(i, 0, 1, u))
                    for c in range(PAIRM):
                        last = tp(PS[u][:, 3, c * TOK:(c + 1) * TOK], OHw[u][:TOK, c * 128:(c + 1) * 128], C["ident"][:TOK, :TOK])
                    last.then_inc(oh_turned, 1)
                for u in UU:
                    pe.wait_ge(xg_copied, nth(i, 0, 1, u))
                    for m in range(MEM):
                        for c in range(KC):
                            last = mm(PS[u][:LOW, 0, m * SLOT:(m + 1) * SLOT], C["wgk1"][:, (c * MEM + m) * LOW:(c * MEM + m + 1) * LOW],
                                      xg[u][:, c * 256 + m * SLOT:c * 256 + (m + 1) * SLOT], start=(c == 0), stop=(c == KC - 1))
                    last.then_inc(z1_prod, 1)
                    for c in range(KC):
                        mm(PS[u][:, 1, 0:256], C["wq"][:, c * 128:(c + 1) * 128], xg[u][:, c * 256:(c + 1) * 256], start=(c == 0), stop=(c == KC - 1))
                    for m in range(MEM):
                        for c in range(KC):
                            last = mm(PS[u][:, 1, 256 + m * SLOT:256 + (m + 1) * SLOT], C["wk"][:, (c * MEM + m) * 128:(c * MEM + m + 1) * 128],
                                      xg[u][:, c * 256 + m * SLOT:c * 256 + (m + 1) * SLOT], start=(c == 0), stop=(c == KC - 1))
                    last.then_inc(qm_prod, 1)
                    for m in range(MEM):
                        for c in range(KC):
                            p = (m % 2) * SLOT
                            last = mm(PS[u][p:p + SLOT, 2, (m // 2) * E:(m // 2 + 1) * E],
                                      xg[u][:, c * 256 + m * SLOT:c * 256 + (m + 1) * SLOT],
                                      C["wv"][:, (c * MEM + m) * E:(c * MEM + m + 1) * E], start=(c == 0), stop=(c == KC - 1),
                                      skip_group_check=True)
                    last.then_inc(vm_prod, 1)
                for u in UU:
                    pe.wait_ge(z1_copied, nth(i, 0, 1, u))
                    pe.wait_ge(oh_copied, nth(i, 0, 1, u))
                    for m in range(MEM):
                        mm(PS[u][:, 3, m * SLOT:(m + 1) * SLOT], C["wgk2"][:LOW, m * 128:(m + 1) * 128], z1M[u][:LOW, m * SLOT:(m + 1) * SLOT], start=True, stop=True)
                    mm(PS[u][:, 3, 256:256 + TOK], C["wgk2s"][:LOW, :], z1S[u][:LOW, :], start=True, stop=True).then_inc(z2_prod, 1)
                for u in UU:
                    pe.wait_ge(mem_prod, nth(i, 0, 1, u))
                    for mp in range(PAIRM):
                        for t in range(CAP):
                            mm(PS[u][:, 0, mp * 36 + 4 * t:mp * 36 + 4 * t + 4],
                               U[u][:, t * MEM * SLOT + mp * 128:t * MEM * SLOT + (mp + 1) * 128], C["hsel"], start=True, stop=True)
                    pe.wait_ge(sh_pairs, nth(i, 0, 1, u))
                    for t in range(S):
                        last = mm(PS[u][:TOK, 0, 72 + 4 * t:76 + 4 * t], U[u][:, DM + t * TOK:DM + (t + 1) * TOK], C["hsel"], start=True, stop=True)
                    last.then_inc(a_prod, 1)
                for u in UU:
                    pe.wait_ge(a_spread, nth(i, 0, 1, u))
                    for mp in range(PAIRM):
                        for hd in range(H1):
                            last = mm(PS[u][:, 1, mp * E + hd * DV:mp * E + (hd + 1) * DV], AbM[u][:, (mp * H1 + hd) * 128:(mp * H1 + hd + 1) * 128],
                                      vM[u][:, mp * E + hd * DV:mp * E + (hd + 1) * DV], start=True, stop=True)
                    last.then_inc(om_prod, 1)
                for u in UU:
                    pe.wait_ge(om_copied, nth(i, 0, 1, u))
                    for mp in range(PAIRM):
                        mm(PS[u][:TOK, 2, 0:E], ohT[u][:, mp * TOK:(mp + 1) * TOK], oM[u][:, mp * E:(mp + 1) * E],
                           start=(mp == 0), stop=False, skip_group_check=True)
                    for hd in range(H1):
                        last = mm(PS[u][:TOK, 2, hd * DV:(hd + 1) * DV], AbS[u][:TOK, hd * TOK:(hd + 1) * TOK],
                                  vsh[u][:TOK, hd * DV:(hd + 1) * DV], start=False, stop=(hd == H1 - 1), skip_group_check=True)
                    last.then_inc(o_prod, 1)
                for u in UU:
                    pe.wait_ge(gated, nth(i, 0, 1, u))
                    for c in range(KC):
                        last = tp(PS[u][:, 3, c * TOK:(c + 1) * TOK], oS[u][:TOK, c * 128:(c + 1) * 128], C["ident"][:TOK, :TOK])
                    last.then_inc(turned, 1)
                for u in UU:
                    pe.wait_ge(turn_copied, nth(i, 6, TURN, u))
                    for c in range(KC):
                        last = mm(PS[u][:TOK, 1, 0:E], xT[u][:, c * TOK:(c + 1) * TOK], C["w_o"][:, c * E:(c + 1) * E], start=(c == 0), stop=(c == KC - 1))
                    last.then_inc(projected, 1)
                for u in UU:
                    pe.wait_ge(norm, nth(i, 5, LN, u))
                    for c in range(KC):
                        last = tp(PS[u][:, 3, c * TOK:(c + 1) * TOK], xn[u][:TOK, c * 128:(c + 1) * 128], C["ident"][:TOK, :TOK])
                    last.then_inc(turned, 1)
                for u in UU:
                    pe.wait_ge(turn_copied, nth(i, 7, TURN, u))
                    x0 = [xT[u][:, c * TOK:(c + 1) * TOK] for c in range(KC)]
                    for c in range(KC):
                        last = mm(PS[u][:TOK, 0, 0:NE1], x0[c], C["w_r"][:, c * NE1:(c + 1) * NE1], start=(c == 0), stop=(c == KC - 1))
                    last.then_inc(gate, 1)
                    for n, w in enumerate(("sg", "su")):
                        for c in range(KC):
                            last = mm(PS[u][:TOK, 1 + n, :], x0[c], C[w][:, c * FF:(c + 1) * FF], start=(c == 0), stop=(c == KC - 1))
                    last.then_inc(up_prod, 1)
                for u in UU:
                    pe.wait_ge(inner_ready, nth(i, 0, 1, u))
                    for c in range(4):
                        last = tp(PS[u][:, 3, c * TOK:(c + 1) * TOK], hm[u][:TOK, c * 128:(c + 1) * 128], C["ident"][:TOK, :TOK])
                    last.then_inc(inner_turned, 1)
                for u in UU:
                    pe.wait_ge(inner_copied, nth(i, 0, 1, u))
                    for c in range(4):
                        last = mm(PS[u][:TOK, 1, 0:E], hmT[u][:, c * TOK:(c + 1) * TOK], C["sd"][:, c * E:(c + 1) * E], start=(c == 0), stop=(c == 3))
                    last.then_inc(projected, 1)

        @block.scalar
        def _(act):
            A = nc.scalar.activation
            nc.scalar.preload_act_table_set("natural_log_exp_and_others")
            act.wait_ge(landed["l0"], 16)
            act.wait_ge(landed["l1"], 16)
            with act.Fori(0, PAIRS) as i:
                own = Steps(act, act_step)

                def copy_turn(k, n):
                    for u in UU:
                        act.wait_ge(turned, nth(i, k, TURN, u))
                        A(xT[u][:, 0:n * TOK], PS[u][:, 3, 0:n * TOK], ACT.Copy).then_inc(turn_copied, 1)

                def softmax_exp(k, n, dst):
                    for u in UU:
                        act.wait_ge(logits, nth(i, k, 3, u))
                        A(dst[u][:TOK, 0:n], d8[u][:TOK, 0:n], ACT.Exp, accum_out=ssum[u][:TOK, :]).then_inc(softmaxed, 1)

                for k in (0, 1):
                    copy_turn(2 * k, 2 + 2 * k)
                    for u in UU:
                        act.wait_ge(qkv, nth(i, k, 2, u))
                        for j in range(4):
                            dst = (qT if j < 2 else kT)[u]
                            last = A(dst[:, (j % 2) * TOK:(j % 2 + 1) * TOK], PS[u][:, j // 2, (j % 2) * TOK:(j % 2 + 1) * TOK],
                                     ACT.Identity, bias=C[f"bqk{k}"][:, j:j + 1])
                        last.then_inc(qk_copied, 1)
                    for u in UU:
                        act.wait_ge(shifted, nth(i, k, 2, u))
                        A(dA[u][:TOK, :], dA[u][:TOK, :], ACT.Exp, scale=float(D0) ** -0.5).then_inc(exped, 1)
                    for u in UU:
                        act.wait_ge(p_turned, i * 8 + 4 * k + 2 * u + 1)
                        A(view(kPT[u][:TOK], 0, [4 * TOK, 2], [1, 4 * TOK]), view(PS[u][:TOK, 0, :], 0, [512, 2], [1, 4 * TOK]), ACT.Copy).then_inc(pt_act, 1)
                    copy_turn(2 * k + 1, 2)
                copy_turn(4, 2)
                softmax_exp(0, NE0, pr)
                for u in UU:
                    act.wait_ge(c_turned, nth(i, 0, 1, u))
                    A(cT[u][:NE0, :], PS[u][:NE0, 0, 128:128 + TOK], ACT.Copy).then_inc(c_copied, 1)
                copy_turn(5, 2)
                softmax_exp(1, MEM, pr4)
                for u in UU:
                    act.wait_ge(sh_prod, nth(i, 0, 1, u))
                    A(qS[u][:], PS[u][:, 2, 0:TOK], ACT.Copy, scale=QSCALE1)
                    A(kS[u][:], PS[u][:, 2, TOK:2 * TOK], ACT.Copy)
                    A(z1S[u][:LOW, :], PS[u][:LOW, 2, 2 * TOK:3 * TOK], ACT.Copy).then_inc(sh_copied, 1)
                    act.wait_ge(g_prod, nth(i, 0, 1, u))
                    A(egs[u][:TOK, :], PS[u][:TOK, 1, 0:E], ACT.Exp, scale=-1.0).then_inc(g_exped, 1)
                for u in UU:
                    act.wait_ge(gathered, nth(i, 0, 1, u))
                    A(xg[u][:], PS[u][:, 1, :], ACT.Copy).then_inc(xg_copied, 1)
                for u in UU:
                    act.wait_ge(oh_turned, nth(i, 0, 1, u))
                    A(ohT[u][:], PS[u][:, 3, 0:PAIRM * TOK], ACT.Copy).then_inc(oh_copied, 1)
                for u in UU:
                    act.wait_ge(z1_prod, nth(i, 0, 1, u))
                    A(z1M[u][:LOW, :], PS[u][:LOW, 0, 0:256], ACT.Copy).then_inc(z1_copied, 1)
                for u in UU:
                    act.wait_ge(qm_prod, nth(i, 0, 1, u))
                    A(view(qP[u][:], 0, [SEQS, MEM], [1, SEQS], [MEM * SEQS, CAP]), view(PS[u][:, 1, :], 0, [SLOT, MEM], [CAP, SEQS], [1, CAP]),
                      ACT.Copy, scale=QSCALE1)
                    A(kM[u][:], PS[u][:, 1, 256:512], ACT.Copy).then_inc(qm_copied, 1)
                for u in UU:
                    act.wait_ge(zabs, nth(i, 0, 1, u))
                    own.mark(A(az[u], az[u], ACT.Exp, scale=-1.0), u)
                for u in UU:
                    own.wait(u)
                    A(az[u], az[u], ACT.Ln, bias=1.0).then_inc(lned, 1)
                for u in UU:
                    act.wait_ge(exponents, nth(i, 0, 1, u))
                    A(U[u][:], Dp[:], ACT.Exp, scale=1.0 / GATE_NORM).then_inc(dexped, 1)
                for u in UU:
                    act.wait_ge(om_prod, nth(i, 0, 1, u))
                    A(oM[u][:], PS[u][:, 1, :], ACT.Copy).then_inc(om_copied, 1)
                copy_turn(6, 2)
                copy_turn(7, 2)
                softmax_exp(2, NE1, pr)
                for u in UU:
                    act.wait_ge(up_prod, nth(i, 0, 1, u))
                    A(eg[u][:TOK, :], PS[u][:TOK, 1, :], ACT.Exp, scale=-1.0).then_inc(ff_exped, 1)
                for u in UU:
                    act.wait_ge(inner_turned, nth(i, 0, 1, u))
                    A(hmT[u][:], PS[u][:, 3, 0:4 * TOK], ACT.Copy).then_inc(inner_copied, 1)
                own.end()

        @block.gpsimd
        def _(pool):
            G = nc.gpsimd
            for u in UU:
                G.memset(vS[u][:], 1.0)
                G.memset(pr4[u][:], -1.0)
                G.memset(AbM[u][:], 0.0)
            G.memset(half[:, 0:4], -0.5)
            G.memset(half[:, 4:5], EPS)
            G.memset(zeros[:], 0.0)
            G.memset(Dp[:], FAR).then_inc(pool_ready, 1)
            for u in UU:
                pool.sem_inc(done[u], 1)
                pool.sem_inc(x_stored[u], 16)
            pool.sem_inc(dexped, 1)
            pool.wait_ge(pool_ready, 1)
            for k in ("l0", "l0f", "l1"):
                pool.wait_ge(landed[k], 16)
            with pool.Fori(0, PAIRS) as i:
                own = Steps(pool, pool_step)

                def inverse_root(k):
                    for u in UU:
                        pool.wait_ge(stats, nth(i, k, LN, u))
                        own.mark(G.tensor_tensor(ve[u][:TOK, :], mv[u][:TOK, 1:2], half[:TOK, 4:5], ALU.add), u)
                    for u in UU:
                        own.wait(u)
                        G.tensor_tensor(rstd[u][:TOK, :], ve[u][:TOK, :], half[:TOK, 0:1], ALU.pow).then_inc(rstd_ready, 1)

                def keys_by_head(k):
                    for u in UU:
                        pool.wait_ge(qk_copied, nth(i, k, 2, u))
                        for c in range(2):
                            last = G.tensor_tensor(view(kPT[u], c * 8 * TOK, [TOK, 8], [1, TOK]), view(kT[u], c * TOK, [0, 8], [1, TOK]),
                                                   view(C["headmask"], 0, [1, 8], [0, TOK]), ALU.mult)
                        last.then_inc(km_ready, 1)

                def affine_norm(k, w, b):
                    for u in UU:
                        pool.wait_ge(norm, nth(i, 2 + k, LN, u))
                        own.mark(G.tensor_tensor(xn[u][:TOK, :], xn[u][:TOK, :], C[w][:TOK, :], ALU.mult), u)
                    for u in UU:
                        own.wait(u)
                        if k == 0:
                            G.tensor_tensor(xa[u][:TOK, :], xn[u][:TOK, :], C[b][:TOK, :], ALU.add).then_inc(affine, 1)
                        else:
                            own.mark(G.tensor_tensor(xn[u][:TOK, :], xn[u][:TOK, :], C[b][:TOK, :], ALU.add), u)

                inverse_root(0)
                for u in UU:
                    pool.wait_ge(norm, nth(i, 0, LN, u))
                    G.tensor_tensor(hb[u][:TOK, :], h[u][:TOK, :], C["bo0"][:TOK, :], ALU.add).then_inc(res_ready, 1)
                keys_by_head(0)
                inverse_root(1)
                for u in UU:
                    pool.wait_ge(norm, nth(i, 1, LN, u))
                    G.tensor_tensor(rq[u][:TOK, :], xa[u][:TOK, :], C["rope_cos"][:TOK, :], ALU.mult)
                    G.tensor_tensor(view(rr[u][:TOK], 0, [2, 128]), view(xa[u][:TOK], 1, [2, 128]), C["rope_sin"][:TOK, :], ALU.mult)
                    own.mark(G.tensor_tensor(view(rr[u][:TOK], 1, [2, 128]), view(xa[u][:TOK], 0, [2, 128]), C["rope_sin"][:TOK, :], ALU.mult), u)
                for u in UU:
                    own.wait(u)
                    own.mark(G.tensor_tensor(view(rr[u][:TOK], 0, [2, 128]), view(rq[u][:TOK], 0, [2, 128]), view(rr[u][:TOK], 0, [2, 128]), ALU.subtract), u)
                    G.tensor_tensor(view(rr[u][:TOK], 1, [2, 128]), view(rq[u][:TOK], 1, [2, 128]), view(rr[u][:TOK], 1, [2, 128]), ALU.add).then_inc(roped, 1)
                    G.tensor_tensor(hb[u][:TOK, :], xa[u][:TOK, :], C["bo1"][:TOK, :], ALU.add).then_inc(res_ready, 1)
                keys_by_head(1)
                inverse_root(2)
                affine_norm(0, "ln1_w", "ln1_b")
                inverse_root(3)
                affine_norm(1, "ln2_w", "ln2_b")
                for u in UU:
                    own.wait(u)
                    G.tensor_tensor(h[u][:TOK, :], h[u][:TOK, :], xn[u][:TOK, :], ALU.add).then_inc(affine, 1)
                inverse_root(4)
                for u in UU:
                    pool.wait_ge(onehot, nth(i, 0, 1, u))
                    G.tensor_tensor(view(OHw[u][:TOK], 0, [SLOT, MEM], [1, SLOT]), view(OH[u][:TOK], 0, [SLOT, MEM], [1, SLOT]),
                                    view(w2[u][:TOK], 0, [1, MEM], [0, SLOT]), ALU.mult).then_inc(weighted, 1)
                    own.mark(G.tensor_tensor(gs[u][:TOK, :], gs[u][:TOK, :], C["norm_w"][:TOK, :], ALU.mult), u)
                for u in UU:
                    pool.wait_ge(dexped, nth(i, 0, 1, u) + 1)
                    e = view(U[u][:], DM, [TOK, S], [1, TOK])
                    own.mark(G.tensor_tensor(e, e, view(kS[u][:], 0, [0, S], [1, TOK]), ALU.mult), u)
                    own.wait(u)
                    e = view(U[u][:], DM, [TOK, S], [S, SEQS], [1, S])
                    G.tensor_tensor(e, e, view(qS[u][:], 0, [1, S], [S, SEQS], [0, S]), ALU.mult).then_inc(sh_pairs, 1)
                for u in UU:
                    pool.wait_ge(rms_ms, nth(i, 0, 1, u))
                    G.tensor_tensor(rs4[u][:TOK, :], mse[u][:TOK, :], half[:TOK, 0:4], ALU.pow).then_inc(rms_ready, 1)
                inverse_root(5)
                own.end()

        @block.vector
        def _(dve):
            V = nc.vector
            TT, TS, STT = V.tensor_tensor, V.tensor_scalar, V.scalar_tensor_tensor
            dve.wait_ge(pool_ready, 1)
            for k in ("l0", "l0f", "l1"):
                dve.wait_ge(landed[k], 16)
            with dve.Fori(0, PAIRS) as i:
                own = Steps(dve, dve_step)
                mark, wait = own.mark, own.wait

                def layer_norm(k, src, dst):
                    for u in UU:
                        wait(u)
                        mark(V.bn_stats(st[u][:TOK, :], src[u][:TOK, :]), u)
                    for u in UU:
                        wait(u)
                        V.bn_aggr(mv[u][:TOK, :], st[u][:TOK, :]).then_inc(stats, 1)
                    for u in UU:
                        dve.wait_ge(rstd_ready, nth(i, k, LN, u))
                        TS(dst[u][:TOK, :], src[u][:TOK, :], mv[u][:TOK, 0:1], rstd[u][:TOK, :], ALU.subtract, ALU.mult).then_inc(norm, 1)

                def top_two(k, n, p):
                    for u in UU:
                        wait(u)
                        mark(V.tensor_reduce(mxs[u][:TOK, :], lg[u][:TOK, 0:n], AX.X, ALU.max), u)
                    for u in UU:
                        wait(u)
                        TS(d8[u][:TOK, 0:n], lg[u][:TOK, 0:n], mxs[u][:TOK, :], None, ALU.subtract).then_inc(logits, 1)
                    for u in UU:
                        dve.wait_ge(softmaxed, nth(i, k, 3, u))
                        mark(V.reciprocal(rsum[u][:TOK, :], ssum[u][:TOK, :]), u)
                    for u in UU:
                        wait(u)
                        mark(TS(p[u][:TOK, 0:n], p[u][:TOK, 0:n], rsum[u][:TOK, :], None, ALU.mult), u)
                    for u in UU:
                        wait(u)
                        mark(V.max(mx8[u][:TOK, :], p[u][:TOK, :]), u)
                    for u in UU:
                        wait(u)
                        mark(V.max_index(ix[u][:TOK, :], mx8[u][:TOK, :], p[u][:TOK, :]), u)
                    for u in UU:
                        wait(u)
                        mark(V.tensor_copy(ixf[u][:TOK, :], ix[u][:TOK, 0:2]), u)
                    for u in UU:
                        wait(u)
                        STT(c0[u][:TOK, 0:n], C["iota8"][:TOK, 0:n], ixf[u][:TOK, 0:1], p[u][:TOK, 0:n], ALU.is_equal, ALU.mult)
                        mark(STT(c1[u][:TOK, 0:n], C["iota8"][:TOK, 0:n], ixf[u][:TOK, 1:2], p[u][:TOK, 0:n], ALU.is_equal, ALU.mult), u)

                for u in UU:
                    dve.wait_ge(x_stored[u], (i + 1) * 16)
                    dve.wait_ge(tok_used[u], i + 1)
                    mark(V.tensor_copy(h[u][:TOK, :], PS[u][:TOK, 0, 0:E]), u)
                layer_norm(0, h, xn)
                for k in (0, 1):
                    for u in UU:
                        dve.wait_ge(qkv, nth(i, k, 2, u))
                        TT(view(vS[u][:TOK], 0, [D0 + 1, H0], [1, D0]), view(PS[u][:TOK, 2, :], 0, [D0, H0], [1, D0]),
                           view(C[f"bv{k}"][:TOK], 0, [D0, H0], [1, D0]), ALU.add).then_inc(v_copied, 1)
                    for u in UU:
                        dve.wait_ge(scores, nth(i, k, 2, u))
                        s = view(PS[u][:TOK, 0, :], 0, [512, 4], [TOK, 4], [1, TOK])
                        mark(V.tensor_reduce(mxh[u][:TOK, :], s, AX.X, ALU.max), u)
                        wait(u)
                        TT(view(dA[u][:TOK], 0, [4 * TOK, 4], [TOK, 4], [1, TOK]), s, view(mxh[u][:TOK], 0, [4, 4], [1, 4], [0, TOK]),
                           ALU.subtract).then_inc(shifted, 1)
                    for u in UU:
                        dve.wait_ge(p_turned, i * 8 + 4 * k + 2 * u + 2)
                        V.tensor_copy(view(kPT[u][:TOK], 8 * TOK, [4 * TOK, 2], [1, 4 * TOK]),
                                      view(PS[u][:TOK, 2, :], 0, [512, 2], [1, 4 * TOK])).then_inc(pt_dve, 1)
                    for u in UU:
                        dve.wait_ge(av, nth(i, k, 2, u))
                        mark(V.reciprocal(rden[u][:TOK, :], view(PS[u][:TOK, 0, :], D0, [D0 + 1, H0])), u)
                    for u in UU:
                        wait(u)
                        TT(view(o[u][:TOK], 0, [D0, H0], [1, D0]), view(PS[u][:TOK, 0, :], 0, [D0 + 1, H0], [1, D0]),
                           view(rden[u][:TOK], 0, [1, H0], [0, D0]), ALU.mult).then_inc(attended, 1)
                    for u in UU:
                        dve.wait_ge(projected, nth(i, k, 4, u))
                        dve.wait_ge(res_ready, nth(i, k, 2, u))
                        dst = (h, xn)[k]
                        mark(TT(dst[u][:TOK, :], PS[u][:TOK, 1, 0:E], hb[u][:TOK, :], ALU.add), u)
                    if k == 0:
                        layer_norm(1, h, xa)
                    else:
                        layer_norm(2, xn, xn)

                for u in UU:
                    dve.wait_ge(gate, nth(i, 0, 3, u))
                    mark(TT(lg[u][:TOK, :], PS[u][:TOK, 0, 0:NE0], C["b_gate0"][:TOK, :], ALU.add), u)
                top_two(0, NE0, pr)
                for u in UU:
                    wait(u)
                    TT(cw[u][:TOK, :], c0[u][:TOK, :], c1[u][:TOK, :], ALU.add).then_inc(c_ready, 1)
                for j in range(4):
                    for e in range(2):
                        for u in UU:
                            if j == 0 and e == 0:
                                dve.wait_ge(c_ready, nth(i, 0, 1, u))
                            else:
                                wait(u)
                            if e == 0:
                                dve.wait_ge(experts, nth(i, j, 4, u))
                            ins = STT(acc[u][:TOK, :], PS[u][:TOK, 1 + j % 3, e * E:(e + 1) * E], cw[u][:TOK, 2 * j + e:2 * j + e + 1],
                                      (xa if (j, e) == (0, 0) else acc)[u][:TOK, :], ALU.mult, ALU.add)
                            mark(ins, u)
                            if e == 1:
                                wait(u)
                                V.tensor_copy(vd[u][:TOK, 0:1], cw[u][:TOK, 0:1]).then_inc(exp_read, 1)
                for u in UU:
                    dve.wait_ge(bias_ready, nth(i, 0, 1, u))
                    mark(TT(acc[u][:TOK, :], acc[u][:TOK, :], PS[u][:TOK, 0, 256:512], ALU.add), u)
                layer_norm(3, acc, xn)
                for u in UU:
                    dve.wait_ge(affine, nth(i, 1, 2, u))
                layer_norm(4, h, xn)

                for u in UU:
                    dve.wait_ge(gate, nth(i, 1, 3, u))
                    mark(V.tensor_copy(lg[u][:TOK, 0:MEM], PS[u][:TOK, 0, 0:MEM]), u)
                top_two(1, MEM, pr4)
                for u in UU:
                    mark(TT(p12[u][:TOK, :], mx8[u][:TOK, 0:1], mx8[u][:TOK, 1:2], ALU.add), u)
                for u in UU:
                    wait(u)
                    mark(V.reciprocal(rp[u][:TOK, :], p12[u][:TOK, :]), u)
                for u in UU:
                    mark(TT(w2[u][:TOK, :], c0[u][:TOK, 0:MEM], c1[u][:TOK, 0:MEM], ALU.add), u)
                for u in UU:
                    wait(u)
                    mark(TS(w2[u][:TOK, :], w2[u][:TOK, :], rp[u][:TOK, :], None, ALU.mult), u)
                for u in UU:
                    mark(TS(t9[u][:TOK, :], C["iota8"][:TOK, 0:MEM], ixf[u][:TOK, 0:1], None, ALU.is_equal), u)
                    wait(u)
                    STT(rt[u][:TOK, :], C["iota8"][:TOK, 0:MEM], ixf[u][:TOK, 1:2], t9[u][:TOK, :], ALU.is_equal, ALU.add).then_inc(routed, 1)
                for u in UU:
                    dve.wait_ge(vs_prod, nth(i, 0, 1, u))
                    V.tensor_copy(vsh[u][:TOK, :], PS[u][:TOK, 3, 0:E])
                    dve.wait_ge(g_exped, nth(i, 0, 1, u))
                    mark(TS(egs[u][:TOK, :], egs[u][:TOK, :], 1.0, None, ALU.add), u)
                for u in UU:
                    wait(u)
                    mark(V.reciprocal(egs[u][:TOK, :], egs[u][:TOK, :]), u)
                for u in UU:
                    wait(u)
                    mark(TT(gs[u][:TOK, :], PS[u][:TOK, 1, 0:E], egs[u][:TOK, :], ALU.mult), u)
                for u in UU:
                    dve.wait_ge(counted, nth(i, 0, 1, u))
                    mark(TS(t9[u][:TOK, :], PS[u][:TOK, 0, 12:16], -float(CAP), 0.0, ALU.add, ALU.max), u)
                for u in UU:
                    wait(u)
                    mark(TT(s1[u][:TOK, :], PS[u][:TOK, 0, 8:12], t9[u][:TOK, :], ALU.subtract), u)
                for u in UU:
                    wait(u)
                    mark(STT(vd[u][:TOK, :], s1[u][:TOK, :], 1.0, rt[u][:TOK, :], ALU.is_ge, ALU.mult), u)
                for u in UU:
                    wait(u)
                    mark(STT(code[u][:TOK, :], s1[u][:TOK, :], C["seq9"][:TOK, :], vd[u][:TOK, :], ALU.add, ALU.mult), u)
                for u in UU:
                    wait(u)
                    TT(view(OH[u][:TOK], 0, [SLOT, MEM], [1, SLOT]), view(C["iota64"][:TOK], 0, [0, MEM], [1, SLOT]),
                       view(code[u][:TOK], 0, [1, MEM], [0, SLOT]), ALU.is_equal).then_inc(onehot, 1)
                for u in UU:
                    dve.wait_ge(vm_prod, nth(i, 0, 1, u))
                    V.tensor_copy(vM[u][:], PS[u][:, 2, :])
                for u in UU:
                    dve.wait_ge(z2_prod, nth(i, 0, 1, u))
                    TT(view(zz[u], 0, [SLOT, MEM], [1, SLOT]), view(PS[u][:, 3, :], 0, [SLOT, MEM], [1, SLOT]),
                       view(C["bgk"], 0, [1, MEM], [0, SLOT]), ALU.add)
                    mark(TS(zz[u][:, 256:NZ], PS[u][:, 3, 256:NZ], C["bgk"][:, MEM:MEM + 1], None, ALU.add), u)
                for u in UU:
                    wait(u)
                    STT(az[u], zz[u], -1.0, zz[u], ALU.mult, ALU.max).then_inc(zabs, 1)
                for u in UU:
                    dve.wait_ge(lned, nth(i, 0, 1, u))
                    mark(STT(lgz[u], zz[u], 0.0, az[u], ALU.min, ALU.subtract), u)
                for u in UU:
                    wait(u)
                    mark(V.tensor_tensor_scan(Gc[u][:], C["keep"], lgz[u], 0.0, ALU.mult, ALU.add), u)
                for u in UU:
                    wait(u)
                    dve.wait_ge(dexped, 2 * i + u + 1)
                    for t in range(CAP):
                        TT(view(Dp[:], t * MEM * SLOT, [SLOT, MEM], [CAP, SEQS], [1, t + 1]),
                           view(Gc[u][:], t, [SLOT, MEM], [CAP, SEQS], [0, t + 1]),
                           view(Gc[u][:], 0, [SLOT, MEM], [CAP, SEQS], [1, t + 1]), ALU.subtract)
                    for t in range(S):
                        last = TT(view(Dp[:], DM + t * TOK, [S, SEQS], [1, t + 1]),
                                  view(Gc[u][:], 256 + t, [S, SEQS], [0, t + 1]),
                                  view(Gc[u][:], 256, [S, SEQS], [1, t + 1]), ALU.subtract)
                    last.then_inc(exponents, 1)
                for u in UU:
                    dve.wait_ge(dexped, nth(i, 0, 1, u) + 1)
                    dve.wait_ge(qm_copied, nth(i, 0, 1, u))
                    e = view(U[u][:], 0, [MEM * SLOT, CAP], [1, MEM * SLOT])
                    mark(TT(e, e, view(kM[u][:], 0, [0, CAP], [1, MEM * SLOT]), ALU.mult), u)
                    wait(u)
                    e = view(U[u][:], 0, [SLOT, MEM * CAP], [CAP, SEQS], [1, CAP])
                    TT(e, e, view(qP[u][:], 0, [SEQS, MEM * CAP], [1, SEQS], [0, CAP]), ALU.mult).then_inc(mem_prod, 1)
                for u in UU:
                    dve.wait_ge(a_prod, nth(i, 0, 1, u))
                    for m in range(MEM):
                        p, mp = (m % 2) * SLOT, m // 2
                        TT(view(AbM[u][p:p + SLOT], mp * H1 * 128 + (m % 2) * SLOT, [128, H1], [CAP, SEQS], [1, CAP]),
                           view(PS[u][p:p + SLOT, 0, :], mp * 36, [1, H1], [0, SEQS], [4, CAP]),
                           view(C["bmask9"][p:p + SLOT], 0, [0, H1], [1, SEQS], [0, CAP]), ALU.mult)
                    TT(view(AbS[u][:TOK], 0, [TOK, H1], [S, SEQS], [1, S]), view(PS[u][:TOK, 0, :], 72, [1, H1], [0, SEQS], [4, S]),
                       view(C["bmask17"][:TOK], 0, [0, H1], [1, SEQS], [0, S]), ALU.mult).then_inc(a_spread, 1)
                for u in UU:
                    dve.wait_ge(o_prod, nth(i, 0, 1, u))
                    mark(V.tensor_copy(oS[u][:TOK, :], PS[u][:TOK, 2, 0:E]), u)
                for u in UU:
                    wait(u)
                    mark(TT(sq[u][:TOK, :], oS[u][:TOK, :], oS[u][:TOK, :], ALU.mult), u)
                for u in UU:
                    wait(u)
                    mark(V.tensor_reduce(ms[u][:TOK, :], view(sq[u][:TOK], 0, [DV, H1], [1, DV]), AX.X, ALU.add), u)
                for u in UU:
                    wait(u)
                    TS(mse[u][:TOK, :], ms[u][:TOK, :], 1.0 / DV, EPS, ALU.mult, ALU.add).then_inc(rms_ms, 1)
                for u in UU:
                    dve.wait_ge(rms_ready, nth(i, 0, 1, u))
                    mark(TT(view(oS[u][:TOK], 0, [DV, H1], [1, DV]), view(oS[u][:TOK], 0, [DV, H1], [1, DV]),
                            view(rs4[u][:TOK], 0, [1, H1], [0, DV]), ALU.mult), u)
                for u in UU:
                    wait(u)
                    TT(oS[u][:TOK, :], oS[u][:TOK, :], gs[u][:TOK, :], ALU.mult).then_inc(gated, 1)
                for u in UU:
                    dve.wait_ge(projected, nth(i, 2, 4, u))
                    mark(TT(h[u][:TOK, :], h[u][:TOK, :], PS[u][:TOK, 1, 0:E], ALU.add), u)
                layer_norm(5, h, xn)
                for u in UU:
                    dve.wait_ge(gate, nth(i, 2, 3, u))
                    mark(V.tensor_copy(lg[u][:TOK, :], PS[u][:TOK, 0, 0:NE1]), u)
                top_two(2, NE1, pr)
                for u in UU:
                    V.tensor_copy(view(picked[:TOK], (2 * i + u) * 4, [1, 2]), ixf[u][:TOK, :])
                    V.tensor_copy(view(picked[:TOK], (2 * i + u) * 4 + 2, [1, 2]), mx8[u][:TOK, 0:2])
                for u in UU:
                    dve.wait_ge(ff_exped, nth(i, 0, 1, u))
                    mark(TS(eg[u][:TOK, :], eg[u][:TOK, :], 1.0, None, ALU.add), u)
                for u in UU:
                    wait(u)
                    mark(V.reciprocal(eg[u][:TOK, :], eg[u][:TOK, :]), u)
                for u in UU:
                    wait(u)
                    mark(TT(eg[u][:TOK, :], eg[u][:TOK, :], PS[u][:TOK, 1, :], ALU.mult), u)
                for u in UU:
                    wait(u)
                    TT(hm[u][:TOK, :], eg[u][:TOK, :], PS[u][:TOK, 2, :], ALU.mult).then_inc(inner_ready, 1)
                for u in UU:
                    dve.wait_ge(projected, nth(i, 3, 4, u))
                    TT(view(h_all[:TOK], (2 * i + u) * E, [1, E]), h[u][:TOK, :], PS[u][:TOK, 1, 0:E], ALU.add).then_inc(done[u], 1)
                own.end()

        block_ctx.close()
        phase1.close()
        expert_phase(nc, ctx, PS, C, pack, h_all, picked, x_stored, cleared, out_stored, experts_d, x_d, xs_d, y_d, out_d)


def expert_phase(nc, ctx, PS, C, pack, h_all, picked, x_stored, cleared, out_stored, experts_d, x_d, xs_d, y_d, out_d):
    def sb(name, shape, dt=F32):
        return ctx.enter_context(nc.sbuf_tensor(name, shape, dt))

    def sem(name):
        return ctx.enter_context(nc.semaphore(name))

    GE = GROUPS * NE1
    wx = sb("expert_weights", [128, NE1 * EW])
    rows = sb("token_rows", [128, 2 * GROUPS * E])
    oh = [sb(f"oh{k}", [128, GE]) for k in (0, 1)]
    both, tot, cum, incl, pos = (sb(n, [128, GE]) for n in ("both", "tot", "cum", "incl", "pos"))
    psum_, wgt = sb("p_sum", [128, GROUPS]), [sb(f"wgt{k}", [128, GROUPS]) for k in (0, 1)]
    over, nt, tend, t128 = sb("over", [128, NE1 * FULL]), sb("nt", [128, NE1]), sb("tend", [128, NE1]), sb("t128", [128, NE1])
    posf, posu = sb("posf", [128, 2 * GROUPS]), sb("posu", [128, 2 * GROUPS], U32)
    past, tef, teu = sb("past", [128, TILES * NE1]), sb("tef", [128, TILES]), sb("teu", [128, TILES], mybir.dt.int32)
    xs, xsT, eg, hm, hmT, y = ([sb(f"{n}{u}", [128, w]) for u in (0, 1)]
                               for n, w in (("xs", E), ("xsT", E), ("ex", FF), ("hm2", FF), ("hmT2", FF), ("y", E)))
    x_back, rout, counts, placed, scattered, tile_exp = (sem(n) for n in (
        "x_back", "rout", "counts", "placed", "scattered", "tile_exp"))
    w_landed = sem("w_landed")
    row_landed, y_stored = [sem(f"row_landed{u}") for u in (0, 1)], [sem(f"y_stored{u}") for u in (0, 1)]
    r_turned, r_copied, upped, e_exped, inner, i_turned, i_copied, downed, y_copied, dstep = (sem(n) for n in (
        "r_turned", "r_copied", "upped", "e_exped", "inner", "i_turned", "i_copied", "downed", "y_copied", "dstep"))
    fetched = [sem(f"fetched{g}") for g in range(GROUPS)]
    summed = sem("summed")
    UU = (0, 1)

    def rows_of(g):
        return min(TOK, B * S - g * TOK)

    block = ctx.enter_context(nc.Block())

    @block.sync
    def _(sp):
        for g in range(GROUPS):
            sp.dma_start(rows[:rows_of(g), g * E:(g + 1) * E], x_d[g * TOK:g * TOK + rows_of(g), :]).then_inc(x_back, 16)
        for e in range(NE1):
            sp.dma_start(wx[:, e * EW:(e + 1) * EW], experts_d[:, e * EW:(e + 1) * EW]).then_inc(w_landed, 16)
        sp.wait_ge(scattered, 2 * GROUPS * 16)
        for u in UU:
            sp.dma_start(xs[u][:], xs_d[u * 128:(u + 1) * 128, :]).then_inc(row_landed[u], 16)

        def store_results(i):
            for u in UU:
                sp.wait_ge(y_copied, 2 * i + u + 1)
                sp.dma_start(y_d[bass.ds((2 * i + u) * 128, 128), :], y[u][:]).then_inc(y_stored[u], 16)

        with sp.Fori(0, TILES // 2 - 1) as i:
            for u in UU:
                sp.wait_ge(r_turned, 2 * i + u + 1)
                sp.dma_start(xs[u][:], xs_d[bass.ds((2 * i + 2 + u) * 128, 128), :]).then_inc(row_landed[u], 16)
            store_results(i)
        store_results(TILES // 2 - 1)
        for g in range(GROUPS):
            sp.wait_ge(summed, g + 1)
            sp.dma_start(out_d[g * TOK:g * TOK + rows_of(g), :], h_all[:rows_of(g), g, :]).then_inc(out_stored, 16)
        sp.wait_ge(out_stored, GROUPS * 16)

    @block.tensor
    def _(pe):
        mm, tp = nc.tensor.matmul, nc.tensor.transpose
        pe.wait_ge(rout, 1)
        mm(PS[0][:TOK, 0, 0:GE], C["tri"][:TOK, :], both[:TOK, :], start=True, stop=True)
        mm(PS[0][:TOK, 0, GE:2 * GE], C["ones"][:TOK, :], both[:TOK, :], start=True, stop=True).then_inc(counts, 1)

        def turn_rows(u, landed, read):
            pe.wait_ge(row_landed[u], landed)
            if read is not None:
                pe.wait_ge(y_copied, read)
            tp(PS[u][:, 0, 0:128], xs[u][:, 0:128], C["turner"])
            tp(PS[u][:, 0, 128:256], xs[u][:, 128:256], C["turner"]).then_inc(r_turned, 1)

        def up(u, n, e_at):
            pe.wait_ge(r_copied, n)
            for p in range(2):
                for c in range(KC):
                    last = mm(PS[u][:, 1 + p, :], xsT[u][:, c * 128:(c + 1) * 128],
                              view(wx[:], e_at + (p * KC + c) * FF, [1, FF]), start=(c == 0), stop=(c == KC - 1))
            last.then_inc(upped, 1)

        def turn_inner(u, n):
            pe.wait_ge(inner, n)
            for c in range(4):
                last = tp(PS[u][:, 3, c * 128:(c + 1) * 128], hm[u][:, c * 128:(c + 1) * 128], C["turner"])
            last.then_inc(i_turned, 1)

        def down(u, n, e_at):
            pe.wait_ge(i_copied, n)
            for c in range(4):
                last = mm(PS[u][:, 0, 256:512], hmT[u][:, c * 128:(c + 1) * 128],
                          view(wx[:], e_at + 2 * KC * FF + c * E, [1, E]), start=(c == 0), stop=(c == 3))
            last.then_inc(downed, 1)

        def expert_of(j):
            return pe.value_load(teu[0:1, bass.ds(j, 1)], min_val=0, max_val=(NE1 - 1) * EW)

        pe.wait_ge(tile_exp, 1)
        turn_rows(0, 16, None)
        turn_rows(1, 16, None)
        pe.wait_ge(w_landed, NE1 * 16)
        up(0, 1, expert_of(0))
        with pe.Fori(0, TILES // 2 - 1) as i:
            e0, e1, e2 = expert_of(2 * i), expert_of(2 * i + 1), expert_of(2 * i + 2)
            up(1, 2 * i + 2, e1)
            turn_inner(0, 2 * i + 1)
            down(0, 2 * i + 1, e0)
            turn_rows(0, i * 16 + 32, 2 * i + 1)
            up(0, 2 * i + 3, e2)
            turn_inner(1, 2 * i + 2)
            down(1, 2 * i + 2, e1)
            turn_rows(1, i * 16 + 32, 2 * i + 2)
        e0, e1 = expert_of(TILES - 2), expert_of(TILES - 1)
        up(1, TILES, e1)
        turn_inner(0, TILES - 1)
        down(0, TILES - 1, e0)
        turn_inner(1, TILES)
        down(1, TILES, e1)

    @block.scalar
    def _(act):
        A = nc.scalar.activation

        def copy_rows(u, n):
            act.wait_ge(r_turned, n)
            A(xsT[u][:], PS[u][:, 0, 0:256], ACT.Copy).then_inc(r_copied, 1)

        def exp_up(u, n):
            act.wait_ge(upped, n)
            A(eg[u][:], PS[u][:, 1, :], ACT.Exp, scale=-1.0).then_inc(e_exped, 1)

        def copy_inner(u, n):
            act.wait_ge(i_turned, n)
            A(hmT[u][:], PS[u][:, 3, :], ACT.Copy).then_inc(i_copied, 1)

        def copy_y(u, n, stored):
            act.wait_ge(downed, n)
            act.wait_ge(y_stored[u], stored)
            A(y[u][:], PS[u][:, 0, 256:512], ACT.Copy).then_inc(y_copied, 1)

        copy_rows(0, 1)
        copy_rows(1, 2)
        exp_up(0, 1)
        with act.Fori(0, TILES // 2 - 1) as i:
            exp_up(1, 2 * i + 2)
            copy_inner(0, 2 * i + 1)
            copy_y(0, 2 * i + 1, i * 16 + 16)
            copy_rows(0, 2 * i + 3)
            exp_up(0, 2 * i + 3)
            copy_inner(1, 2 * i + 2)
            copy_y(1, 2 * i + 2, i * 16 + 16)
            copy_rows(1, 2 * i + 4)
        exp_up(1, TILES)
        copy_inner(0, TILES - 1)
        copy_y(0, TILES - 1, (TILES // 2) * 16)
        copy_inner(1, TILES)
        copy_y(1, TILES, (TILES // 2) * 16)

    @block.gpsimd
    def _(pool):
        G = nc.gpsimd
        for u in UU:
            pool.sem_inc(y_stored[u], 16)
        pool.wait_ge(placed, 1)
        pool.wait_ge(x_back, GROUPS * 16)
        for k in (0, 1):
            for g in range(GROUPS):
                n = rows_of(g)
                G.indirect_dma_start(xs_d, bass.IndirectOffsetOnAxis(posu[:n, k * GROUPS + g:k * GROUPS + g + 1], 0),
                                     rows[:n, g * E:(g + 1) * E], None).then_inc(scattered, 16)
        for u in UU:
            pool.wait_ge(y_stored[u], (TILES // 2 + 1) * 16)
        for g in range(GROUPS):
            n = rows_of(g)
            for k in (0, 1):
                at = (2 * g + k) * E
                G.indirect_dma_start(rows[:n, at:at + E], None, y_d,
                                     bass.IndirectOffsetOnAxis(posu[:n, k * GROUPS + g:k * GROUPS + g + 1], 0)).then_inc(fetched[g], 16)

    @block.vector
    def _(dve):
        V = nc.vector
        TT, TS, STT = V.tensor_tensor, V.tensor_scalar, V.scalar_tensor_tensor
        n_steps = [0]

        def link(ins):
            ins.then_inc(dstep, 1)
            n_steps[0] += 1
            dve.wait_ge(dstep, n_steps[0])

        T = slice(0, TOK)
        g_of, e_of = [1, GROUPS], [GROUPS, NE1]
        link(TT(psum_[T, :], view(picked[T], 2, [4, GROUPS]), view(picked[T], 3, [4, GROUPS]), ALU.add))
        link(TS(psum_[T, :], psum_[T, :], 1e-20, None, ALU.add))
        link(V.reciprocal(psum_[T, :], psum_[T, :]))
        for k in (0, 1):
            link(TT(wgt[k][T, :], view(picked[T], 2 + k, [4, GROUPS]), psum_[T, :], ALU.mult))
            link(TT(view(oh[k][T], 0, e_of, g_of), view(C["eight"][T], 0, [1, NE1], [0, GROUPS]),
                    view(picked[T], k, [0, NE1], [4, GROUPS]), ALU.is_equal))
            link(TT(view(oh[k][T], 0, e_of, g_of), view(oh[k][T], 0, e_of, g_of), view(C["valid"][T], 0, [0, NE1], g_of), ALU.mult))
        TT(both[T, :], oh[0][T, :], oh[1][T, :], ALU.add).then_inc(rout, 1)
        dve.wait_ge(counts, 1)
        link(V.tensor_copy(tot[T, :], PS[0][T, 0, GE:2 * GE]))
        link(V.tensor_tensor_scan(incl[T, :], C["step_g"][T, :], tot[T, :], 0.0, ALU.mult, ALU.add))
        link(TT(view(over[T], 0, [FULL, NE1], [1, FULL]), view(incl[T], GROUPS - 1, [GROUPS, NE1], [0, FULL]),
                view(C["fills"][T], 0, [0, NE1], [1, FULL]), ALU.is_gt))
        link(V.tensor_reduce(nt[T, :], view(over[T], 0, [FULL, NE1], [1, FULL]), AX.X, ALU.add))
        link(V.tensor_tensor_scan(tend[T, :], C["step_e"][T, :], nt[T, :], 0.0, ALU.mult, ALU.add))
        link(TT(t128[T, :], tend[T, :], nt[T, :], ALU.subtract))
        link(TS(t128[T, :], t128[T, :], 128.0, -1.0, ALU.mult, ALU.add))
        link(TT(pos[T, :], incl[T, :], tot[T, :], ALU.subtract))
        link(TT(pos[T, :], pos[T, :], PS[0][T, 0, 0:GE], ALU.add))
        link(TT(view(pos[T], 0, e_of, g_of), view(pos[T], 0, e_of, g_of), view(t128[T], 0, [1, NE1], [0, GROUPS]), ALU.add))
        for k in (0, 1):
            link(TT(cum[T, :], pos[T, :], oh[k][T, :], ALU.mult))
            link(V.tensor_reduce(posf[T, k * GROUPS:(k + 1) * GROUPS], view(cum[T], 0, g_of, e_of), AX.X, ALU.add))
        V.tensor_copy(posu[T, :], posf[T, :]).then_inc(placed, 1)
        link(TT(view(past[T], 0, [NE1, TILES], [1, NE1]), view(C["tile_no"][T], 0, [1, TILES], [0, NE1]),
                view(tend[T], 0, [0, TILES], [1, NE1]), ALU.is_ge))
        link(V.tensor_reduce(tef[T, :], view(past[T], 0, [NE1, TILES], [1, NE1]), AX.X, ALU.add))
        link(TS(tef[T, :], tef[T, :], float(NE1 - 1), float(EW), ALU.min, ALU.mult))
        V.tensor_copy(teu[T, :], tef[T, :]).then_inc(tile_exp, 1)

        own = n_steps[0]
        per = 6

        def swish(u, base, n):
            dve.wait_ge(e_exped, n)
            TS(eg[u][:], eg[u][:], 1.0, None, ALU.add).then_inc(dstep, 1)
            dve.wait_ge(dstep, base + 1)
            V.reciprocal(eg[u][:], eg[u][:]).then_inc(dstep, 1)
            dve.wait_ge(dstep, base + 2)
            TT(eg[u][:], eg[u][:], PS[u][:, 1, :], ALU.mult).then_inc(dstep, 1)
            dve.wait_ge(dstep, base + 3)
            TT(hm[u][:], eg[u][:], PS[u][:, 2, :], ALU.mult).then_inc(inner, 1)

        with dve.Fori(0, TILES // 2) as i:
            for u in UU:
                swish(u, i * per + own + 3 * u, 2 * i + u + 1)
        n_steps[0] += 3 * TILES
        for g in range(GROUPS):
            n = rows_of(g)
            dve.wait_ge(fetched[g], 32)
            link(STT(h_all[:n, g, :], rows[:n, 2 * g * E:(2 * g + 1) * E], wgt[0][:n, g:g + 1], h_all[:n, g, :], ALU.mult, ALU.add))
            STT(h_all[:n, g, :], rows[:n, (2 * g + 1) * E:(2 * g + 2) * E], wgt[1][:n, g:g + 1], h_all[:n, g, :], ALU.mult, ALU.add).then_inc(summed, 1)


def _pack_arrays(inp, np):
    f = np.float32

    def rows(w):
        k, n = w.shape
        return w.reshape(k // 128, 128, n).transpose(1, 0, 2).reshape(128, -1)

    def row(v, n=128):
        return np.broadcast_to(v.reshape(1, -1), (n, v.size))

    def col(v):
        return v.reshape(-1, 128).T

    tok = np.arange(TOK)
    seq, pos = tok // S, tok % S
    a = {}
    a["ident"] = np.eye(128, dtype=f)
    a["w_tok"] = rows(inp["L0_tok_W"])
    a["cls"] = inp["cls_tok"].reshape(1, E)
    a["is_cls"] = (pos == 0).astype(f)[None]
    w = inp["L0_attn_W_qkv"].reshape(H0, 3, D0, E)
    bq = inp["L0_attn_b_qkv"].reshape(H0, 3, D0)
    q, k, v = (w[:, j].reshape(E, E).T for j in range(3))
    a["wqk0"], a["wv0"] = rows(np.concatenate([q, k], 1)), rows(v)
    a["bqk0"] = np.concatenate([col(bq[:, 0].reshape(-1)), col(bq[:, 1].reshape(-1))], 1)
    a["bv0"] = row(bq[:, 2].reshape(-1))
    a["wo0"], a["bo0"] = rows(inp["L0_attn_W_out"].T), row(inp["L0_attn_b_out"])
    a["headmask"] = (np.arange(128)[:, None] // D0 == np.arange(8)[None]).astype(f)
    w, bb = inp["L0_ffn_in_proj_w"], inp["L0_ffn_in_proj_b"]
    a["wqk1"], a["wv1"] = rows(w[:2 * E].T), rows(w[2 * E:].T)
    a["bqk1"], a["bv1"] = col(bb[:2 * E]), row(bb[2 * E:])
    a["wo1"], a["bo1"] = rows(inp["L0_ffn_out_proj_w"].T), row(inp["L0_ffn_out_proj_b"])
    inv = (1.0 / 10000.0 ** (np.arange(0, D0, 2, dtype=f) / f(D0))).astype(f)
    ang = pos.astype(f)[:, None] * inv[None]
    a["rope_cos"] = np.tile(np.repeat(np.cos(ang), 2, axis=1), (1, H0))
    a["rope_sin"] = np.tile(np.sin(ang), (1, H0))
    a["w_gate0"], a["b_gate0"] = rows(inp["L0_ffn_gate_w"].T), row(inp["L0_ffn_gate_b"])
    a["w_exp0"] = rows(inp["L0_ffn_expert_w"].transpose(2, 0, 1).reshape(E, NE0 * E))
    a["b_exp0"] = inp["L0_ffn_expert_b"]
    for n in ("ln1_w", "ln1_b", "ln2_w", "ln2_b"):
        a[n] = row(inp[f"L0_ffn_{n}"])
    a["iota8"] = row(np.arange(8, dtype=f))
    a["w_gate1"], a["w_g"] = rows(inp["L1_attn_w_gate"]), rows(inp["L1_attn_w_g"])
    a["wq"], a["wks"], a["wvs"] = rows(inp["L1_attn_w_q"]), rows(inp["L1_attn_w_ks"]), rows(inp["L1_attn_w_vs"])
    a["wgk1s"], a["wgk2s"] = rows(inp["L1_attn_w_gk1s"]), inp["L1_attn_w_gk2s"]
    a["wk"] = rows(inp["L1_attn_w_k"].transpose(1, 0, 2).reshape(E, -1))
    a["wv"] = rows(inp["L1_attn_w_v"].transpose(1, 0, 2).reshape(E, -1))
    a["wgk1"] = rows(inp["L1_attn_w_gk1"].transpose(1, 0, 2).reshape(E, -1))
    a["wgk2"] = inp["L1_attn_w_gk2"].transpose(1, 0, 2).reshape(LOW, -1)
    a["bgk"] = np.concatenate([inp["L1_attn_b_gk"].T, inp["L1_attn_b_gks"][:, None]], 1)
    a["w_o"], a["norm_w"] = rows(inp["L1_attn_w_o"]), row(np.tile(inp["L1_attn_norm_w"], H1))
    same = seq[:, None] == seq[None]
    a["same"] = same.astype(f)
    a["upto"] = (same & (pos[:, None] <= pos[None])).astype(f)
    a["seq9"] = (seq * CAP).astype(f)[:, None]
    a["iota64"] = row(np.arange(1, SLOT + 1, dtype=f))
    slot = np.arange(SLOT)
    a["keep"] = row(np.concatenate([np.tile((slot % CAP != 0) & (slot < SEQS * CAP), MEM), pos != 0]).astype(f))
    a["hsel"] = (np.arange(128)[:, None] // DK == np.arange(H1)[None]).astype(f)
    a["bmask9"] = ((np.arange(128) % SLOT)[:, None] // CAP == np.arange(SEQS)[None]).astype(f)
    a["bmask17"] = (seq[:, None] == np.arange(SEQS)[None]).astype(f)
    a["w_r"], a["sg"], a["su"], a["sd"] = (rows(inp[f"L1_ffn_{n}"]) for n in ("Wr", "Sg", "Su", "Sd"))
    a["turner"] = np.eye(128, dtype=f)
    a["tri"] = (tok[:, None] <= tok[None]).astype(f)
    a["ones"] = np.ones((TOK, TOK), f)
    a["eight"] = row(np.arange(NE1, dtype=f))
    a["valid"] = (np.arange(GROUPS)[None] * TOK + tok[:, None] < B * S).astype(f)
    a["step_g"] = row(np.tile(np.arange(GROUPS) != 0, NE1).astype(f))
    a["step_e"] = row(np.ones(NE1, f))
    a["fills"] = row(np.arange(FULL, dtype=f) * 128)
    a["tile_no"] = row(np.arange(TILES, dtype=f))
    out = {}
    for k, parts in PACKS.items():
        p = np.zeros((128, WIDTH[k]), f)
        at = 0
        for name, wd in parts:
            assert a[name].shape[1] == wd, (name, a[name].shape, wd)
            p[:a[name].shape[0], at:at + wd] = a[name]
            at += wd
        out[k] = p
    return out


def kernel(**inputs):
    import ml_dtypes
    import numpy as np
    import concourse.bacc as bacc
    from concourse.bass_utils import run_bass_kernel_spmd as run

    inp = {k: np.asarray(v) for k, v in inputs.items()}
    packs = _pack_arrays(inp, np)
    x = inp["x"].reshape(B, 4, 16, 4, 16, 3).transpose(0, 1, 3, 2, 4, 5).reshape(B, PATCHES, FEAT)
    xt = np.zeros((GROUPS * SEQS, S, FEAT), x.dtype)
    xt[:B, 1:] = x
    xt = xt.reshape(GROUPS, TOK, FC, 128).transpose(0, 3, 2, 1).reshape(GROUPS, 128, FC * TOK)
    tok = np.arange(TOK)
    same = tok[:, None] // S == tok[None] // S
    masks = np.zeros((128, 2 * TOK + 128), np.float32)
    masks[:TOK, 0:TOK] = np.where(same, 0.0, FAR)
    masks[:TOK, TOK:2 * TOK] = np.where(same & (tok[None] <= tok[:, None]), 0.0, FAR)
    masks[:, 2 * TOK:] = np.eye(128)
    masks = masks.astype(ml_dtypes.bfloat16)

    ew = np.zeros((128, NE1, EW), np.float32)
    for n, name in enumerate(("L1_ffn_Wg", "L1_ffn_Wu")):
        ew[:, :, n * KC * FF:(n + 1) * KC * FF] = inp[name].reshape(NE1, KC, 128, FF).transpose(2, 0, 1, 3).reshape(128, NE1, KC * FF)
    ew[:, :, 2 * KC * FF:] = inp["L1_ffn_Wd"].reshape(NE1, 4, 128, E).transpose(2, 0, 1, 3).reshape(128, NE1, 4 * E)

    nc = bacc.Bacc("TRN2", target_bir_lowering=False, num_devices=1)
    arrays = {"in_patches": np.ascontiguousarray(xt), "in_masks": masks, "in_experts": ew.reshape(128, NE1 * EW), **{f"in_{k}": v for k, v in packs.items()}}
    aps = {k: nc.dram_tensor(k, a.shape, mybir.dt.from_np(a.dtype), kind="ExternalInput").ap() for k, a in arrays.items()}
    out = nc.dram_tensor("out_0_dram", (B * S, E), F32, kind="ExternalOutput").ap()
    x_d = nc.dram_tensor("expert_in", (GROUPS * TOK, E), F32, kind="Internal").ap()
    xs_d = nc.dram_tensor("expert_rows", (TILES * 128, E), F32, kind="Internal").ap()
    y_d = nc.dram_tensor("expert_out", (TILES * 128, E), F32, kind="Internal").ap()
    tower_kernel(nc, aps["in_patches"], {k: aps[f"in_{k}"] for k in PACKS}, aps["in_masks"], aps["in_experts"], x_d, xs_d, y_d, out)
    r = run(nc, [arrays], core_ids=[0])
    return r.results[0]["out_0_dram"].reshape(B, S, E)
```

```python
from contextlib import ExitStack

import concourse.bass as bass
from concourse import mybir

F32 = mybir.dt.float32
BF16 = mybir.dt.bfloat16
U32 = mybir.dt.uint32
ALU = mybir.AluOpType
ACT = mybir.ActivationFunctionType
AX = mybir.AxisListType

B, PATCHES, S = 64, 16, 17
E = 256
KC = E // 128
FEAT = 768
FC = FEAT // 128
SEQS = 7
TOK = SEQS * S
GROUPS = -(-B // SEQS)
PAIRS = GROUPS // 2
H0, D0 = 16, 16
NE0 = 8
H1, DK, DV = 4, 32, 64
MEM, CAP, LOW = 4, 9, 16
SLOT = 64
PAIRM = MEM // 2
NE1, FF = 8, 512
EPS = 1e-5
FAR = -1e30
GATE_NORM = 16.0
QSCALE1 = float(DK) ** -0.5
DM = MEM * CAP * SLOT
DALL = DM + S * TOK

TILES = (2 * B * S + NE1 * 127) // 128
FULL = -(-B * S // 128)
EW = 2 * KC * FF + (FF // 128) * E
PACKS = {
    "tok": [("w_tok", FC * E), ("cls", E), ("is_cls", TOK)],
    "l0": [("wqk0", KC * 2 * E), ("wv0", KC * E), ("wo0", KC * E), ("bqk0", 4), ("bv0", E), ("bo0", E),
           ("headmask", 8),
           ("wqk1", KC * 2 * E), ("wv1", KC * E), ("wo1", KC * E), ("bqk1", 4), ("bv1", E), ("bo1", E),
           ("rope_cos", E), ("rope_sin", 128)],
    "l0f": [("w_gate0", KC * NE0), ("b_gate0", NE0), ("w_exp0", KC * NE0 * E), ("b_exp0", E),
            ("ln1_w", E), ("ln1_b", E), ("ln2_w", E), ("ln2_b", E)],
    "l1": [("w_gate1", KC * MEM), ("w_g", KC * E), ("wq", KC * 128), ("wks", KC * 128), ("wvs", KC * E),
           ("wgk1s", KC * LOW), ("wgk2s", 128), ("wk", KC * MEM * 128), ("wv", KC * MEM * E),
           ("wgk1", KC * MEM * LOW), ("wgk2", MEM * 128), ("bgk", MEM + 1), ("w_o", KC * E),
           ("norm_w", E), ("upto", TOK), ("same", TOK), ("seq9", 1), ("iota64", SLOT), ("keep", MEM * SLOT + TOK),
           ("hsel", H1), ("bmask9", SEQS), ("bmask17", SEQS),
           ("w_r", KC * NE1), ("sg", KC * FF), ("su", KC * FF), ("sd", (FF // 128) * E)],
}
PACKS["route"] = [("turner", 128), ("tri", TOK), ("ones", TOK), ("eight", NE1), ("valid", GROUPS), ("step_g", NE1 * GROUPS), ("step_e", NE1),
                  ("fills", FULL), ("tile_no", TILES)]
WIDTH = {k: sum(w for _, w in v) for k, v in PACKS.items()}
EARLY = (WIDTH["l0"] + WIDTH["l0f"] + WIDTH["tok"]) // EW


def view(ap, off, *dims):
    return bass.AP(ap.tensor, ap.offset + off, [list(ap.ap[0])] + [list(d) for d in dims])


class Steps:

    def __init__(self, eng, sem):
        self.eng, self.sem, self.n = eng, sem, 0

    def mark(self, ins):
        ins.then_inc(self.sem, 1)
        self.n += 1

    def wait(self):
        self.eng.wait_ge(self.sem, self.n)

    def end(self):
        self.wait()
        self.eng.sem_clear(self.sem)


def weave(*halves):
    due = [[next(h, None), n, h] for n, h in enumerate(halves)]
    due = [d for d in due if d[0] is not None]
    while due:
        due.sort(key=lambda d: d[:2])
        at = next(due[0][2], None)
        if at is None:
            due.pop(0)
        else:
            due[0][0] = at


def in_turn(*parts):
    for p in parts:
        yield from p


def all_groups(eng, begin, front, back):
    begin = begin or (lambda u, i: ())
    weave(in_turn(begin(0, 0)))
    weave(front(0, 0), in_turn(begin(1, 0)))
    with eng.Fori(0, PAIRS - 1) as i:
        weave(in_turn(back(0, i), begin(0, i + 1)), front(1, i))
        weave(in_turn(back(1, i), begin(1, i + 1)), front(0, i + 1))
    weave(back(0, PAIRS - 1), front(1, PAIRS - 1))
    weave(back(1, PAIRS - 1))


def tower_kernel(nc, xp_d, packs_d, masks_d, experts_d, x_d, xs_d, y_d, out_d):
    with ExitStack() as ctx, ExitStack() as phase1:
        def keep(name, shape, dt=F32):
            return ctx.enter_context(nc.sbuf_tensor(name, shape, dt))

        def sb(name, shape, dt=F32):
            return phase1.enter_context(nc.sbuf_tensor(name, shape, dt))

        def sem(name):
            return ctx.enter_context(nc.semaphore(name))

        PS = [ctx.enter_context(nc.psum_tensor(f"ps{u}", [128, 4, 512], F32)) for u in (0, 1)]
        pack = {"route": keep("pack_route", [128, WIDTH["route"]])}
        h_all = keep("h_all", [128, GROUPS, E])
        picked = keep("picked", [128, GROUPS * 4])
        arena = keep("arena", [128, NE1 * EW])
        at = 0
        for k in ("l0", "l0f", "tok", "l1"):
            pack[k] = arena[:, at:at + WIDTH[k]]
            at += WIDTH[k]
        xp = [arena[:, at + u * FC * TOK:at + (u + 1) * FC * TOK] for u in (0, 1)]
        C = {}
        for k, parts in PACKS.items():
            at = 0
            for name, w in parts:
                C[name] = pack[k][:, at:at + w]
                at += w
        masks = sb("masks", [128, 2 * TOK + 128], BF16)
        identb = masks[:, 2 * TOK:]
        zeros = sb("zeros", [128, E])
        Dp = sb("pair_exponents", [128, DALL])
        roots = sb("roots", [128, 4])

        def two(name, shape, dt=F32):
            return [sb(f"{name}{u}", shape, dt) for u in (0, 1)]

        h = two("h", [128, E])
        xn = two("xn", [128, E])
        xa = two("xa", [128, E])
        hb = two("hb", [128, E])
        xT = two("xT", [128, 4 * TOK])
        vS = two("v_ones", [128, H0 * (D0 + 1)])
        cT = two("cT", [128, TOK])
        qS, kS = two("q_shared", [128, TOK]), two("k_shared", [128, TOK])
        vsh = two("v_shared", [128, E])
        gs = two("silu_g", [128, E])
        ohT = two("combineT", [128, PAIRM * TOK])
        qP = two("q_mem", [128, MEM * CAP * SEQS])
        kM = two("k_mem", [128, MEM * SLOT])
        vM = two("v_mem", [128, PAIRM * E])
        Gc = two("decay_sums", [128, MEM * SLOT + TOK])
        AbM = two("a_mem", [128, PAIRM * H1 * 128])
        st, mv, ve, rstd = two("st", [128, 6]), two("mv", [128, 2]), two("ve", [128, 1]), two("rstd", [128, 1])
        lg, d8, pr, pr4, mx8 = (two(n, [128, 8]) for n in ("lg", "d8", "pr", "pr4", "mx8"))
        ix = two("ix", [128, 8], U32)
        ixf = two("ixf", [128, 2])
        mxs, ssum, rsum = two("mxs", [128, 1]), two("ssum", [128, 1]), two("rsum", [128, 1])
        mxh = two("mxh", [128, H0])
        rden = two("rden", [128, H0])
        c0, c1, cw = two("c0", [128, 8]), two("c1", [128, 8]), two("cw", [128, 8])
        p12, rp = two("p12", [128, 1]), two("rp", [128, 1])
        rt, w2, t9, s1, vd, code = (two(n, [128, 4]) for n in ("rt", "w2", "t9", "s1", "vd", "code"))
        ms, mse, rs4 = (two(n, [128, 4]) for n in ("ms", "mse", "rs4"))
        U = two("area", [128, DALL])
        SC = H0 * TOK
        dA = [U[u][:, 0:SC] for u in (0, 1)]
        kPT = [U[u][:, SC:2 * SC] for u in (0, 1)]
        qT = [U[u][:, 2 * SC:2 * SC + 2 * TOK] for u in (0, 1)]
        kT = [U[u][:, 2 * SC + 2 * TOK:2 * SC + 4 * TOK] for u in (0, 1)]
        o = [U[u][:, 2 * SC:2 * SC + E] for u in (0, 1)]
        rr = [U[u][:, SC:SC + E] for u in (0, 1)]
        rq = [U[u][:, SC + E:SC + 2 * E] for u in (0, 1)]
        acc = [U[u][:, 0:E] for u in (0, 1)]
        NZ = MEM * SLOT + TOK
        xg = [U[u][:, 0:512] for u in (0, 1)]
        z1M = [U[u][:, 512:768] for u in (0, 1)]
        z1S = [U[u][:, 768:768 + TOK] for u in (0, 1)]
        OH = [U[u][:, 1024:1280] for u in (0, 1)]
        OHw = [U[u][:, 1280:1536] for u in (0, 1)]
        zz = [U[u][:, 1536:1536 + NZ] for u in (0, 1)]
        az = [U[u][:, 1536 + NZ:1536 + 2 * NZ] for u in (0, 1)]
        lgz = [U[u][:, 1536 + 2 * NZ:1536 + 3 * NZ] for u in (0, 1)]
        egs = [U[u][:, 3000:3256] for u in (0, 1)]
        AbS = [U[u][:, 0:H1 * TOK] for u in (0, 1)]
        oM = [U[u][:, 512:1024] for u in (0, 1)]
        oS = [U[u][:, 1024:1280] for u in (0, 1)]
        sq = [U[u][:, 1280:1536] for u in (0, 1)]
        eg = [U[u][:, 1536:2048] for u in (0, 1)]
        hm = [U[u][:, 2048:2560] for u in (0, 1)]
        hmT = [U[u][:, 2560:2560 + 4 * TOK] for u in (0, 1)]

        x_landed = [sem(f"x_landed{u}") for u in (0, 1)]
        tok_used = [sem(f"tok_used{u}") for u in (0, 1)]
        landed = {k: sem(f"landed_{k}") for k in [*PACKS, "masks"]}
        out_stored = sem("out_stored")
        x_stored = [sem(f"x_stored{u}") for u in (0, 1)]
        cleared = sem("rows_cleared")
        w_landed = sem("expert_weights_landed")
        pool_ready = sem("pool_ready")
        own_f = {e: sem(f"{e}_front_step") for e in ("dve", "pool")}
        own_b = {e: sem(f"{e}_back_step") for e in ("dve", "pool", "act")}
        stats, rstd_ready, norm = (
            {"a": sem(f"{n}_begin"), "f": sem(f"{n}_front"), "b": sem(f"{n}_back")} for n in (
                "stats", "rstd_ready", "norm"))
        turned, turn_copied, projected, gate, logits, softmaxed = (
            {"f": sem(f"{n}_front"), "b": sem(f"{n}_back")} for n in (
                "turned", "turn_copied", "projected", "gate", "logits", "softmaxed"))
        (qkv, qk_copied, km_pool, km_dve, v_copied, scores, shifted, exped, p_turned, pt_act, pt_dve, av, attended,
         res_ready, roped, experts, exp_read, c_ready, c_turned, c_copied, bias_ready) = (sem(n) for n in (
            "qkv", "qk_copied", "km_pool", "km_dve", "v_copied", "scores", "shifted", "exped", "p_turned", "pt_act",
            "pt_dve", "av", "attended", "res_ready", "roped", "experts", "exp_read", "c_ready", "c_turned",
            "c_copied", "bias_ready"))
        (g_prod, sh_prod, vs_prod, sh_copied, routed, counted, onehot, weighted, gathered, xg_copied, oh_turned,
         oh_copied, z1_prod, z1_copied, qm_prod, qm_copied, vm_prod, z2_prod, zabs, lned, sig_in, sig_out,
         exponents, dexped_m, mem_prod, sh_pairs, a_prod, a_spread, om_prod, om_copied, o_prod, gated, up_prod,
         inner_ready, inner_turned, inner_copied, rms_ms, rms_ready, gs_ready, gs_scaled, g_copied) = (sem(n) for n in (
            "g_prod", "sh_prod", "vs_prod", "sh_copied", "routed", "counted", "onehot", "weighted", "gathered",
            "xg_copied", "oh_turned", "oh_copied", "z1_prod", "z1_copied", "qm_prod", "qm_copied", "vm_prod",
            "z2_prod", "zabs", "lned", "sig_in", "sig_out", "exponents", "dexped_m", "mem_prod", "sh_pairs",
            "a_prod", "a_spread", "om_prod", "om_copied", "o_prod", "gated", "up_prod", "inner_ready",
            "inner_turned", "inner_copied", "rms_ms", "rms_ready", "gs_ready", "gs_scaled", "g_copied"))
        dexped = [sem(f"dexped{u}") for u in (0, 1)]

        def nth(i, k, per_half, u):
            return i * (2 * per_half) + (u * per_half + k + 1)

        LNF, LNB, TF, TC, TB = 2, 2, 6, 5, 3
        ROOTS = 4
        UU = (0, 1)
        T = slice(0, TOK)
        block_ctx = ExitStack()
        block = block_ctx.enter_context(nc.Block())

        @block.sync
        def _(sp):
            sp.dma_start(pack["route"][:], packs_d["route"]).then_inc(landed["route"], 16)
            sp.dma_start(pack["tok"], packs_d["tok"]).then_inc(landed["tok"], 16)
            for u in UU:
                sp.dma_start(xp[u], xp_d[u]).then_inc(x_landed[u], 16)
            sp.dma_start(masks[:], masks_d).then_inc(landed["masks"], 16)
            for k in ("l0", "l0f", "l1"):
                sp.dma_start(pack[k], packs_d[k]).then_inc(landed[k], 16)
            sp.wait_ge(pool_ready, 1)
            for j in range(TILES):
                sp.dma_start(xs_d[j * 128:(j + 1) * 128, :], zeros[:]).then_inc(cleared, 16)

            def store_inputs(i, u):
                sp.wait_ge(norm["b"], nth(i, 1, LNB, u))
                sp.dma_start(x_d[bass.ds((2 * i + u) * TOK, TOK), :], xn[u][:TOK, :]).then_inc(x_stored[u], 16)

            with sp.Fori(0, PAIRS - 1) as i:
                for u in UU:
                    sp.wait_ge(tok_used[u], i + 1)
                    sp.dma_start(xp[u], xp_d[bass.ds(2 * i + 2 + u, 1)].rearrange("o p f -> (o p) f")).then_inc(x_landed[u], 16)
                for u in UU:
                    store_inputs(i, u)
            store_inputs(PAIRS - 1, 0)
            sp.wait_ge(norm["b"], nth(PAIRS - 1, 0, LNB, 1))
            for e in range(EARLY):
                sp.dma_start(arena[:, e * EW:(e + 1) * EW], experts_d[:, e * EW:(e + 1) * EW]).then_inc(w_landed, 16)
            store_inputs(PAIRS - 1, 1)
            for u in UU:
                sp.wait_ge(x_stored[u], (PAIRS + 1) * 16)
            sp.wait_ge(cleared, TILES * 16)

        @block.tensor
        def _(pe):
            mm, tp = nc.tensor.matmul, nc.tensor.transpose
            pe.wait_ge(landed["route"], 16)
            pe.wait_ge(landed["tok"], 16)

            def turn(u, half, blocks, bank=3):
                for c, s in enumerate(blocks):
                    last = tp(PS[u][:, bank, c * TOK:(c + 1) * TOK], s, C["turner"][:TOK, :TOK])
                last.then_inc(turned[half], 1)

            def chunks(x, n=KC):
                return [x[:TOK, c * 128:(c + 1) * 128] for c in range(n)]

            def rows_product(u, bank, w, n, lo=0):
                for c in range(KC):
                    last = mm(PS[u][:TOK, bank, lo:lo + n], xT[u][:, c * TOK:(c + 1) * TOK],
                              w[:, c * n:(c + 1) * n], start=(c == 0), stop=(c == KC - 1))
                return last

            def begin(u, i):
                yield 72.5
                pe.wait_ge(x_landed[u], i * 16 + 16)
                mm(PS[u][:TOK, 0, 0:E], C["is_cls"][0:1, :], C["cls"][0:1, :], start=True, stop=False)
                for c in range(FC):
                    last = mm(PS[u][:TOK, 0, 0:E], xp[u][:, c * TOK:(c + 1) * TOK], C["w_tok"][:, c * E:(c + 1) * E],
                              start=False, stop=(c == FC - 1))
                last.then_inc(tok_used[u], 1)

            def front(u, i):
                for k in (0, 1):
                    z = 35 * k
                    if k == 0:
                        yield 0
                        pe.wait_ge(norm["a"], nth(i, 0, 1, u))
                        turn(u, "f", chunks(xn[u]))
                    else:
                        yield 31.5
                        pe.wait_ge(norm["f"], nth(i, 0, LNF, u))
                        turn(u, "f", chunks(xa[u]))
                        yield 33
                        pe.wait_ge(roped, nth(i, 0, 1, u))
                        turn(u, "f", chunks(rr[u]), bank=0)
                    yield 1 + z
                    pe.wait_ge(landed["l0"], 16)
                    pe.wait_ge(turn_copied["f"], nth(i, 2 * k, TC, u))
                    qk_at = 2 * k
                    for j in (2, 0, 3, 1):
                        for c in range(KC):
                            w = C[f"wqk{k}"][:, c * 2 * E + j * 128:c * 2 * E + (j + 1) * 128]
                            last = mm(PS[u][:, j // 2, (j % 2) * TOK:(j % 2 + 1) * TOK], w,
                                      xT[u][:, (qk_at + c) * TOK:(qk_at + c + 1) * TOK], start=(c == 0), stop=(c == KC - 1))
                    last.then_inc(qkv, 1)
                    yield 3.5 + z
                    rows_product(u, 2, C[f"wv{k}"], E).then_inc(qkv, 1)
                    for hf in (0, 1):
                        for b in (2 * hf, 2 * hf + 1):
                            yield 7 + z + b
                            if b == 0:
                                pe.wait_ge(landed["masks"], 16)
                                pe.wait_ge(qk_copied, nth(i, 3 * k + 2, 6, u))
                                pe.wait_ge(km_pool, nth(i, k, 2, u))
                            if b == 2:
                                pe.wait_ge(km_dve, nth(i, k, 2, u))
                                pe.wait_ge(v_copied, nth(i, k, 2, u))
                            mm(view(PS[u][:TOK, b, :], 0, [TOK, 4], [1, TOK]), identb[:TOK, :TOK],
                               view(masks[:TOK], k * TOK, [0, 4], [1, TOK]), start=True, stop=False)
                            last = mm(PS[u][:TOK, b, 0:4 * TOK], qT[u][:, (b // 2) * TOK:(b // 2 + 1) * TOK],
                                      kPT[u][:, b * 4 * TOK:(b + 1) * 4 * TOK], start=False, stop=True)
                        last.then_inc(scores, 1)
                    for hf in (0, 1):
                        yield 13 + z + 2.5 * hf
                        pe.wait_ge(exped, nth(i, 2 * k + hf, 4, u))
                        for hd in range(8 * hf, 8 * hf + 8):
                            last = tp(PS[u][:TOK, hd // 4, (hd % 4) * TOK:(hd % 4 + 1) * TOK],
                                      dA[u][:TOK, hd * TOK:(hd + 1) * TOK], C["turner"][:TOK, :TOK])
                        last.then_inc(p_turned, 1)
                    W = D0 + 1
                    for hd in range(H0):
                        if hd % 4 == 0:
                            yield 17.5 + z + 0.4 * hd
                        if hd == 0:
                            pe.wait_ge(pt_act, nth(i, k, 2, u))
                        if hd == 8:
                            pe.wait_ge(pt_dve, nth(i, k, 2, u))
                        last = mm(PS[u][:TOK, 0, hd * W:(hd + 1) * W], kPT[u][:TOK, hd * TOK:(hd + 1) * TOK],
                                  vS[u][:TOK, hd * W:(hd + 1) * W], start=True, stop=True)
                    last.then_inc(av, 1)
                    yield 25.5 + z
                    pe.wait_ge(attended, nth(i, k, 2, u))
                    turn(u, "f", chunks(o[u]))
                    yield 26.5 + z
                    pe.wait_ge(turn_copied["f"], nth(i, 2 * k + 1, TC, u))
                    rows_product(u, 1, C[f"wo{k}"], E).then_inc(projected["f"], 1)

                yield 65.5
                pe.wait_ge(norm["f"], nth(i, 1, LNF, u))
                turn(u, "f", chunks(xa[u]))
                yield 66.5
                pe.wait_ge(landed["l0f"], 16)
                pe.wait_ge(turn_copied["f"], nth(i, 4, TC, u))
                rows_product(u, 0, C["w_gate0"], NE0).then_inc(gate["f"], 1)
                for j in range(4):
                    yield (66.6, 68.5, 70.5, 76)[j]
                    if j == 3:
                        pe.wait_ge(exp_read, nth(i, 0, 4, u))
                    for c in range(KC):
                        last = mm(PS[u][:TOK, 1 + j % 3, :], xT[u][:, c * TOK:(c + 1) * TOK],
                                  C["w_exp0"][:, c * NE0 * E + j * 512:c * NE0 * E + (j + 1) * 512],
                                  start=(c == 0), stop=(c == KC - 1))
                    last.then_inc(experts, 1)
                    if j == 2:
                        yield 72
                        pe.wait_ge(c_ready, nth(i, 0, 1, u))
                        tp(PS[u][:NE0, 0, 128:128 + TOK], cw[u][:TOK, :], C["turner"][:TOK, :TOK]).then_inc(c_turned, 1)
                        yield 73
                        pe.wait_ge(c_copied, nth(i, 0, 1, u))
                        mm(PS[u][:TOK, 0, 256:512], cT[u][:NE0, :], C["b_exp0"][:NE0, :], start=True, stop=True).then_inc(bias_ready, 1)

            def back(u, i):
                yield 0
                pe.wait_ge(norm["b"], nth(i, 0, LNB, u))
                turn(u, "b", chunks(xn[u]))
                yield 1
                pe.wait_ge(landed["l1"], 16)
                pe.wait_ge(turn_copied["b"], nth(i, 0, TB, u))
                x0 = [xT[u][:, c * TOK:(c + 1) * TOK] for c in range(KC)]
                rows_product(u, 0, C["w_gate1"], MEM).then_inc(gate["b"], 1)
                rows_product(u, 1, C["w_g"], E).then_inc(g_prod, 1)
                yield 2.5
                for n, (w, m) in enumerate((("wq", 128), ("wks", 128), ("wgk1s", LOW))):
                    for c in range(KC):
                        last = mm(PS[u][:m, 2, n * TOK:(n + 1) * TOK], C[w][:, c * m:(c + 1) * m], x0[c], start=(c == 0), stop=(c == KC - 1))
                last.then_inc(sh_prod, 1)
                yield 4
                rows_product(u, 3, C["wvs"], E).then_inc(vs_prod, 1)
                yield 6
                pe.wait_ge(routed, nth(i, 0, 1, u))
                mm(PS[u][:TOK, 0, 8:8 + MEM], C["upto"][:TOK, :], rt[u][:TOK, :], start=True, stop=True)
                mm(PS[u][:TOK, 0, 12:12 + MEM], C["same"][:TOK, :], rt[u][:TOK, :], start=True, stop=True).then_inc(counted, 1)
                yield 9
                pe.wait_ge(onehot, nth(i, 0, 1, u))
                pe.wait_ge(g_copied, nth(i, 0, 1, u))
                for c in range(KC):
                    last = mm(PS[u][:, 1, c * 256:(c + 1) * 256], xn[u][:TOK, c * 128:(c + 1) * 128], OH[u][:TOK, :], start=True, stop=True)
                last.then_inc(gathered, 1)
                yield 10.5
                pe.wait_ge(weighted, nth(i, 0, 1, u))
                pe.wait_ge(sh_copied, nth(i, 1, 2, u))
                for c in range(PAIRM):
                    last = tp(PS[u][:, 3, c * TOK:(c + 1) * TOK], OHw[u][:TOK, c * 128:(c + 1) * 128], C["turner"][:TOK, :TOK])
                last.then_inc(oh_turned, 1)
                yield 11.5
                pe.wait_ge(xg_copied, nth(i, 0, 1, u))
                for m in range(MEM):
                    for c in range(KC):
                        last = mm(PS[u][:LOW, 0, m * SLOT:(m + 1) * SLOT], C["wgk1"][:, (c * MEM + m) * LOW:(c * MEM + m + 1) * LOW],
                                  xg[u][:, c * 256 + m * SLOT:c * 256 + (m + 1) * SLOT], start=(c == 0), stop=(c == KC - 1))
                last.then_inc(z1_prod, 1)
                yield 12.5
                for c in range(KC):
                    mm(PS[u][:, 1, 0:256], C["wq"][:, c * 128:(c + 1) * 128], xg[u][:, c * 256:(c + 1) * 256], start=(c == 0), stop=(c == KC - 1))
                for m in range(MEM):
                    for c in range(KC):
                        last = mm(PS[u][:, 1, 256 + m * SLOT:256 + (m + 1) * SLOT], C["wk"][:, (c * MEM + m) * 128:(c * MEM + m + 1) * 128],
                                  xg[u][:, c * 256 + m * SLOT:c * 256 + (m + 1) * SLOT], start=(c == 0), stop=(c == KC - 1))
                last.then_inc(qm_prod, 1)
                yield 14
                pe.wait_ge(z1_copied, nth(i, 0, 1, u))
                pe.wait_ge(oh_copied, nth(i, 0, 1, u))
                for m in range(MEM):
                    mm(PS[u][:, 3, m * SLOT:(m + 1) * SLOT], C["wgk2"][:LOW, m * 128:(m + 1) * 128], z1M[u][:LOW, m * SLOT:(m + 1) * SLOT], start=True, stop=True)
                mm(PS[u][:, 3, 256:256 + TOK], C["wgk2s"][:LOW, :], z1S[u][:LOW, :], start=True, stop=True).then_inc(z2_prod, 1)
                yield 16
                for m in range(MEM):
                    for c in range(KC):
                        p = (m % 2) * SLOT
                        last = mm(PS[u][p:p + SLOT, 2, (m // 2) * E:(m // 2 + 1) * E],
                                  xg[u][:, c * 256 + m * SLOT:c * 256 + (m + 1) * SLOT],
                                  C["wv"][:, (c * MEM + m) * E:(c * MEM + m + 1) * E], start=(c == 0), stop=(c == KC - 1),
                                  skip_group_check=True)
                last.then_inc(vm_prod, 1)
                yield 30
                pe.wait_ge(mem_prod, nth(i, 0, 1, u))
                for mp in range(PAIRM):
                    for t in range(CAP):
                        if mp + t and t % 3 == 0:
                            yield 30 + (mp * CAP + t) * 0.4
                        last = mm(PS[u][:, 0, mp * 36 + 4 * t:mp * 36 + 4 * t + 4],
                                  U[u][:, t * MEM * SLOT + mp * 128:t * MEM * SLOT + (mp + 1) * 128], C["hsel"], start=True, stop=True)
                last.then_inc(a_prod, 1)
                for t in range(S):
                    if t % 4 == 0:
                        yield 37.5 + t * 0.4
                    if t == 0:
                        pe.wait_ge(sh_pairs, nth(i, 0, 1, u))
                    last = mm(PS[u][:TOK, 3, 4 * t:4 + 4 * t], U[u][:, DM + t * TOK:DM + (t + 1) * TOK], C["hsel"], start=True, stop=True)
                last.then_inc(a_prod, 1)
                yield 44.5
                pe.wait_ge(a_spread, nth(i, 0, 2, u))
                pe.wait_ge(qm_copied, nth(i, 1, 2, u))
                for mp in range(PAIRM):
                    for hd in range(H1):
                        last = mm(PS[u][:, 1, mp * E + hd * DV:mp * E + (hd + 1) * DV], AbM[u][:, (mp * H1 + hd) * 128:(mp * H1 + hd + 1) * 128],
                                  vM[u][:, mp * E + hd * DV:mp * E + (hd + 1) * DV], start=True, stop=True)
                last.then_inc(om_prod, 1)
                yield 48.5
                pe.wait_ge(om_copied, nth(i, 0, 1, u))
                pe.wait_ge(a_spread, nth(i, 1, 2, u))
                for mp in range(PAIRM):
                    mm(PS[u][:TOK, 2, 0:E], ohT[u][:, mp * TOK:(mp + 1) * TOK], oM[u][:, mp * E:(mp + 1) * E],
                       start=(mp == 0), stop=False, skip_group_check=True)
                for hd in range(H1):
                    last = mm(PS[u][:TOK, 2, hd * DV:(hd + 1) * DV], AbS[u][:TOK, hd * TOK:(hd + 1) * TOK],
                              vsh[u][:TOK, hd * DV:(hd + 1) * DV], start=False, stop=(hd == H1 - 1), skip_group_check=True)
                last.then_inc(o_prod, 1)
                yield 55
                pe.wait_ge(gated, nth(i, 0, 1, u))
                turn(u, "b", chunks(oS[u]))
                yield 56
                pe.wait_ge(turn_copied["b"], nth(i, 1, TB, u))
                rows_product(u, 1, C["w_o"], E).then_inc(projected["b"], 1)
                yield 60
                pe.wait_ge(norm["b"], nth(i, 1, LNB, u))
                turn(u, "b", chunks(xn[u]))
                yield 61
                pe.wait_ge(turn_copied["b"], nth(i, 2, TB, u))
                rows_product(u, 1, C["sg"], FF).then_inc(up_prod, 1)
                rows_product(u, 0, C["w_r"], NE1).then_inc(gate["b"], 1)
                yield 62.7
                rows_product(u, 2, C["su"], FF).then_inc(up_prod, 1)
                yield 69
                pe.wait_ge(inner_ready, nth(i, 0, 1, u))
                for c in range(4):
                    last = tp(PS[u][:, 3, c * TOK:(c + 1) * TOK], hm[u][:TOK, c * 128:(c + 1) * 128], C["turner"][:TOK, :TOK])
                last.then_inc(inner_turned, 1)
                yield 70.5
                pe.wait_ge(inner_copied, nth(i, 0, 1, u))
                for c in range(4):
                    last = mm(PS[u][:TOK, 1, 0:E], hmT[u][:, c * TOK:(c + 1) * TOK], C["sd"][:, c * E:(c + 1) * E], start=(c == 0), stop=(c == 3))
                last.then_inc(projected["b"], 1)

            all_groups(pe, begin, front, back)

        @block.scalar
        def _(act):
            A = nc.scalar.activation
            nc.scalar.preload_act_table_set("natural_log_exp_and_others")
            act.wait_ge(landed["l0"], 16)

            def copy_turn(u, half, value, bank=3, to=0):
                act.wait_ge(turned[half], value)
                return A(xT[u][:, to * TOK:(to + 2) * TOK], PS[u][:, bank, 0:2 * TOK], ACT.Copy)

            def softmax_exp(u, half, value, n, dst):
                act.wait_ge(logits[half], value)
                A(dst[u][:TOK, 0:n], d8[u][:TOK, 0:n], ACT.Exp, accum_out=ssum[u][:TOK, :]).then_inc(softmaxed[half], 1)

            def front(u, i):
                for k in (0, 1):
                    z = 35 * k
                    if k == 0:
                        yield 0.5
                        copy_turn(u, "f", nth(i, 0, TF, u)).then_inc(turn_copied["f"], 1)
                    else:
                        yield 32
                        copy_turn(u, "f", nth(i, 2, TF, u))
                        yield 33.5
                        copy_turn(u, "f", nth(i, 3, TF, u), bank=0, to=2).then_inc(turn_copied["f"], 1)
                    yield 3.5 + z
                    act.wait_ge(qkv, nth(i, 2 * k, 4, u))
                    for j in (2, 3, 0, 1):
                        dst = (qT if j < 2 else kT)[u]
                        last = A(dst[:, (j % 2) * TOK:(j % 2 + 1) * TOK], PS[u][:, j // 2, (j % 2) * TOK:(j % 2 + 1) * TOK],
                                 ACT.Identity, bias=C[f"bqk{k}"][:, j:j + 1])
                        if j:
                            last.then_inc(qk_copied, 1)
                    for hf in (0, 1):
                        yield 11.5 + z + 2.2 * hf
                        act.wait_ge(shifted, nth(i, 2 * k + hf, 4, u))
                        s = dA[u][:TOK, hf * 8 * TOK:(hf + 1) * 8 * TOK]
                        A(s, s, ACT.Exp, scale=float(D0) ** -0.5).then_inc(exped, 1)
                    yield 14.5 + z
                    act.wait_ge(p_turned, nth(i, 2 * k, 4, u))
                    A(view(kPT[u][:TOK], 0, [4 * TOK, 2], [1, 4 * TOK]), view(PS[u][:TOK, 0, :], 0, [512, 2], [1, 4 * TOK]), ACT.Copy).then_inc(pt_act, 1)
                    yield 26 + z
                    copy_turn(u, "f", nth(i, 1 if k == 0 else 4, TF, u)).then_inc(turn_copied["f"], 1)
                yield 66
                copy_turn(u, "f", nth(i, 5, TF, u)).then_inc(turn_copied["f"], 1)
                yield 68
                softmax_exp(u, "f", nth(i, 0, 1, u), NE0, pr)
                yield 72.5
                act.wait_ge(c_turned, nth(i, 0, 1, u))
                A(cT[u][:NE0, :], PS[u][:NE0, 0, 128:128 + TOK], ACT.Copy).then_inc(c_copied, 1)

            def back(u, i):
                own = Steps(act, own_b["act"])

                def sigmoid_parts(k, g, dst, at):
                    own.mark(A(dst, g, ACT.Abs))
                    own.wait()
                    own.mark(A(dst, dst, ACT.Exp, scale=-1.0))
                    own.wait()
                    A(dst, dst, ACT.Ln, bias=1.0).then_inc(sig_out, 1)
                    yield at + 2
                    act.wait_ge(sig_in, nth(i, k, 2, u))
                    A(dst, dst, ACT.Exp).then_inc(sig_out, 1)

                yield 0.5
                copy_turn(u, "b", nth(i, 0, TB, u)).then_inc(turn_copied["b"], 1)
                yield 2.5
                softmax_exp(u, "b", nth(i, 0, 2, u), MEM, pr4)
                yield 3.5
                act.wait_ge(g_prod, nth(i, 0, 1, u))
                A(gs[u][:TOK, :], PS[u][:TOK, 1, 0:E], ACT.Copy).then_inc(g_copied, 1)
                yield 4
                act.wait_ge(sh_prod, nth(i, 0, 1, u))
                A(qS[u][:], PS[u][:, 2, 0:TOK], ACT.Copy, scale=QSCALE1)
                A(kS[u][:], PS[u][:, 2, TOK:2 * TOK], ACT.Copy)
                A(z1S[u][:LOW, :], PS[u][:LOW, 2, 2 * TOK:3 * TOK], ACT.Copy).then_inc(sh_copied, 1)
                yield 5.5
                act.wait_ge(vs_prod, nth(i, 0, 1, u))
                A(vsh[u][:TOK, :], PS[u][:TOK, 3, 0:E], ACT.Copy).then_inc(sh_copied, 1)
                yield 6.5
                act.wait_ge(g_copied, nth(i, 0, 1, u))
                yield from sigmoid_parts(0, gs[u][:TOK, :], egs[u][:TOK, :], 6.5)
                yield 10.8
                act.wait_ge(gathered, nth(i, 0, 1, u))
                A(xg[u][:], PS[u][:, 1, :], ACT.Copy).then_inc(xg_copied, 1)
                yield 11.4
                act.wait_ge(oh_turned, nth(i, 0, 1, u))
                A(ohT[u][:], PS[u][:, 3, 0:PAIRM * TOK], ACT.Copy).then_inc(oh_copied, 1)
                yield 12.5
                act.wait_ge(z1_prod, nth(i, 0, 1, u))
                A(z1M[u][:LOW, :], PS[u][:LOW, 0, 0:256], ACT.Copy).then_inc(z1_copied, 1)
                yield 14.5
                act.wait_ge(qm_prod, nth(i, 0, 1, u))
                A(view(qP[u][:], 0, [SEQS, MEM], [1, SEQS], [MEM * SEQS, CAP]), view(PS[u][:, 1, :], 0, [SLOT, MEM], [CAP, SEQS], [1, CAP]),
                  ACT.Copy, scale=QSCALE1)
                A(kM[u][:], PS[u][:, 1, 256:512], ACT.Copy).then_inc(qm_copied, 1)
                yield 16
                act.wait_ge(zabs, nth(i, 0, 1, u))
                own.mark(A(az[u], az[u], ACT.Exp, scale=-1.0))
                own.wait()
                A(az[u], az[u], ACT.Ln, bias=1.0).then_inc(lned, 1)
                yield 17.5
                act.wait_ge(vm_prod, nth(i, 0, 1, u))
                A(vM[u][:], PS[u][:, 2, :], ACT.Copy).then_inc(qm_copied, 1)
                yield 21
                act.wait_ge(exponents, nth(i, 0, 2, u))
                A(U[u][:, 0:DM], Dp[:, 0:DM], ACT.Exp, scale=1.0 / GATE_NORM).then_inc(dexped_m, 1)
                yield 23.5
                act.wait_ge(exponents, nth(i, 1, 2, u))
                A(U[u][:, DM:DALL], Dp[:, DM:DALL], ACT.Exp, scale=1.0 / GATE_NORM).then_inc(dexped[u], 1)
                yield 48
                act.wait_ge(om_prod, nth(i, 0, 1, u))
                A(oM[u][:], PS[u][:, 1, :], ACT.Copy).then_inc(om_copied, 1)
                yield 55.5
                copy_turn(u, "b", nth(i, 1, TB, u)).then_inc(turn_copied["b"], 1)
                yield 60.5
                copy_turn(u, "b", nth(i, 2, TB, u)).then_inc(turn_copied["b"], 1)
                yield 62.5
                act.wait_ge(up_prod, nth(i, 0, 2, u))
                yield from sigmoid_parts(1, PS[u][:TOK, 1, :], eg[u][:TOK, :], 63.5)
                yield 65.6
                softmax_exp(u, "b", nth(i, 1, 2, u), NE1, pr)
                yield 70
                act.wait_ge(inner_turned, nth(i, 0, 1, u))
                A(hmT[u][:], PS[u][:, 3, 0:4 * TOK], ACT.Copy).then_inc(inner_copied, 1)
                own.end()

            all_groups(act, None, front, back)

        @block.gpsimd
        def _(pool):
            G = nc.gpsimd
            for u in UU:
                G.memset(vS[u][:], 1.0)
                G.memset(pr4[u][:], -1.0)
                G.memset(AbM[u][:], 0.0)
            G.memset(roots[:], -0.5)
            G.memset(zeros[:], 0.0)
            G.memset(Dp[:], FAR).then_inc(pool_ready, 1)
            for u in UU:
                pool.sem_inc(x_stored[u], 16)
            pool.sem_inc(dexped[1], 1)
            pool.wait_ge(pool_ready, 1)

            def inverse_root(u, half, value):
                pool.wait_ge(stats[half], value)
                G.tensor_tensor(rstd[u][:TOK, :], ve[u][:TOK, :], roots[:TOK, 0:1], ALU.pow).then_inc(rstd_ready[half], 1)

            def begin(u, i):
                yield 77
                inverse_root(u, "a", nth(i, 0, 1, u))

            def front(u, i):
                for k in (0, 1):
                    z = 35 * k
                    yield (0, 33)[k]
                    pool.wait_ge(landed["l0"], 16)
                    if k == 0:
                        pool.wait_ge(norm["a"], nth(i, 0, 1, u))
                    else:
                        pool.wait_ge(norm["f"], nth(i, 0, LNF, u))
                    G.tensor_tensor(hb[u][:TOK, :], (h, xa)[k][u][:TOK, :], C[f"bo{k}"][:TOK, :], ALU.add).then_inc(res_ready, 1)
                    yield 4 + z
                    pool.wait_ge(qk_copied, nth(i, 3 * k, 6, u))
                    G.tensor_tensor(view(kPT[u], 0, [TOK, 8], [1, TOK]), view(kT[u], 0, [0, 8], [1, TOK]),
                                    view(C["headmask"], 0, [1, 8], [0, TOK]), ALU.mult).then_inc(km_pool, 1)
                    yield 29.5 + z
                    inverse_root(u, "f", nth(i, k, ROOTS, u))
                yield 81.5
                inverse_root(u, "f", nth(i, 2, ROOTS, u))
                yield 84.5
                inverse_root(u, "f", nth(i, 3, ROOTS, u))

            def back(u, i):
                own = Steps(pool, own_b["pool"])
                yield 9
                pool.wait_ge(onehot, nth(i, 0, 1, u))
                G.tensor_tensor(view(OHw[u][:TOK], 0, [SLOT, MEM], [1, SLOT]), view(OH[u][:TOK], 0, [SLOT, MEM], [1, SLOT]),
                                view(w2[u][:TOK], 0, [1, MEM], [0, SLOT]), ALU.mult).then_inc(weighted, 1)
                yield 25.5
                pool.wait_ge(dexped[u], i + 1 + u)
                e = view(U[u][:], DM, [TOK, S], [1, TOK])
                own.mark(G.tensor_tensor(e, e, view(kS[u][:], 0, [0, S], [1, TOK]), ALU.mult))
                own.wait()
                e = view(U[u][:], DM, [TOK, S], [S, SEQS], [1, S])
                G.tensor_tensor(e, e, view(qS[u][:], 0, [1, S], [S, SEQS], [0, S]), ALU.mult).then_inc(sh_pairs, 1)
                yield 34
                pool.wait_ge(landed["l1"], 16)
                pool.wait_ge(gs_ready, nth(i, 0, 1, u))
                G.tensor_tensor(gs[u][:TOK, :], gs[u][:TOK, :], C["norm_w"][:TOK, :], ALU.mult).then_inc(gs_scaled, 1)
                yield 52
                pool.wait_ge(rms_ms, nth(i, 0, 1, u))
                G.tensor_tensor(rs4[u][:TOK, :], mse[u][:TOK, :], roots[:TOK, 0:4], ALU.pow).then_inc(rms_ready, 1)
                yield 58.2
                inverse_root(u, "b", nth(i, 0, 1, u))
                own.end()

            all_groups(pool, begin, front, back)

        @block.vector
        def _(dve):
            V = nc.vector
            TT, TS, STT = V.tensor_tensor, V.tensor_scalar, V.scalar_tensor_tensor
            dve.wait_ge(pool_ready, 1)
            dve.wait_ge(landed["route"], 16)

            def statistics(own, u, half, src):
                own.wait()
                own.mark(V.bn_stats(st[u][:TOK, :], src[u][:TOK, :]))
                own.wait()
                own.mark(V.bn_aggr(mv[u][:TOK, :], st[u][:TOK, :]))
                own.wait()
                TS(ve[u][:TOK, :], mv[u][:TOK, 1:2], EPS, None, ALU.add).then_inc(stats[half], 1)

            def normalize(u, half, src, dst):
                TS(dst[u][:TOK, :], src[u][:TOK, :], mv[u][:TOK, 0:1], rstd[u][:TOK, :], ALU.subtract, ALU.mult).then_inc(norm[half], 1)

            def weighted_norm(own, u, value, src, dst, w, b):
                own.wait()
                own.mark(STT(src[u][:TOK, :], src[u][:TOK, :], mv[u][:TOK, 0:1], C[w][:TOK, :], ALU.subtract, ALU.mult))
                own.wait()
                dve.wait_ge(rstd_ready["f"], value)
                return STT(dst[u][:TOK, :], src[u][:TOK, :], rstd[u][:TOK, :], C[b][:TOK, :], ALU.mult, ALU.add)

            def top_two(own, u, half, value, n, p, at):
                own.wait()
                own.mark(V.tensor_reduce(mxs[u][:TOK, :], lg[u][:TOK, 0:n], AX.X, ALU.max))
                own.wait()
                TS(d8[u][:TOK, 0:n], lg[u][:TOK, 0:n], mxs[u][:TOK, :], None, ALU.subtract).then_inc(logits[half], 1)
                yield at
                dve.wait_ge(softmaxed[half], value)
                own.mark(V.reciprocal(rsum[u][:TOK, :], ssum[u][:TOK, :]))
                own.wait()
                own.mark(TS(p[u][:TOK, 0:n], p[u][:TOK, 0:n], rsum[u][:TOK, :], None, ALU.mult))
                own.wait()
                own.mark(V.max(mx8[u][:TOK, :], p[u][:TOK, :]))
                own.wait()
                own.mark(V.max_index(ix[u][:TOK, :], mx8[u][:TOK, :], p[u][:TOK, :]))
                own.wait()
                own.mark(V.tensor_copy(ixf[u][:TOK, :], ix[u][:TOK, 0:2]))
                own.wait()
                if half == "f" or n == MEM:
                    STT(c0[u][:TOK, 0:n], C["eight"][:TOK, 0:n], ixf[u][:TOK, 0:1], p[u][:TOK, 0:n], ALU.is_equal, ALU.mult)
                    own.mark(STT(c1[u][:TOK, 0:n], C["eight"][:TOK, 0:n], ixf[u][:TOK, 1:2], p[u][:TOK, 0:n], ALU.is_equal, ALU.mult))

            def begin(u, i):
                own = Steps(dve, own_b["dve"])
                yield 75.5
                dve.wait_ge(x_stored[u], i * 16 + 16)
                dve.wait_ge(tok_used[u], i + 1)
                own.mark(V.tensor_copy(h[u][:TOK, :], PS[u][:TOK, 0, 0:E]))
                statistics(own, u, "a", h)
                yield 78
                dve.wait_ge(rstd_ready["a"], nth(i, 0, 1, u))
                normalize(u, "a", h, xn)
                own.end()

            def front(u, i):
                own = Steps(dve, own_f["dve"])
                mark, wait = own.mark, own.wait
                for k in (0, 1):
                    z = 35 * k
                    yield 4 + z
                    dve.wait_ge(landed["l0"], 16)
                    dve.wait_ge(qkv, nth(i, 2 * k + 1, 4, u))
                    TT(view(vS[u][:TOK], 0, [D0 + 1, H0], [1, D0]), view(PS[u][:TOK, 2, :], 0, [D0, H0], [1, D0]),
                       view(C[f"bv{k}"][:TOK], 0, [D0, H0], [1, D0]), ALU.add).then_inc(v_copied, 1)
                    yield 4.5 + z
                    dve.wait_ge(qk_copied, nth(i, 3 * k + 1, 6, u))
                    TT(view(kPT[u], 8 * TOK, [TOK, 8], [1, TOK]), view(kT[u], TOK, [0, 8], [1, TOK]),
                       view(C["headmask"], 0, [1, 8], [0, TOK]), ALU.mult).then_inc(km_dve, 1)
                    for hf in (0, 1):
                        yield 9 + z + 2.3 * hf
                        dve.wait_ge(scores, nth(i, 2 * k + hf, 4, u))
                        s = view(PS[u][:TOK, 2 * hf, :], 0, [512, 2], [TOK, 4], [1, TOK])
                        mark(V.tensor_reduce(mxh[u][:TOK, 8 * hf:8 * hf + 8], s, AX.X, ALU.max))
                        wait()
                        TT(view(dA[u][:TOK], 8 * hf * TOK, [4 * TOK, 2], [TOK, 4], [1, TOK]), s, view(mxh[u][:TOK], 8 * hf, [4, 2], [1, 4], [0, TOK]),
                           ALU.subtract).then_inc(shifted, 1)
                    yield 16.5 + z
                    dve.wait_ge(p_turned, nth(i, 2 * k + 1, 4, u))
                    V.tensor_copy(view(kPT[u][:TOK], 8 * TOK, [4 * TOK, 2], [1, 4 * TOK]),
                                  view(PS[u][:TOK, 2, :], 0, [512, 2], [1, 4 * TOK])).then_inc(pt_dve, 1)
                    yield 24.5 + z
                    dve.wait_ge(av, nth(i, k, 2, u))
                    mark(V.reciprocal(rden[u][:TOK, :], view(PS[u][:TOK, 0, :], D0, [D0 + 1, H0])))
                    wait()
                    TT(view(o[u][:TOK], 0, [D0, H0], [1, D0]), view(PS[u][:TOK, 0, :], 0, [D0 + 1, H0], [1, D0]),
                       view(rden[u][:TOK], 0, [1, H0], [0, D0]), ALU.mult).then_inc(attended, 1)
                    yield 28 + z
                    dve.wait_ge(projected["f"], nth(i, k, 2, u))
                    dve.wait_ge(res_ready, nth(i, k, 2, u))
                    dst = (h, xn)[k]
                    mark(TT(dst[u][:TOK, :], PS[u][:TOK, 1, 0:E], hb[u][:TOK, :], ALU.add))
                    statistics(own, u, "f", dst)
                    if k == 0:
                        yield 30.8
                        dve.wait_ge(rstd_ready["f"], nth(i, 0, ROOTS, u))
                        normalize(u, "f", h, xa)
                        dve.wait_ge(norm["f"], nth(i, 0, LNF, u))
                        TT(rq[u][:TOK, :], xa[u][:TOK, :], C["rope_cos"][:TOK, :], ALU.mult)
                        TT(view(rr[u][:TOK], 0, [2, 128]), view(xa[u][:TOK], 1, [2, 128]), C["rope_sin"][:TOK, :], ALU.mult)
                        mark(TT(view(rr[u][:TOK], 1, [2, 128]), view(xa[u][:TOK], 0, [2, 128]), C["rope_sin"][:TOK, :], ALU.mult))
                        wait()
                        TT(view(rr[u][:TOK], 0, [2, 128]), view(rq[u][:TOK], 0, [2, 128]), view(rr[u][:TOK], 0, [2, 128]), ALU.subtract)
                        TT(view(rr[u][:TOK], 1, [2, 128]), view(rq[u][:TOK], 1, [2, 128]), view(rr[u][:TOK], 1, [2, 128]), ALU.add).then_inc(roped, 1)
                    else:
                        yield 65
                        dve.wait_ge(landed["l0f"], 16)
                        weighted_norm(own, u, nth(i, 1, ROOTS, u), xn, xa, "ln1_w", "ln1_b").then_inc(norm["f"], 1)

                yield 67
                dve.wait_ge(gate["f"], nth(i, 0, 1, u))
                mark(TT(lg[u][:TOK, :], PS[u][:TOK, 0, 0:NE0], C["b_gate0"][:TOK, :], ALU.add))
                yield from top_two(own, u, "f", nth(i, 0, 1, u), NE0, pr, 68.5)
                wait()
                TT(cw[u][:TOK, :], c0[u][:TOK, :], c1[u][:TOK, :], ALU.add).then_inc(c_ready, 1)
                for j in range(4):
                    yield (71, 72, 73.5, 78)[j]
                    for e in range(2):
                        if j == 0 and e == 0:
                            dve.wait_ge(c_ready, nth(i, 0, 1, u))
                        elif e == 0:
                            dve.wait_ge(exp_read, nth(i, j - 1, 4, u))
                        else:
                            wait()
                        if e == 0:
                            dve.wait_ge(experts, nth(i, j, 4, u))
                        ins = STT(acc[u][:TOK, :], PS[u][:TOK, 1 + j % 3, e * E:(e + 1) * E], cw[u][:TOK, 2 * j + e:2 * j + e + 1],
                                  (xa if (j, e) == (0, 0) else acc)[u][:TOK, :], ALU.mult, ALU.add)
                        if e == 0:
                            mark(ins)
                        else:
                            ins.then_inc(exp_read, 1)
                yield 79
                dve.wait_ge(bias_ready, nth(i, 0, 1, u))
                dve.wait_ge(exp_read, nth(i, 3, 4, u))
                mark(TT(acc[u][:TOK, :], acc[u][:TOK, :], PS[u][:TOK, 0, 256:512], ALU.add))
                statistics(own, u, "f", acc)
                yield 82
                mark(weighted_norm(own, u, nth(i, 2, ROOTS, u), acc, xa, "ln2_w", "ln2_b"))
                wait()
                mark(TT(h[u][:TOK, :], h[u][:TOK, :], xa[u][:TOK, :], ALU.add))
                statistics(own, u, "f", h)
                own.end()

            def back(u, i):
                own = Steps(dve, own_b["dve"])
                mark, wait = own.mark, own.wait

                def sigmoid(k, g, e, at):
                    yield at
                    dve.wait_ge(sig_out, nth(i, 2 * k, 4, u))
                    STT(e, g, 0.0, e, ALU.min, ALU.subtract).then_inc(sig_in, 1)
                    yield at + 1.5
                    dve.wait_ge(sig_out, nth(i, 2 * k + 1, 4, u))

                yield 0
                dve.wait_ge(rstd_ready["f"], nth(i, 3, ROOTS, u))
                normalize(u, "b", h, xn)
                yield 1.5
                dve.wait_ge(gate["b"], nth(i, 0, 2, u))
                mark(V.tensor_copy(lg[u][:TOK, 0:MEM], PS[u][:TOK, 0, 0:MEM]))
                yield from top_two(own, u, "b", nth(i, 0, 2, u), MEM, pr4, 3)
                mark(TS(t9[u][:TOK, :], C["eight"][:TOK, 0:MEM], ixf[u][:TOK, 0:1], None, ALU.is_equal))
                wait()
                STT(rt[u][:TOK, :], C["eight"][:TOK, 0:MEM], ixf[u][:TOK, 1:2], t9[u][:TOK, :], ALU.is_equal, ALU.add).then_inc(routed, 1)
                mark(TT(p12[u][:TOK, :], mx8[u][:TOK, 0:1], mx8[u][:TOK, 1:2], ALU.add))
                wait()
                mark(V.reciprocal(rp[u][:TOK, :], p12[u][:TOK, :]))
                mark(TT(w2[u][:TOK, :], c0[u][:TOK, 0:MEM], c1[u][:TOK, 0:MEM], ALU.add))
                wait()
                mark(TS(w2[u][:TOK, :], w2[u][:TOK, :], rp[u][:TOK, :], None, ALU.mult))
                yield 6.5
                dve.wait_ge(landed["l1"], 16)
                dve.wait_ge(counted, nth(i, 0, 1, u))
                mark(TS(t9[u][:TOK, :], PS[u][:TOK, 0, 12:16], -float(CAP), 0.0, ALU.add, ALU.max))
                wait()
                mark(TT(s1[u][:TOK, :], PS[u][:TOK, 0, 8:12], t9[u][:TOK, :], ALU.subtract))
                wait()
                mark(STT(vd[u][:TOK, :], s1[u][:TOK, :], 1.0, rt[u][:TOK, :], ALU.is_ge, ALU.mult))
                wait()
                mark(STT(code[u][:TOK, :], s1[u][:TOK, :], C["seq9"][:TOK, :], vd[u][:TOK, :], ALU.add, ALU.mult))
                wait()
                TT(view(OH[u][:TOK], 0, [SLOT, MEM], [1, SLOT]), view(C["iota64"][:TOK], 0, [0, MEM], [1, SLOT]),
                   view(code[u][:TOK], 0, [1, MEM], [0, SLOT]), ALU.is_equal).then_inc(onehot, 1)
                yield from sigmoid(0, gs[u][:TOK, :], egs[u][:TOK, :], 9)
                TT(gs[u][:TOK, :], egs[u][:TOK, :], gs[u][:TOK, :], ALU.mult).then_inc(gs_ready, 1)
                yield 15
                dve.wait_ge(z2_prod, nth(i, 0, 1, u))
                TT(view(zz[u], 0, [SLOT, MEM], [1, SLOT]), view(PS[u][:, 3, :], 0, [SLOT, MEM], [1, SLOT]),
                   view(C["bgk"], 0, [1, MEM], [0, SLOT]), ALU.add)
                mark(TS(zz[u][:, 256:NZ], PS[u][:, 3, 256:NZ], C["bgk"][:, MEM:MEM + 1], None, ALU.add))
                wait()
                STT(az[u], zz[u], -1.0, zz[u], ALU.mult, ALU.max).then_inc(zabs, 1)
                yield 17.5
                dve.wait_ge(lned, nth(i, 0, 1, u))
                mark(STT(lgz[u], zz[u], 0.0, az[u], ALU.min, ALU.subtract))
                wait()
                mark(V.tensor_tensor_scan(Gc[u][:], C["keep"], lgz[u], 0.0, ALU.mult, ALU.add))
                wait()
                dve.wait_ge(dexped[1 - u], i + 1)
                for t in range(CAP):
                    last = TT(view(Dp[:], t * MEM * SLOT, [SLOT, MEM], [CAP, SEQS], [1, t + 1]),
                              view(Gc[u][:], t, [SLOT, MEM], [CAP, SEQS], [0, t + 1]),
                              view(Gc[u][:], 0, [SLOT, MEM], [CAP, SEQS], [1, t + 1]), ALU.subtract)
                last.then_inc(exponents, 1)
                yield 20.5
                for t in range(S):
                    last = TT(view(Dp[:], DM + t * TOK, [S, SEQS], [1, t + 1]),
                              view(Gc[u][:], 256 + t, [S, SEQS], [0, t + 1]),
                              view(Gc[u][:], 256, [S, SEQS], [1, t + 1]), ALU.subtract)
                last.then_inc(exponents, 1)
                yield 24
                dve.wait_ge(dexped_m, nth(i, 0, 1, u))
                dve.wait_ge(qm_copied, nth(i, 0, 2, u))
                e = view(U[u][:], 0, [MEM * SLOT, CAP], [1, MEM * SLOT])
                mark(TT(e, e, view(kM[u][:], 0, [0, CAP], [1, MEM * SLOT]), ALU.mult))
                wait()
                yield 27
                e = view(U[u][:], 0, [SLOT, MEM * CAP], [CAP, SEQS], [1, CAP])
                TT(e, e, view(qP[u][:], 0, [SEQS, MEM * CAP], [1, SEQS], [0, CAP]), ALU.mult).then_inc(mem_prod, 1)
                yield 37.5
                dve.wait_ge(a_prod, nth(i, 0, 2, u))
                for m in range(MEM):
                    p, mp = (m % 2) * SLOT, m // 2
                    last = TT(view(AbM[u][p:p + SLOT], mp * H1 * 128 + (m % 2) * SLOT, [128, H1], [CAP, SEQS], [1, CAP]),
                              view(PS[u][p:p + SLOT, 0, :], mp * 36, [1, H1], [0, SEQS], [4, CAP]),
                              view(C["bmask9"][p:p + SLOT], 0, [0, H1], [1, SEQS], [0, CAP]), ALU.mult)
                last.then_inc(a_spread, 1)
                yield 44.5
                dve.wait_ge(a_prod, nth(i, 1, 2, u))
                TT(view(AbS[u][:TOK], 0, [TOK, H1], [S, SEQS], [1, S]), view(PS[u][:TOK, 3, :], 0, [1, H1], [0, SEQS], [4, S]),
                   view(C["bmask17"][:TOK], 0, [0, H1], [1, SEQS], [0, S]), ALU.mult).then_inc(a_spread, 1)
                yield 51
                dve.wait_ge(o_prod, nth(i, 0, 1, u))
                mark(V.tensor_copy(oS[u][:TOK, :], PS[u][:TOK, 2, 0:E]))
                wait()
                mark(TT(sq[u][:TOK, :], oS[u][:TOK, :], oS[u][:TOK, :], ALU.mult))
                wait()
                mark(V.tensor_reduce(ms[u][:TOK, :], view(sq[u][:TOK], 0, [DV, H1], [1, DV]), AX.X, ALU.add))
                wait()
                TS(mse[u][:TOK, :], ms[u][:TOK, :], 1.0 / DV, EPS, ALU.mult, ALU.add).then_inc(rms_ms, 1)
                yield 53.5
                dve.wait_ge(gs_scaled, nth(i, 0, 1, u))
                mark(TT(sq[u][:TOK, :], oS[u][:TOK, :], gs[u][:TOK, :], ALU.mult))
                wait()
                dve.wait_ge(rms_ready, nth(i, 0, 1, u))
                TT(view(oS[u][:TOK], 0, [DV, H1], [1, DV]), view(sq[u][:TOK], 0, [DV, H1], [1, DV]),
                   view(rs4[u][:TOK], 0, [1, H1], [0, DV]), ALU.mult).then_inc(gated, 1)
                yield 57
                dve.wait_ge(projected["b"], nth(i, 0, 2, u))
                mark(TT(h[u][:TOK, :], h[u][:TOK, :], PS[u][:TOK, 1, 0:E], ALU.add))
                statistics(own, u, "b", h)
                yield 59
                dve.wait_ge(rstd_ready["b"], nth(i, 0, 1, u))
                normalize(u, "b", h, xn)
                yield 62.8
                dve.wait_ge(gate["b"], nth(i, 1, 2, u))
                dve.wait_ge(up_prod, nth(i, 0, 2, u))
                mark(V.tensor_copy(lg[u][:TOK, :], PS[u][:TOK, 0, 0:NE1]))
                yield from sigmoid(1, PS[u][:TOK, 1, :], eg[u][:TOK, :], 65)
                mark(TT(eg[u][:TOK, :], eg[u][:TOK, :], PS[u][:TOK, 1, :], ALU.mult))
                yield 67
                wait()
                dve.wait_ge(up_prod, nth(i, 1, 2, u))
                TT(hm[u][:TOK, :], eg[u][:TOK, :], PS[u][:TOK, 2, :], ALU.mult).then_inc(inner_ready, 1)
                yield from top_two(own, u, "b", nth(i, 1, 2, u), NE1, pr, 70)
                V.tensor_copy(view(picked[:TOK], (2 * i + u) * 4, [1, 2]), ixf[u][:TOK, :])
                V.tensor_copy(view(picked[:TOK], (2 * i + u) * 4 + 2, [1, 2]), mx8[u][:TOK, 0:2])
                yield 72
                dve.wait_ge(projected["b"], nth(i, 1, 2, u))
                TT(view(h_all[:TOK], (2 * i + u) * E, [1, E]), h[u][:TOK, :], PS[u][:TOK, 1, 0:E], ALU.add)
                own.end()

            all_groups(dve, begin, front, back)

        block_ctx.close()
        phase1.close()
        expert_phase(nc, ctx, PS, C, arena, w_landed, h_all, picked, out_stored, experts_d, x_d, xs_d, y_d, out_d)


def expert_phase(nc, ctx, PS, C, arena, w_landed, h_all, picked, out_stored, experts_d, x_d, xs_d, y_d, out_d):
    def sb(name, shape, dt=F32):
        return ctx.enter_context(nc.sbuf_tensor(name, shape, dt))

    def sem(name):
        return ctx.enter_context(nc.semaphore(name))

    GE = GROUPS * NE1
    rows = sb("token_rows", [128, 2 * GROUPS * E])
    oh = [sb(f"oh{k}", [128, GE]) for k in (0, 1)]
    both, tot, cum, incl, pos = (sb(n, [128, GE]) for n in ("both", "tot", "cum", "incl", "pos"))
    psum_, wgt = sb("p_sum", [128, GROUPS]), [sb(f"wgt{k}", [128, GROUPS]) for k in (0, 1)]
    over, nt, tend, t128 = sb("over", [128, NE1 * FULL]), sb("nt", [128, NE1]), sb("tend", [128, NE1]), sb("t128", [128, NE1])
    posf, posu = sb("posf", [128, 2 * GROUPS]), sb("posu", [128, 2 * GROUPS], U32)
    past, tef, teu = sb("past", [128, TILES * NE1]), sb("tef", [128, TILES]), sb("teu", [128, TILES], mybir.dt.int32)
    xs, xsT, eg, hm, hmT, y = ([sb(f"{n}{u}", [128, w]) for u in (0, 1)]
                               for n, w in (("xs", E), ("xsT", E), ("ex", FF), ("hm2", FF), ("hmT2", FF), ("y", E)))
    x_back, rout, counts, placed, scattered, tile_exp = (sem(n) for n in (
        "x_back", "rout", "counts", "placed", "scattered", "tile_exp"))
    row_landed, y_stored = [sem(f"row_landed{u}") for u in (0, 1)], [sem(f"y_stored{u}") for u in (0, 1)]
    (r_turned, r_copied, gated, upped, logged, lowered, sigmoided, inner, i_turned, i_copied, downed, y_copied, dstep,
     astep) = (sem(n) for n in (
        "r_turned", "r_copied", "tile_gated", "upped", "logged", "lowered", "sigmoided", "inner", "i_turned",
        "i_copied", "downed", "y_copied", "dve_link", "act_link"))
    fetched = [sem(f"fetched{g}") for g in range(GROUPS)]
    summed = sem("summed")
    UU = (0, 1)

    def rows_of(g):
        return min(TOK, B * S - g * TOK)

    block = ctx.enter_context(nc.Block())

    @block.sync
    def _(sp):
        for g in range(GROUPS):
            sp.dma_start(rows[:rows_of(g), g * E:(g + 1) * E], x_d[g * TOK:g * TOK + rows_of(g), :]).then_inc(x_back, 16)
        for e in range(EARLY, NE1):
            sp.dma_start(arena[:, e * EW:(e + 1) * EW], experts_d[:, e * EW:(e + 1) * EW]).then_inc(w_landed, 16)
        sp.wait_ge(scattered, 2 * GROUPS * 16)
        for u in UU:
            sp.dma_start(xs[u][:], xs_d[u * 128:(u + 1) * 128, :]).then_inc(row_landed[u], 16)

        def store_results(i):
            for u in UU:
                sp.wait_ge(y_copied, 2 * i + u + 3)
                sp.dma_start(y_d[bass.ds((2 * i + u) * 128, 128), :], y[u][:]).then_inc(y_stored[u], 16)

        with sp.Fori(0, TILES // 2 - 1) as i:
            for u in UU:
                sp.wait_ge(r_turned, 2 * i + u + 1)
                sp.dma_start(xs[u][:], xs_d[bass.ds((2 * i + 2 + u) * 128, 128), :]).then_inc(row_landed[u], 16)
            store_results(i)
        store_results(TILES // 2 - 1)
        for g in range(GROUPS):
            sp.wait_ge(summed, g + 1)
            sp.dma_start(out_d[g * TOK:g * TOK + rows_of(g), :], h_all[:rows_of(g), g, :]).then_inc(out_stored, 16)
        sp.wait_ge(out_stored, GROUPS * 16)

    @block.tensor
    def _(pe):
        mm, tp = nc.tensor.matmul, nc.tensor.transpose
        pe.wait_ge(rout, 1)
        mm(PS[0][:TOK, 0, 0:GE], C["tri"][:TOK, :], both[:TOK, :], start=True, stop=True)
        mm(PS[0][:TOK, 0, GE:2 * GE], C["ones"][:TOK, :], both[:TOK, :], start=True, stop=True).then_inc(counts, 1)

        def turn_rows(u, landed):
            pe.wait_ge(row_landed[u], landed)
            tp(PS[u][:, 0, 0:128], xs[u][:, 0:128], C["turner"])
            tp(PS[u][:, 0, 128:256], xs[u][:, 128:256], C["turner"]).then_inc(r_turned, 1)

        def up(u, n, e_at):
            pe.wait_ge(r_copied, n)
            for p, ready in enumerate((gated, upped)):
                for c in range(KC):
                    last = mm(PS[u][:, 1 + p, :], xsT[u][:, c * 128:(c + 1) * 128],
                              view(arena[:], e_at + (p * KC + c) * FF, [1, FF]), start=(c == 0), stop=(c == KC - 1))
                last.then_inc(ready, 1)

        def turn_inner(u, n):
            pe.wait_ge(inner, n)
            for c in range(4):
                last = tp(PS[u][:, 3, c * 128:(c + 1) * 128], hm[u][:, c * 128:(c + 1) * 128], C["turner"])
            last.then_inc(i_turned, 1)

        def down(u, n, e_at, rows_read=None):
            pe.wait_ge(i_copied, n)
            if rows_read is not None:
                pe.wait_ge(r_copied, rows_read)
            for c in range(4):
                last = mm(PS[u][:, 0, 256:512], hmT[u][:, c * 128:(c + 1) * 128],
                          view(arena[:], e_at + 2 * KC * FF + c * E, [1, E]), start=(c == 0), stop=(c == 3))
            last.then_inc(downed, 1)

        def expert_of(j):
            return pe.value_load(teu[0:1, bass.ds(j, 1)], min_val=0, max_val=(NE1 - 1) * EW)

        pe.wait_ge(tile_exp, 1)
        turn_rows(0, 16)
        turn_rows(1, 16)
        pe.wait_ge(w_landed, NE1 * 16)
        up(0, 1, expert_of(0))
        with pe.Fori(0, TILES // 2 - 1) as i:
            e0, e1, e2 = expert_of(2 * i), expert_of(2 * i + 1), expert_of(2 * i + 2)
            up(1, 2 * i + 2, e1)
            turn_inner(0, 2 * i + 1)
            pe.wait_ge(y_copied, 2 * i + 1)
            turn_rows(0, i * 16 + 32)
            down(0, 2 * i + 1, e0, 2 * i + 3)
            up(0, 2 * i + 3, e2)
            turn_inner(1, 2 * i + 2)
            pe.wait_ge(y_copied, 2 * i + 2)
            turn_rows(1, i * 16 + 32)
            down(1, 2 * i + 2, e1, 2 * i + 4)
        e0, e1 = expert_of(TILES - 2), expert_of(TILES - 1)
        up(1, TILES, e1)
        turn_inner(0, TILES - 1)
        down(0, TILES - 1, e0)
        turn_inner(1, TILES)
        down(1, TILES, e1)

    @block.scalar
    def _(act):
        A = nc.scalar.activation

        def log_part(u, n):
            act.wait_ge(gated, n)
            A(eg[u][:], PS[u][:, 1, :], ACT.Abs).then_inc(astep, 1)
            act.wait_ge(astep, 2 * n - 1)
            A(eg[u][:], eg[u][:], ACT.Exp, scale=-1.0).then_inc(astep, 1)
            act.wait_ge(astep, 2 * n)
            A(eg[u][:], eg[u][:], ACT.Ln, bias=1.0).then_inc(logged, 1)

        def sigmoid(u, n):
            act.wait_ge(lowered, n)
            A(eg[u][:], eg[u][:], ACT.Exp).then_inc(sigmoided, 1)

        def copy_inner(u, n):
            act.wait_ge(i_turned, n)
            A(hmT[u][:], PS[u][:, 3, :], ACT.Copy).then_inc(i_copied, 1)

        def copy_y(u, n, stored):
            act.wait_ge(downed, n)
            act.wait_ge(y_stored[u], stored)
            A(y[u][:], PS[u][:, 0, 256:512], ACT.Copy).then_inc(y_copied, 1)

        log_part(0, 1)
        sigmoid(0, 1)
        with act.Fori(0, TILES // 2 - 1) as i:
            for u in UU:
                log_part(1 - u, 2 * i + u + 2)
                copy_inner(u, 2 * i + u + 1)
                sigmoid(1 - u, 2 * i + u + 2)
                copy_y(u, 2 * i + u + 1, i * 16 + 16)
        log_part(1, TILES)
        copy_inner(0, TILES - 1)
        sigmoid(1, TILES)
        copy_y(0, TILES - 1, (TILES // 2) * 16)
        copy_inner(1, TILES)
        copy_y(1, TILES, (TILES // 2) * 16)

    @block.gpsimd
    def _(pool):
        G = nc.gpsimd
        for u in UU:
            pool.sem_inc(y_stored[u], 16)
            pool.sem_inc(y_copied, 1)
        pool.wait_ge(placed, 1)
        pool.wait_ge(x_back, GROUPS * 16)
        for k in (0, 1):
            for g in range(GROUPS):
                n = rows_of(g)
                G.indirect_dma_start(xs_d, bass.IndirectOffsetOnAxis(posu[:n, k * GROUPS + g:k * GROUPS + g + 1], 0),
                                     rows[:n, g * E:(g + 1) * E], None).then_inc(scattered, 16)
        for u in UU:
            pool.wait_ge(y_stored[u], (TILES // 2 + 1) * 16)
        for g in range(GROUPS):
            n = rows_of(g)
            for k in (0, 1):
                at = (2 * g + k) * E
                G.indirect_dma_start(rows[:n, at:at + E], None, y_d,
                                     bass.IndirectOffsetOnAxis(posu[:n, k * GROUPS + g:k * GROUPS + g + 1], 0)).then_inc(fetched[g], 16)

    @block.vector
    def _(dve):
        V = nc.vector
        TT, TS, STT = V.tensor_tensor, V.tensor_scalar, V.scalar_tensor_tensor
        n_steps = [0]

        def link(ins):
            ins.then_inc(dstep, 1)
            n_steps[0] += 1
            dve.wait_ge(dstep, n_steps[0])

        T = slice(0, TOK)
        g_of, e_of = [1, GROUPS], [GROUPS, NE1]
        link(TT(psum_[T, :], view(picked[T], 2, [4, GROUPS]), view(picked[T], 3, [4, GROUPS]), ALU.add))
        link(TS(psum_[T, :], psum_[T, :], 1e-20, None, ALU.add))
        link(V.reciprocal(psum_[T, :], psum_[T, :]))
        for k in (0, 1):
            link(TT(wgt[k][T, :], view(picked[T], 2 + k, [4, GROUPS]), psum_[T, :], ALU.mult))
            link(TT(view(oh[k][T], 0, e_of, g_of), view(C["eight"][T], 0, [1, NE1], [0, GROUPS]),
                    view(picked[T], k, [0, NE1], [4, GROUPS]), ALU.is_equal))
            link(TT(view(oh[k][T], 0, e_of, g_of), view(oh[k][T], 0, e_of, g_of), view(C["valid"][T], 0, [0, NE1], g_of), ALU.mult))
        TT(both[T, :], oh[0][T, :], oh[1][T, :], ALU.add).then_inc(rout, 1)
        dve.wait_ge(counts, 1)
        link(V.tensor_copy(tot[T, :], PS[0][T, 0, GE:2 * GE]))
        link(V.tensor_tensor_scan(incl[T, :], C["step_g"][T, :], tot[T, :], 0.0, ALU.mult, ALU.add))
        link(TT(view(over[T], 0, [FULL, NE1], [1, FULL]), view(incl[T], GROUPS - 1, [GROUPS, NE1], [0, FULL]),
                view(C["fills"][T], 0, [0, NE1], [1, FULL]), ALU.is_gt))
        link(V.tensor_reduce(nt[T, :], view(over[T], 0, [FULL, NE1], [1, FULL]), AX.X, ALU.add))
        link(V.tensor_tensor_scan(tend[T, :], C["step_e"][T, :], nt[T, :], 0.0, ALU.mult, ALU.add))
        link(TT(t128[T, :], tend[T, :], nt[T, :], ALU.subtract))
        link(TS(t128[T, :], t128[T, :], 128.0, -1.0, ALU.mult, ALU.add))
        link(TT(pos[T, :], incl[T, :], tot[T, :], ALU.subtract))
        link(TT(pos[T, :], pos[T, :], PS[0][T, 0, 0:GE], ALU.add))
        link(TT(view(pos[T], 0, e_of, g_of), view(pos[T], 0, e_of, g_of), view(t128[T], 0, [1, NE1], [0, GROUPS]), ALU.add))
        for k in (0, 1):
            link(TT(cum[T, :], pos[T, :], oh[k][T, :], ALU.mult))
            link(V.tensor_reduce(posf[T, k * GROUPS:(k + 1) * GROUPS], view(cum[T], 0, g_of, e_of), AX.X, ALU.add))
        V.tensor_copy(posu[T, :], posf[T, :]).then_inc(placed, 1)
        link(TT(view(past[T], 0, [NE1, TILES], [1, NE1]), view(C["tile_no"][T], 0, [1, TILES], [0, NE1]),
                view(tend[T], 0, [0, TILES], [1, NE1]), ALU.is_ge))
        link(V.tensor_reduce(tef[T, :], view(past[T], 0, [NE1, TILES], [1, NE1]), AX.X, ALU.add))
        link(TS(tef[T, :], tef[T, :], float(NE1 - 1), float(EW), ALU.min, ALU.mult))
        V.tensor_copy(teu[T, :], tef[T, :]).then_inc(tile_exp, 1)

        own = n_steps[0]

        def copy_rows(u, n):
            dve.wait_ge(r_turned, n)
            V.tensor_copy(xsT[u][:], PS[u][:, 0, 0:256]).then_inc(r_copied, 1)

        def lower(u, n):
            dve.wait_ge(logged, n)
            STT(eg[u][:], PS[u][:, 1, :], 0.0, eg[u][:], ALU.min, ALU.subtract).then_inc(lowered, 1)

        def products(u, n):
            dve.wait_ge(sigmoided, n)
            TT(eg[u][:], eg[u][:], PS[u][:, 1, :], ALU.mult).then_inc(dstep, 1)
            dve.wait_ge(upped, n)
            dve.wait_ge(dstep, n + own)
            TT(hm[u][:], eg[u][:], PS[u][:, 2, :], ALU.mult).then_inc(inner, 1)

        copy_rows(0, 1)
        copy_rows(1, 2)
        lower(0, 1)
        products(0, 1)
        with dve.Fori(0, TILES // 2 - 1) as i:
            for u in UU:
                lower(1 - u, 2 * i + u + 2)
                copy_rows(u, 2 * i + u + 3)
                products(1 - u, 2 * i + u + 2)
        lower(1, TILES)
        products(1, TILES)
        n_steps[0] += TILES
        for g in range(GROUPS):
            n = rows_of(g)
            dve.wait_ge(fetched[g], 32)
            link(STT(h_all[:n, g, :], rows[:n, 2 * g * E:(2 * g + 1) * E], wgt[0][:n, g:g + 1], h_all[:n, g, :], ALU.mult, ALU.add))
            STT(h_all[:n, g, :], rows[:n, (2 * g + 1) * E:(2 * g + 2) * E], wgt[1][:n, g:g + 1], h_all[:n, g, :], ALU.mult, ALU.add).then_inc(summed, 1)


def _pack_arrays(inp, np):
    f = np.float32

    def rows(w):
        k, n = w.shape
        return w.reshape(k // 128, 128, n).transpose(1, 0, 2).reshape(128, -1)

    def row(v, n=128):
        return np.broadcast_to(v.reshape(1, -1), (n, v.size))

    def col(v):
        return v.reshape(-1, 128).T

    tok = np.arange(TOK)
    seq, pos = tok // S, tok % S
    a = {}
    a["w_tok"] = rows(inp["L0_tok_W"])
    a["cls"] = inp["cls_tok"].reshape(1, E)
    a["is_cls"] = (pos == 0).astype(f)[None]
    w = inp["L0_attn_W_qkv"].reshape(H0, 3, D0, E)
    bq = inp["L0_attn_b_qkv"].reshape(H0, 3, D0)
    q, k, v = (w[:, j].reshape(E, E).T for j in range(3))
    a["wqk0"], a["wv0"] = rows(np.concatenate([q, k], 1)), rows(v)
    a["bqk0"] = np.concatenate([col(bq[:, 0].reshape(-1)), col(bq[:, 1].reshape(-1))], 1)
    a["bv0"] = row(bq[:, 2].reshape(-1))
    a["wo0"], a["bo0"] = rows(inp["L0_attn_W_out"].T), row(inp["L0_attn_b_out"])
    a["headmask"] = (np.arange(128)[:, None] // D0 == np.arange(8)[None]).astype(f)
    w, bb = inp["L0_ffn_in_proj_w"], inp["L0_ffn_in_proj_b"]
    a["wqk1"], a["wv1"] = rows(w[:2 * E].T), rows(w[2 * E:].T)
    a["bqk1"], a["bv1"] = col(bb[:2 * E]), row(bb[2 * E:])
    a["wo1"], a["bo1"] = rows(inp["L0_ffn_out_proj_w"].T), row(inp["L0_ffn_out_proj_b"])
    inv = (1.0 / 10000.0 ** (np.arange(0, D0, 2, dtype=f) / f(D0))).astype(f)
    ang = pos.astype(f)[:, None] * inv[None]
    a["rope_cos"] = np.tile(np.repeat(np.cos(ang), 2, axis=1), (1, H0))
    a["rope_sin"] = np.tile(np.sin(ang), (1, H0))
    a["w_gate0"], a["b_gate0"] = rows(inp["L0_ffn_gate_w"].T), row(inp["L0_ffn_gate_b"])
    a["w_exp0"] = rows(inp["L0_ffn_expert_w"].transpose(2, 0, 1).reshape(E, NE0 * E))
    a["b_exp0"] = inp["L0_ffn_expert_b"]
    for n in ("ln1_w", "ln1_b", "ln2_w", "ln2_b"):
        a[n] = row(inp[f"L0_ffn_{n}"])
    a["w_gate1"], a["w_g"] = rows(inp["L1_attn_w_gate"]), rows(inp["L1_attn_w_g"])
    a["wq"], a["wks"], a["wvs"] = rows(inp["L1_attn_w_q"]), rows(inp["L1_attn_w_ks"]), rows(inp["L1_attn_w_vs"])
    a["wgk1s"], a["wgk2s"] = rows(inp["L1_attn_w_gk1s"]), inp["L1_attn_w_gk2s"]
    a["wk"] = rows(inp["L1_attn_w_k"].transpose(1, 0, 2).reshape(E, -1))
    a["wv"] = rows(inp["L1_attn_w_v"].transpose(1, 0, 2).reshape(E, -1))
    a["wgk1"] = rows(inp["L1_attn_w_gk1"].transpose(1, 0, 2).reshape(E, -1))
    a["wgk2"] = inp["L1_attn_w_gk2"].transpose(1, 0, 2).reshape(LOW, -1)
    a["bgk"] = np.concatenate([inp["L1_attn_b_gk"].T, inp["L1_attn_b_gks"][:, None]], 1)
    a["w_o"], a["norm_w"] = rows(inp["L1_attn_w_o"]), row(np.tile(inp["L1_attn_norm_w"], H1))
    same = seq[:, None] == seq[None]
    a["same"] = same.astype(f)
    a["upto"] = (same & (pos[:, None] <= pos[None])).astype(f)
    a["seq9"] = (seq * CAP).astype(f)[:, None]
    a["iota64"] = row(np.arange(1, SLOT + 1, dtype=f))
    slot = np.arange(SLOT)
    a["keep"] = row(np.concatenate([np.tile((slot % CAP != 0) & (slot < SEQS * CAP), MEM), pos != 0]).astype(f))
    a["hsel"] = (np.arange(128)[:, None] // DK == np.arange(H1)[None]).astype(f)
    a["bmask9"] = ((np.arange(128) % SLOT)[:, None] // CAP == np.arange(SEQS)[None]).astype(f)
    a["bmask17"] = (seq[:, None] == np.arange(SEQS)[None]).astype(f)
    a["w_r"], a["sg"], a["su"], a["sd"] = (rows(inp[f"L1_ffn_{n}"]) for n in ("Wr", "Sg", "Su", "Sd"))
    a["turner"] = np.eye(128, dtype=f)
    a["tri"] = (tok[:, None] <= tok[None]).astype(f)
    a["ones"] = np.ones((TOK, TOK), f)
    a["eight"] = row(np.arange(NE1, dtype=f))
    a["valid"] = (np.arange(GROUPS)[None] * TOK + tok[:, None] < B * S).astype(f)
    a["step_g"] = row(np.tile(np.arange(GROUPS) != 0, NE1).astype(f))
    a["step_e"] = row(np.ones(NE1, f))
    a["fills"] = row(np.arange(FULL, dtype=f) * 128)
    a["tile_no"] = row(np.arange(TILES, dtype=f))
    out = {}
    for k, parts in PACKS.items():
        p = np.zeros((128, WIDTH[k]), f)
        at = 0
        for name, wd in parts:
            assert a[name].shape[1] == wd, (name, a[name].shape, wd)
            p[:a[name].shape[0], at:at + wd] = a[name]
            at += wd
        out[k] = p
    return out


def kernel(**inputs):
    import ml_dtypes
    import numpy as np
    import concourse.bacc as bacc
    from concourse.bass_utils import run_bass_kernel_spmd as run

    inp = {k: np.asarray(v) for k, v in inputs.items()}
    packs = _pack_arrays(inp, np)
    x = inp["x"].reshape(B, 4, 16, 4, 16, 3).transpose(0, 1, 3, 2, 4, 5).reshape(B, PATCHES, FEAT)
    xt = np.zeros((GROUPS * SEQS, S, FEAT), x.dtype)
    xt[:B, 1:] = x
    xt = xt.reshape(GROUPS, TOK, FC, 128).transpose(0, 3, 2, 1).reshape(GROUPS, 128, FC * TOK)
    tok = np.arange(TOK)
    same = tok[:, None] // S == tok[None] // S
    masks = np.zeros((128, 2 * TOK + 128), np.float32)
    masks[:TOK, 0:TOK] = np.where(same, 0.0, FAR)
    masks[:TOK, TOK:2 * TOK] = np.where(same & (tok[None] <= tok[:, None]), 0.0, FAR)
    masks[:, 2 * TOK:] = np.eye(128)
    masks = masks.astype(ml_dtypes.bfloat16)

    ew = np.zeros((128, NE1, EW), np.float32)
    for n, name in enumerate(("L1_ffn_Wg", "L1_ffn_Wu")):
        ew[:, :, n * KC * FF:(n + 1) * KC * FF] = inp[name].reshape(NE1, KC, 128, FF).transpose(2, 0, 1, 3).reshape(128, NE1, KC * FF)
    ew[:, :, 2 * KC * FF:] = inp["L1_ffn_Wd"].reshape(NE1, 4, 128, E).transpose(2, 0, 1, 3).reshape(128, NE1, 4 * E)

    nc = bacc.Bacc("TRN2", target_bir_lowering=False, num_devices=1)
    arrays = {"in_patches": np.ascontiguousarray(xt), "in_masks": masks, "in_experts": ew.reshape(128, NE1 * EW), **{f"in_{k}": v for k, v in packs.items()}}
    aps = {k: nc.dram_tensor(k, a.shape, mybir.dt.from_np(a.dtype), kind="ExternalInput").ap() for k, a in arrays.items()}
    out = nc.dram_tensor("out_0_dram", (B * S, E), F32, kind="ExternalOutput").ap()
    x_d = nc.dram_tensor("expert_in", (GROUPS * TOK, E), F32, kind="Internal").ap()
    xs_d = nc.dram_tensor("expert_rows", (TILES * 128, E), F32, kind="Internal").ap()
    y_d = nc.dram_tensor("expert_out", (TILES * 128, E), F32, kind="Internal").ap()
    tower_kernel(nc, aps["in_patches"], {k: aps[f"in_{k}"] for k in PACKS}, aps["in_masks"], aps["in_experts"], x_d, xs_d, y_d, out)
    r = run(nc, [arrays], core_ids=[0])
    return r.results[0]["out_0_dram"].reshape(B, S, E)
```

```python
from contextlib import ExitStack

import concourse.bass as bass
from concourse import mybir

F32 = mybir.dt.float32
BF16 = mybir.dt.bfloat16
U32 = mybir.dt.uint32
ALU = mybir.AluOpType
ACT = mybir.ActivationFunctionType
AX = mybir.AxisListType

B, PATCHES, S = 64, 16, 17
E = 256
KC = E // 128
FEAT = 768
FC = FEAT // 128
SEQS = 7
TOK = SEQS * S
GROUPS = -(-B // SEQS)
PAIRS = GROUPS // 2
LAST_TOK = (B - (GROUPS - 1) * SEQS) * S
H0, D0 = 16, 16
NE0 = 8
H1, DK, DV = 4, 32, 64
MEM, CAP, LOW = 4, 9, 16
SLOT = 64
PAIRM = MEM // 2
NE1, FF = 8, 512
EPS = 1e-5
FAR = -1e30
GATE_NORM = 16.0
QSCALE1 = float(DK) ** -0.5
DM = MEM * CAP * SLOT
DALL = DM + S * TOK
M_PARTS = [range(3 * p, 3 * p + 3) for p in range(CAP // 3)]
S_PARTS = [range(0, 9), range(9, S)]
MP, SP = len(M_PARTS), len(S_PARTS)
FILL_V, FILL_A = 96, 96

TILES = (2 * B * S + NE1 * 127) // 128
FULL = -(-B * S // 128)
EW = 2 * KC * FF + (FF // 128) * E
PACKS = {
    "tok": [("w_tok", FC * E), ("cls", E), ("is_cls", TOK)],
    "l0": [("wqk0", KC * 2 * E), ("wv0", KC * E), ("wo0", KC * E), ("bqk0", 4), ("bv0", E), ("bo0", E),
           ("headmask", 8),
           ("wqk1", KC * 2 * E), ("wv1", KC * E), ("wo1", KC * E), ("bqk1", 4), ("bv1", E), ("bo1", E),
           ("rope_cos", E), ("rope_sin", 128)],
    "l0f": [("w_gate0", KC * NE0), ("b_gate0", NE0), ("w_exp0", KC * NE0 * E), ("b_exp0", E),
            ("ln1_w", E), ("ln1_b", E), ("ln2_w", E), ("ln2_b", E)],
    "l1": [("w_gate1", KC * MEM), ("w_g", KC * E), ("wq", KC * 128), ("wks", KC * 128), ("wvs", KC * E),
           ("wgk1s", KC * LOW), ("wgk2s", 128), ("wk", KC * MEM * 128), ("wv", KC * MEM * E),
           ("wgk1", KC * MEM * LOW), ("wgk2", MEM * 128), ("bgk", MEM + 1), ("w_o", KC * E),
           ("norm_w", E), ("upto", TOK), ("same", TOK), ("seq9", 1), ("iota64", SLOT), ("keep", MEM * SLOT + TOK),
           ("hsel", FILL_A), ("bmask9", SEQS), ("bmask17", SEQS),
           ("w_r", KC * NE1)],
}
PACKS["route"] = [("turner", 128), ("tri", TOK), ("ones", TOK), ("eight", NE1), ("valid", GROUPS), ("step_g", NE1 * GROUPS), ("step_e", NE1),
                  ("fills", FULL), ("tile_no", TILES)]
WIDTH = {k: sum(w for _, w in v) for k, v in PACKS.items()}
SLOTS = 1 + NE1
ARENA = {"l0": WIDTH["l0"], "l0f": WIDTH["l0f"], "tok": WIDTH["tok"], "patches": 2 * FC * TOK, "area0": DALL,
         "l1": WIDTH["l1"]}
EARLY = sum(w for k, w in ARENA.items() if k != "l1") // EW
SHARED = B * S // 128 + (B * S % 128 > 0)
FIRST = 5
UNROLL = 4
assert TILES % UNROLL == 0


def view(ap, off, *dims):
    return bass.AP(ap.tensor, ap.offset + off, [list(ap.ap[0])] + [list(d) for d in dims])


FRONT_AT = (-1, 6.4, 17, 31.3, 41.2, 51.2, 56.2, 66.2, 79.7)


class Steps:

    def __init__(self, eng, sem):
        self.eng, self.sem, self.n = eng, sem, 0

    def mark(self, ins):
        ins.then_inc(self.sem, 1)
        self.n += 1

    def wait(self):
        self.eng.wait_ge(self.sem, self.n)

    def end(self):
        self.wait()
        self.eng.sem_clear(self.sem)


def weave(*halves):
    due = [[next(h, None), n, h] for n, h in enumerate(halves)]
    due = [d for d in due if d[0] is not None]
    while due:
        due.sort(key=lambda d: d[:2])
        at = next(due[0][2], None)
        if at is None:
            due.pop(0)
        else:
            due[0][0] = at


def in_turn(*parts):
    for p in parts:
        yield from p


def placed(half):
    for at in half:
        n = min(max(int(at // 10), 0), len(FRONT_AT) - 2)
        yield FRONT_AT[n] + (at - 10 * n) * (FRONT_AT[n + 1] - FRONT_AT[n]) / 10


def all_groups(eng, begin, front, back):
    weave(in_turn(begin(0, 0)))
    weave(placed(front(0, 0)), in_turn(begin(1, 0)))
    with eng.Fori(0, PAIRS - 1) as i:
        weave(in_turn(back(0, i), begin(0, i + 1)), placed(front(1, i)))
        weave(in_turn(back(1, i), begin(1, i + 1)), placed(front(0, i + 1)))
    weave(back(0, PAIRS - 1), placed(front(1, PAIRS - 1)))
    weave(back(1, PAIRS - 1))


def tower_kernel(nc, xp_d, packs_d, masks_d, experts_d, x_d, xs_d, y_d, ysh_d, out_d):
    with ExitStack() as ctx, ExitStack() as phase1:
        def keep(name, shape, dt=F32):
            return ctx.enter_context(nc.sbuf_tensor(name, shape, dt))

        def sb(name, shape, dt=F32):
            return phase1.enter_context(nc.sbuf_tensor(name, shape, dt))

        def sem(name):
            return ctx.enter_context(nc.semaphore(name))

        PS = [ctx.enter_context(nc.psum_tensor(f"ps{u}", [128, 4, 512], F32)) for u in (0, 1)]
        pack = {"route": keep("pack_route", [128, WIDTH["route"]])}
        h_all = keep("h_all", [128, GROUPS, E])
        picked = keep("picked", [128, GROUPS * 4])
        arena = keep("arena", [128, SLOTS * EW])
        used = 0
        for k, w in ARENA.items():
            pack[k] = arena[:, used:used + w]
            used += w
        xp = [pack["patches"][:, u * FC * TOK:(u + 1) * FC * TOK] for u in (0, 1)]
        C = {}
        for k, parts in PACKS.items():
            at = 0
            for name, w in parts:
                C[name] = pack[k][:, at:at + w]
                at += w
        masks = sb("masks", [128, 2 * TOK + 128], BF16)
        identb = masks[:, 2 * TOK:]
        zeros = sb("zeros", [128, E])
        Dp = sb("pair_exponents", [128, DALL])
        roots = sb("roots", [128, 4])

        def two(name, shape, dt=F32):
            return [sb(f"{name}{u}", shape, dt) for u in (0, 1)]

        h = two("h", [128, E])
        xn = two("xn", [128, E])
        xa = two("xa", [128, E])
        hb = two("hb", [128, E])
        xT = two("xT", [128, 4 * TOK])
        vS = two("v_ones", [128, H0 * (D0 + 1) + FILL_V])
        cT = two("cT", [128, TOK])
        qS, kS = two("q_shared", [128, TOK]), two("k_shared", [128, TOK])
        vsh = two("v_shared", [128, E])
        gs = two("silu_g", [128, E])
        ohT = two("combineT", [128, PAIRM * TOK])
        qP = two("q_mem", [128, MEM * CAP * SEQS])
        kM = two("k_mem", [128, MEM * SLOT])
        vM = two("v_mem", [128, PAIRM * E])
        Gc = two("decay_sums", [128, MEM * SLOT + TOK])
        AbM = two("a_mem", [128, PAIRM * H1 * 128])
        st, mv, ve, rstd = two("st", [128, 6]), two("mv", [128, 2]), two("ve", [128, 1]), two("rstd", [128, 1])
        lg, d8, pr, pr4, mx8 = (two(n, [128, 8]) for n in ("lg", "d8", "pr", "pr4", "mx8"))
        ix = two("ix", [128, 8], U32)
        ixf = two("ixf", [128, 2])
        mxs, ssum, rsum = two("mxs", [128, 1]), two("ssum", [128, 1]), two("rsum", [128, 1])
        mxh = two("mxh", [128, H0])
        rden = two("rden", [128, H0])
        c0, c1, cw = two("c0", [128, 8]), two("c1", [128, 8]), two("cw", [128, 8])
        p12, rp = two("p12", [128, 1]), two("rp", [128, 1])
        rt, w2, t9, s1, vd, code = (two(n, [128, 4]) for n in ("rt", "w2", "t9", "s1", "vd", "code"))
        ms, mse, rs4 = (two(n, [128, 4]) for n in ("ms", "mse", "rs4"))
        U = [pack["area0"], sb("area", [128, DALL])]
        SC = H0 * TOK
        dA = [U[u][:, 0:SC] for u in (0, 1)]
        kPT = [U[u][:, SC:2 * SC] for u in (0, 1)]
        qT = [U[u][:, 2 * SC:2 * SC + 2 * TOK] for u in (0, 1)]
        kT = [U[u][:, 2 * SC + 2 * TOK:2 * SC + 4 * TOK] for u in (0, 1)]
        o = [U[u][:, 2 * SC:2 * SC + E] for u in (0, 1)]
        rr = [U[u][:, SC:SC + E] for u in (0, 1)]
        rq = [U[u][:, SC + E:SC + 2 * E] for u in (0, 1)]
        acc = [U[u][:, 0:E] for u in (0, 1)]
        NZ = MEM * SLOT + TOK
        xg = [U[u][:, 0:512] for u in (0, 1)]
        z1M = [U[u][:, 512:768] for u in (0, 1)]
        z1S = [U[u][:, 768:768 + TOK] for u in (0, 1)]
        OH = [U[u][:, 1024:1280] for u in (0, 1)]
        OHw = [U[u][:, 1280:1536] for u in (0, 1)]
        zz = [U[u][:, 1536:1536 + NZ] for u in (0, 1)]
        az = [U[u][:, 1536 + NZ:1536 + 2 * NZ] for u in (0, 1)]
        lgz = [U[u][:, 1536 + 2 * NZ:1536 + 3 * NZ] for u in (0, 1)]
        egs = [U[u][:, 3000:3256] for u in (0, 1)]
        AbS = [U[u][:, 0:H1 * TOK] for u in (0, 1)]
        oM = [U[u][:, 512:1024] for u in (0, 1)]
        oS = [U[u][:, 1024:1280] for u in (0, 1)]
        sq = [U[u][:, 1280:1536] for u in (0, 1)]

        x_landed = [sem(f"x_landed{u}") for u in (0, 1)]
        tok_used = [sem(f"tok_used{u}") for u in (0, 1)]
        landed = {k: sem(f"landed_{k}") for k in [*PACKS, "masks"]}
        out_stored = sem("out_stored")
        x_stored = [sem(f"x_stored{u}") for u in (0, 1)]
        cleared = sem("rows_cleared")
        w_landed, shared_landed = sem("expert_weights_landed"), sem("shared_weights_landed")
        pool_ready = sem("pool_ready")
        own_f = {e: sem(f"{e}_front_step") for e in ("dve", "pool")}
        own_b = {e: sem(f"{e}_back_step") for e in ("dve", "pool", "act")}
        stats, rstd_ready, norm = (
            {"a": sem(f"{n}_begin"), "f": sem(f"{n}_front"), "b": sem(f"{n}_back")} for n in (
                "stats", "rstd_ready", "norm"))
        turned, turn_copied = ({"a": sem(f"{n}_begin"), "f": sem(f"{n}_front"), "b": sem(f"{n}_back")} for n in (
            "turned", "turn_copied"))
        projected, gate, logits, softmaxed = ({"f": sem(f"{n}_front"), "b": sem(f"{n}_back")} for n in (
            "projected", "gate", "logits", "softmaxed"))
        qkv, qk_copied, km_pool, km_dve, v_copied = ([sem(f"{n}_{k}") for k in (0, 1)] for n in (
            "qkv", "qk_copied", "km_pool", "km_dve", "v_copied"))
        (scores, maxed, exped, p_turned, pt_act, pt_dve, av, attended,
         res_ready, roped, experts, exp_read, c_ready, c_turned, c_copied, bias_ready) = (sem(n) for n in (
            "scores", "maxed", "exped", "p_turned", "pt_act",
            "pt_dve", "av", "attended", "res_ready", "roped", "experts", "exp_read", "c_ready", "c_turned",
            "c_copied", "bias_ready"))
        (g_prod, sh_prod, vs_prod, sh_copied, routed, counted, onehot, weighted, gathered, xg_copied, oh_turned,
         oh_copied, z1_prod, z1_copied, qm_prod, qm_copied, vm_prod, z2_prod, zabs, lned, sig_in, sig_out,
         summed_up, exponents, sh_exponents, dexped_m, mem_prod, sh_pairs, a_prod, a_spread, om_prod, om_copied, o_prod, gated,
         rms_ms, rms_ready, gs_ready, gs_scaled, g_copied) = (sem(n) for n in (
            "g_prod", "sh_prod", "vs_prod", "sh_copied", "routed", "counted", "onehot", "weighted", "gathered",
            "xg_copied", "oh_turned", "oh_copied", "z1_prod", "z1_copied", "qm_prod", "qm_copied", "vm_prod",
            "z2_prod", "zabs", "lned", "sig_in", "sig_out", "summed_up", "exponents", "sh_exponents", "dexped_m", "mem_prod", "sh_pairs",
            "a_prod", "a_spread", "om_prod", "om_copied", "o_prod", "gated", "rms_ms", "rms_ready", "gs_ready", "gs_scaled", "g_copied"))
        dexped = [sem(f"dexped{u}") for u in (0, 1)]

        def tokens(u, i):
            return LAST_TOK if isinstance(i, int) and (u, i) == (1, PAIRS - 1) else TOK

        def nth(i, k, per_half, u):
            return i * (2 * per_half) + (u * per_half + k + 1)

        LNF, LNB, TF, TC, TB = 2, 2, 5, 5, 3
        ROOTS = 4
        UU = (0, 1)
        block_ctx = ExitStack()
        block = block_ctx.enter_context(nc.Block())

        @block.sync
        def _(sp):
            sp.dma_start(pack["route"][:], packs_d["route"]).then_inc(landed["route"], 16)
            sp.dma_start(pack["tok"], packs_d["tok"]).then_inc(landed["tok"], 16)
            for u in UU:
                sp.dma_start(xp[u], xp_d[u]).then_inc(x_landed[u], 16)
            sp.dma_start(masks[:], masks_d).then_inc(landed["masks"], 16)
            for k in ("l0", "l0f", "l1"):
                sp.dma_start(pack[k], packs_d[k]).then_inc(landed[k], 16)
            sp.wait_ge(pool_ready, 1)
            for j in range(TILES):
                sp.dma_start(xs_d[j * 128:(j + 1) * 128, :], zeros[:]).then_inc(cleared, 16)

            def store_inputs(i, u):
                sp.wait_ge(norm["b"], nth(i, 1, LNB, u))
                sp.dma_start(x_d[bass.ds((2 * i + u) * TOK, TOK), :], xn[u][:TOK, :]).then_inc(x_stored[u], 16)

            with sp.Fori(0, PAIRS - 1) as i:
                for u in UU:
                    sp.wait_ge(tok_used[u], i + 1)
                    sp.dma_start(xp[u], xp_d[bass.ds(2 * i + 2 + u, 1)].rearrange("o p f -> (o p) f")).then_inc(x_landed[u], 16)
                for u in UU:
                    store_inputs(i, u)
            store_inputs(PAIRS - 1, 0)
            sp.wait_ge(norm["b"], nth(PAIRS - 1, 0, LNB, 1))
            for e in range(EARLY):
                sp.dma_start(arena[:, e * EW:(e + 1) * EW], experts_d[:, e * EW:(e + 1) * EW]).then_inc(w_landed if e else shared_landed, 16)
            store_inputs(PAIRS - 1, 1)
            for u in UU:
                sp.wait_ge(x_stored[u], (PAIRS + 1) * 16)
            sp.wait_ge(cleared, TILES * 16)

        @block.tensor
        def _(pe):
            mm, tp = nc.tensor.matmul, nc.tensor.transpose
            pe.wait_ge(landed["route"], 16)
            pe.wait_ge(landed["tok"], 16)

            def turn(u, tk, half, blocks, bank=3):
                for c, s in enumerate(blocks):
                    last = tp(PS[u][:, bank, c * TOK:c * TOK + tk], s, C["turner"][:tk, :tk])
                last.then_inc(turned[half], 1)

            def chunks(x, tk, n=KC):
                return [x[:tk, c * 128:(c + 1) * 128] for c in range(n)]

            def rows_product(u, tk, bank, w, n, lo=0):
                for c in range(KC):
                    last = mm(PS[u][:tk, bank, lo:lo + n], xT[u][:, c * TOK:c * TOK + tk],
                              w[:, c * n:(c + 1) * n], start=(c == 0), stop=(c == KC - 1))
                return last

            def v_product(u, tk, k):
                rows_product(u, tk, 2, C[f"wv{k}"], E).then_inc(qkv[k], 1)

            def qk_products(u, tk, k):
                for j in (2, 3, 0, 1):
                    for c in range(KC):
                        w = C[f"wqk{k}"][:, c * 2 * E + j * 128:c * 2 * E + (j + 1) * 128]
                        last = mm(PS[u][:, j // 2, (j % 2) * TOK:(j % 2) * TOK + tk], w,
                                  xT[u][:, (2 * k + c) * TOK:(2 * k + c) * TOK + tk], start=(c == 0), stop=(c == KC - 1))
                    if j % 2:
                        last.then_inc(qkv[k], 1)

            def begin(u, i):
                yield 62
                pe.wait_ge(x_landed[u], i * 16 + 16)
                mm(PS[u][:TOK, 2, 0:E], C["is_cls"][0:1, :], C["cls"][0:1, :], start=True, stop=False)
                for c in range(FC):
                    last = mm(PS[u][:TOK, 2, 0:E], xp[u][:, c * TOK:(c + 1) * TOK], C["w_tok"][:, c * E:(c + 1) * E],
                              start=False, stop=(c == FC - 1))
                last.then_inc(tok_used[u], 1)
                yield 71
                pe.wait_ge(norm["a"], nth(i, 0, 1, u))
                turn(u, TOK, "a", chunks(xn[u], TOK))
                yield 69.5
                pe.wait_ge(turn_copied["a"], nth(i, 0, 1, u))
                yield 69.5
                pe.wait_ge(landed["l0"], 16)
                qk_products(u, TOK, 0)
                yield 72
                v_product(u, TOK, 0)

            def front(u, i):
                tk = tokens(u, i)
                for k in (0, 1):
                    z = 35 * k - 7
                    if k == 1:
                        yield 24.5
                        pe.wait_ge(norm["f"], nth(i, 0, LNF, u))
                        turn(u, tk, "f", chunks(xa[u], tk))
                        yield 26
                        pe.wait_ge(roped, nth(i, 0, 1, u))
                        turn(u, tk, "f", chunks(rr[u], tk), bank=0)
                        yield 25
                        pe.wait_ge(turn_copied["f"], nth(i, 1, TC, u))
                        v_product(u, tk, 1)
                        yield 28.5
                        pe.wait_ge(turn_copied["f"], nth(i, 2, TC, u))
                        qk_products(u, tk, 1)
                    for hf in (0, 1):
                        for b in (2 * hf, 2 * hf + 1):
                            yield 7 + z + b
                            if b == 0:
                                pe.wait_ge(landed["masks"], 16)
                                pe.wait_ge(qk_copied[k], nth(i, 2, 3, u))
                                pe.wait_ge(km_dve[k], nth(i, 0, 1, u))
                            if b == 2:
                                pe.wait_ge(km_pool[k], nth(i, 0, 1, u))
                                pe.wait_ge(v_copied[k], nth(i, 0, 1, u))
                            mm(view(PS[u][:tk, b, :], 0, [TOK, 4], [1, tk]), identb[:tk, :tk],
                               view(masks[:tk], k * TOK, [0, 4], [1, tk]), start=True, stop=False)
                            mm(view(PS[u][:tk, b, :], 0, [TOK, 4], [1, tk]), qT[u][:, (b // 2) * TOK:(b // 2) * TOK + tk],
                               view(kPT[u], b * 4 * TOK, [TOK, 4], [1, tk]), start=False, stop=True).then_inc(scores, 1)
                    for hf in (0, 1):
                        yield 14 + z + 2.5 * hf
                        for hd in range(8 * hf, 8 * hf + 8):
                            if hd % 4 == 0:
                                pe.wait_ge(exped, nth(i, 4 * k + hd // 4, 8, u))
                            last = tp(PS[u][:tk, hd // 4, (hd % 4) * TOK:(hd % 4) * TOK + tk],
                                      dA[u][:tk, hd * TOK:hd * TOK + tk], C["turner"][:tk, :tk])
                        last.then_inc(p_turned, 1)
                    W = D0 + 1
                    for hd in range(H0):
                        if hd % 4 == 0:
                            yield 17.5 + z + 0.4 * hd
                        if hd == 0:
                            pe.wait_ge(pt_act, nth(i, k, 2, u))
                        if hd == 8:
                            pe.wait_ge(pt_dve, nth(i, k, 2, u))
                        last = mm(PS[u][:tk, 0, hd * W:hd * W + FILL_V], kPT[u][:tk, hd * TOK:hd * TOK + tk],
                                  vS[u][:tk, hd * W:hd * W + FILL_V], start=True, stop=True)
                    last.then_inc(av, 1)
                    yield 25.5 + z
                    pe.wait_ge(attended, nth(i, k, 2, u))
                    turn(u, tk, "f", chunks(o[u], tk))
                    yield 26.5 + z
                    pe.wait_ge(turn_copied["f"], nth(i, 3 * k, TC, u))
                    rows_product(u, tk, 1, C[f"wo{k}"], E).then_inc(projected["f"], 1)

                yield 61
                pe.wait_ge(norm["f"], nth(i, 1, LNF, u))
                turn(u, tk, "f", chunks(xa[u], tk))
                yield 59.5
                pe.wait_ge(landed["l0f"], 16)
                pe.wait_ge(turn_copied["f"], nth(i, 4, TC, u))
                rows_product(u, tk, 0, C["w_gate0"], NE0).then_inc(gate["f"], 1)
                for j in range(4):
                    yield (59.6, 61.5, 63.5, 69)[j]
                    if j == 3:
                        pe.wait_ge(exp_read, nth(i, 0, 4, u))
                    for c in range(KC):
                        last = mm(PS[u][:tk, 1 + j % 3, :], xT[u][:, c * TOK:c * TOK + tk],
                                  C["w_exp0"][:, c * NE0 * E + j * 512:c * NE0 * E + (j + 1) * 512],
                                  start=(c == 0), stop=(c == KC - 1))
                    last.then_inc(experts, 1)
                    if j == 2:
                        yield 65
                        pe.wait_ge(c_ready, nth(i, 0, 1, u))
                        tp(PS[u][:NE0, 0, 128:128 + tk], cw[u][:tk, :], C["turner"][:tk, :tk]).then_inc(c_turned, 1)
                        yield 66
                        pe.wait_ge(c_copied, nth(i, 0, 1, u))
                        mm(PS[u][:tk, 0, 256:512], cT[u][:NE0, :tk], C["b_exp0"][:NE0, :], start=True, stop=True).then_inc(bias_ready, 1)

            def back(u, i):
                tk = tokens(u, i)
                yield 0
                pe.wait_ge(norm["b"], nth(i, 0, LNB, u))
                turn(u, tk, "b", chunks(xn[u], tk))
                yield 2.5
                pe.wait_ge(landed["l1"], 16)
                pe.wait_ge(turn_copied["b"], nth(i, 0, TB, u))
                x0 = [xT[u][:, c * TOK:(c + 1) * TOK] for c in range(KC)]
                rows_product(u, tk, 0, C["w_gate1"], MEM).then_inc(gate["b"], 1)
                rows_product(u, tk, 1, C["w_g"], E).then_inc(g_prod, 1)
                yield 2.5
                for n, (w, m) in enumerate((("wq", 128), ("wks", 128), ("wgk1s", LOW))):
                    for c in range(KC):
                        last = mm(PS[u][:m, 2, n * TOK:(n + 1) * TOK], C[w][:, c * m:(c + 1) * m], x0[c], start=(c == 0), stop=(c == KC - 1))
                last.then_inc(sh_prod, 1)
                yield 4
                rows_product(u, tk, 3, C["wvs"], E).then_inc(vs_prod, 1)
                yield 6
                pe.wait_ge(routed, nth(i, 0, 1, u))
                mm(PS[u][:tk, 0, 8:8 + MEM], C["upto"][:tk, :tk], rt[u][:tk, :], start=True, stop=True)
                mm(PS[u][:tk, 0, 12:12 + MEM], C["same"][:tk, :tk], rt[u][:tk, :], start=True, stop=True).then_inc(counted, 1)
                yield 9
                pe.wait_ge(onehot, nth(i, 0, 1, u))
                pe.wait_ge(g_copied, nth(i, 0, 1, u))
                for c in range(KC):
                    last = mm(PS[u][:, 1, c * 256:(c + 1) * 256], xn[u][:tk, c * 128:(c + 1) * 128], OH[u][:tk, :], start=True, stop=True)
                last.then_inc(gathered, 1)
                yield 10.5
                pe.wait_ge(weighted, nth(i, 0, 1, u))
                pe.wait_ge(sh_copied, nth(i, 1, 2, u))
                for c in range(PAIRM):
                    last = tp(PS[u][:, 3, c * TOK:c * TOK + tk], OHw[u][:tk, c * 128:(c + 1) * 128], C["turner"][:tk, :tk])
                last.then_inc(oh_turned, 1)
                yield 11.5
                pe.wait_ge(xg_copied, nth(i, 0, 1, u))
                for m in range(MEM):
                    for c in range(KC):
                        last = mm(PS[u][:LOW, 0, m * SLOT:(m + 1) * SLOT], C["wgk1"][:, (c * MEM + m) * LOW:(c * MEM + m + 1) * LOW],
                                  xg[u][:, c * 256 + m * SLOT:c * 256 + (m + 1) * SLOT], start=(c == 0), stop=(c == KC - 1))
                last.then_inc(z1_prod, 1)
                yield 12.5
                for c in range(KC):
                    mm(PS[u][:, 1, 0:256], C["wq"][:, c * 128:(c + 1) * 128], xg[u][:, c * 256:(c + 1) * 256], start=(c == 0), stop=(c == KC - 1))
                for m in range(MEM):
                    for c in range(KC):
                        last = mm(PS[u][:, 1, 256 + m * SLOT:256 + (m + 1) * SLOT], C["wk"][:, (c * MEM + m) * 128:(c * MEM + m + 1) * 128],
                                  xg[u][:, c * 256 + m * SLOT:c * 256 + (m + 1) * SLOT], start=(c == 0), stop=(c == KC - 1))
                last.then_inc(qm_prod, 1)
                yield 14
                pe.wait_ge(z1_copied, nth(i, 0, 1, u))
                pe.wait_ge(oh_copied, nth(i, 0, 1, u))
                for m in range(MEM):
                    mm(PS[u][:, 3, m * SLOT:(m + 1) * SLOT], C["wgk2"][:LOW, m * 128:(m + 1) * 128], z1M[u][:LOW, m * SLOT:(m + 1) * SLOT], start=True, stop=True)
                mm(PS[u][:, 3, 256:256 + TOK], C["wgk2s"][:LOW, :], z1S[u][:LOW, :], start=True, stop=True).then_inc(z2_prod, 1)
                yield 12
                for m in range(MEM):
                    if m == 2:
                        yield 17
                    for c in range(KC):
                        p = (m % 2) * SLOT
                        last = mm(PS[u][p:p + SLOT, 2, (m // 2) * E:(m // 2 + 1) * E],
                                  xg[u][:, c * 256 + m * SLOT:c * 256 + (m + 1) * SLOT],
                                  C["wv"][:, (c * MEM + m) * E:(c * MEM + m + 1) * E], start=(c == 0), stop=(c == KC - 1),
                                  skip_group_check=True)
                last.then_inc(vm_prod, 1)
                for p, steps in enumerate(M_PARTS):
                    yield (26, 28, 28.5)[p]
                    pe.wait_ge(mem_prod, nth(i, p, MP, u))
                    for t in steps:
                        for mp in range(PAIRM):
                            at = (t * PAIRM + mp) * H1
                            last = mm(PS[u][:, 0, at:at + FILL_A],
                                      U[u][:, t * MEM * SLOT + mp * 128:t * MEM * SLOT + (mp + 1) * 128], C["hsel"], start=True, stop=True)
                last.then_inc(a_prod, 1)
                for p, steps in enumerate(S_PARTS):
                    for t in steps:
                        if t == steps[0] or t % 4 == 0:
                            yield (32, 33)[p] + t * 0.4
                        if t == steps[0]:
                            pe.wait_ge(sh_pairs, nth(i, p, SP, u))
                        last = mm(PS[u][:tk, 3, H1 * t:H1 * t + FILL_A], U[u][:, DM + t * TOK:DM + t * TOK + tk], C["hsel"], start=True, stop=True)
                last.then_inc(a_prod, 1)
                yield 42
                pe.wait_ge(a_spread, nth(i, 0, 2, u))
                pe.wait_ge(qm_copied, nth(i, 1, 2, u))
                for mp in range(PAIRM):
                    for hd in range(H1):
                        last = mm(PS[u][:, 1, mp * E + hd * DV:mp * E + (hd + 1) * DV], AbM[u][:, (mp * H1 + hd) * 128:(mp * H1 + hd + 1) * 128],
                                  vM[u][:, mp * E + hd * DV:mp * E + (hd + 1) * DV], start=True, stop=True)
                last.then_inc(om_prod, 1)
                yield 47
                pe.wait_ge(om_copied, nth(i, 0, 1, u))
                pe.wait_ge(a_spread, nth(i, 1, 2, u))
                for mp in range(PAIRM):
                    mm(PS[u][:tk, 2, 0:E], ohT[u][:, mp * TOK:mp * TOK + tk], oM[u][:, mp * E:(mp + 1) * E],
                       start=(mp == 0), stop=False, skip_group_check=True)
                for hd in range(H1):
                    last = mm(PS[u][:tk, 2, hd * DV:(hd + 1) * DV], AbS[u][:tk, hd * TOK:hd * TOK + tk],
                              vsh[u][:tk, hd * DV:(hd + 1) * DV], start=False, stop=(hd == H1 - 1), skip_group_check=True)
                last.then_inc(o_prod, 1)
                yield 55
                pe.wait_ge(gated, nth(i, 0, 1, u))
                turn(u, tk, "b", chunks(oS[u], tk))
                yield 56
                pe.wait_ge(turn_copied["b"], nth(i, 1, TB, u))
                rows_product(u, tk, 1, C["w_o"], E).then_inc(projected["b"], 1)
                yield 60
                pe.wait_ge(norm["b"], nth(i, 1, LNB, u))
                turn(u, tk, "b", chunks(xn[u], tk))
                yield 61
                pe.wait_ge(turn_copied["b"], nth(i, 2, TB, u))
                rows_product(u, tk, 0, C["w_r"], NE1).then_inc(gate["b"], 1)

            all_groups(pe, begin, front, back)

        @block.scalar
        def _(act):
            A = nc.scalar.activation
            nc.scalar.preload_act_table_set("natural_log_exp_and_others")
            act.wait_ge(landed["l0"], 16)

            def copy_turn(u, half, value, bank=3, to=0):
                act.wait_ge(turned[half], value)
                return A(xT[u][:, to * TOK:(to + 2) * TOK], PS[u][:, bank, 0:2 * TOK], ACT.Copy)

            def softmax_exp(u, tk, half, value, n, dst):
                act.wait_ge(logits[half], value)
                A(dst[u][:tk, 0:n], d8[u][:tk, 0:n], ACT.Exp, accum_out=ssum[u][:tk, :]).then_inc(softmaxed[half], 1)

            def copy_qk(u, tk, i, k, at):
                for half in (0, 1):
                    yield at + 1.5 * half
                    act.wait_ge(qkv[k], nth(i, k + half, 3, u))
                    for n in (0, 1):
                        last = A((kT, qT)[half][u][:, n * TOK:n * TOK + tk], PS[u][:, 1 - half, n * TOK:n * TOK + tk],
                                 ACT.Identity, bias=C[f"bqk{k}"][:, 2 * (1 - half) + n:2 * (1 - half) + n + 1])
                        if half == 0 or n == 1:
                            last.then_inc(qk_copied[k], 1)

            def begin(u, i):
                yield 69
                copy_turn(u, "a", nth(i, 0, 1, u)).then_inc(turn_copied["a"], 1)
                yield from copy_qk(u, TOK, i, 0, 71.5)

            def front(u, i):
                tk = tokens(u, i)
                for k in (0, 1):
                    z = 35 * k - 7
                    if k == 1:
                        yield 25
                        copy_turn(u, "f", nth(i, 1, TF, u)).then_inc(turn_copied["f"], 1)
                        yield 26.5
                        copy_turn(u, "f", nth(i, 2, TF, u), bank=0, to=2).then_inc(turn_copied["f"], 1)
                        yield from copy_qk(u, tk, i, 1, 35.5)
                    for b in range(4):
                        yield 10.5 + z + 1.1 * b
                        act.wait_ge(maxed, nth(i, 4 * k + b, 8, u))
                        for hd in range(4 * b, 4 * b + 4):
                            last = A(dA[u][:tk, hd * TOK:hd * TOK + tk], PS[u][:tk, hd // 4, (hd % 4) * TOK:(hd % 4) * TOK + tk],
                                     ACT.Exp, scale=float(D0) ** -0.5, bias=mxh[u][:tk, hd:hd + 1])
                        last.then_inc(exped, 1)
                    yield 14.5 + z
                    act.wait_ge(p_turned, nth(i, 2 * k, 4, u))
                    turned_heads = [512, 2], [TOK, 4], [1, tk]
                    A(view(kPT[u][:tk], 0, [4 * TOK, 2], [TOK, 4], [1, tk]), view(PS[u][:tk, 0, :], 0, *turned_heads), ACT.Copy).then_inc(pt_act, 1)
                    yield 26 + z
                    copy_turn(u, "f", nth(i, 3 * k, TF, u)).then_inc(turn_copied["f"], 1)
                yield 59
                copy_turn(u, "f", nth(i, 4, TF, u)).then_inc(turn_copied["f"], 1)
                yield 61
                softmax_exp(u, tk, "f", nth(i, 0, 1, u), NE0, pr)
                yield 65.5
                act.wait_ge(c_turned, nth(i, 0, 1, u))
                A(cT[u][:NE0, :], PS[u][:NE0, 0, 128:128 + TOK], ACT.Copy).then_inc(c_copied, 1)

            def back(u, i):
                tk = tokens(u, i)
                own = Steps(act, own_b["act"])

                def sigmoid_parts(g, dst, at):
                    own.mark(A(dst, g, ACT.Abs))
                    own.wait()
                    own.mark(A(dst, dst, ACT.Exp, scale=-1.0))
                    own.wait()
                    A(dst, dst, ACT.Ln, bias=1.0).then_inc(sig_out, 1)
                    yield at + 2
                    act.wait_ge(sig_in, nth(i, 0, 1, u))
                    A(dst, dst, ACT.Exp).then_inc(sig_out, 1)

                yield 0.5
                copy_turn(u, "b", nth(i, 0, TB, u)).then_inc(turn_copied["b"], 1)
                yield 2
                softmax_exp(u, tk, "b", nth(i, 0, 2, u), MEM, pr4)
                yield 3.5
                act.wait_ge(g_prod, nth(i, 0, 1, u))
                A(gs[u][:tk, :], PS[u][:tk, 1, 0:E], ACT.Copy).then_inc(g_copied, 1)
                yield 4
                act.wait_ge(sh_prod, nth(i, 0, 1, u))
                A(qS[u][:], PS[u][:, 2, 0:TOK], ACT.Copy, scale=QSCALE1)
                A(kS[u][:], PS[u][:, 2, TOK:2 * TOK], ACT.Copy)
                A(z1S[u][:LOW, :], PS[u][:LOW, 2, 2 * TOK:3 * TOK], ACT.Copy).then_inc(sh_copied, 1)
                yield 5.5
                act.wait_ge(vs_prod, nth(i, 0, 1, u))
                A(vsh[u][:tk, :], PS[u][:tk, 3, 0:E], ACT.Copy).then_inc(sh_copied, 1)
                yield 6.5
                act.wait_ge(g_copied, nth(i, 0, 1, u))
                yield from sigmoid_parts(gs[u][:tk, :], egs[u][:tk, :], 9)
                yield 10.8
                act.wait_ge(gathered, nth(i, 0, 1, u))
                A(xg[u][:], PS[u][:, 1, :], ACT.Copy).then_inc(xg_copied, 1)
                yield 11.4
                act.wait_ge(oh_turned, nth(i, 0, 1, u))
                A(ohT[u][:], PS[u][:, 3, 0:PAIRM * TOK], ACT.Copy).then_inc(oh_copied, 1)
                yield 12.5
                act.wait_ge(z1_prod, nth(i, 0, 1, u))
                A(z1M[u][:LOW, :], PS[u][:LOW, 0, 0:256], ACT.Copy).then_inc(z1_copied, 1)
                yield 14.5
                act.wait_ge(qm_prod, nth(i, 0, 1, u))
                A(view(qP[u][:], 0, [SEQS, MEM], [1, SEQS], [MEM * SEQS, CAP]), view(PS[u][:, 1, :], 0, [SLOT, MEM], [CAP, SEQS], [1, CAP]),
                  ACT.Copy, scale=QSCALE1)
                A(kM[u][:], PS[u][:, 1, 256:512], ACT.Copy).then_inc(qm_copied, 1)
                yield 16
                act.wait_ge(zabs, nth(i, 0, 1, u))
                own.mark(A(az[u], az[u], ACT.Exp, scale=-1.0))
                own.wait()
                A(az[u], az[u], ACT.Ln, bias=1.0).then_inc(lned, 1)
                yield 17.5
                act.wait_ge(vm_prod, nth(i, 0, 1, u))
                A(vM[u][:], PS[u][:, 2, :], ACT.Copy).then_inc(qm_copied, 1)
                width = SLOT if tk == TOK else tk // S * CAP
                for p, steps in enumerate(M_PARTS):
                    yield (18.5, 19.5, 21)[p]
                    act.wait_ge(exponents, nth(i, p, MP, u))
                    part = steps[0] * MEM * SLOT, [MEM * SLOT, len(steps)], [SLOT, MEM], [1, width]
                    A(view(U[u][:], *part), view(Dp[:], *part), ACT.Exp, scale=1.0 / GATE_NORM).then_inc(dexped_m, 1)
                for p, steps in enumerate(S_PARTS):
                    yield (22.5, 24.5)[p]
                    act.wait_ge(sh_exponents, nth(i, p, SP, u))
                    part = DM + steps[0] * TOK, [TOK, len(steps)], [1, tk]
                    A(view(U[u][:], *part), view(Dp[:], *part), ACT.Exp, scale=1.0 / GATE_NORM).then_inc(dexped[u], 1)
                yield 47
                act.wait_ge(om_prod, nth(i, 0, 1, u))
                A(oM[u][:], PS[u][:, 1, :], ACT.Copy).then_inc(om_copied, 1)
                yield 55.5
                copy_turn(u, "b", nth(i, 1, TB, u)).then_inc(turn_copied["b"], 1)
                yield 60.5
                copy_turn(u, "b", nth(i, 2, TB, u)).then_inc(turn_copied["b"], 1)
                yield 62.5
                softmax_exp(u, tk, "b", nth(i, 1, 2, u), NE1, pr)
                own.end()

            all_groups(act, begin, front, back)

        @block.gpsimd
        def _(pool):
            G = nc.gpsimd
            for u in UU:
                G.memset(vS[u][:], 1.0)
                G.memset(pr4[u][:], -1.0)
                G.memset(AbM[u][:], 0.0)
            G.memset(roots[:], -0.5)
            G.memset(picked[:], 0.0)
            G.memset(zeros[:], 0.0)
            G.memset(Dp[:], FAR).then_inc(pool_ready, 1)
            for u in UU:
                pool.sem_inc(x_stored[u], 16)
            pool.sem_inc(dexped[1], SP)
            pool.wait_ge(pool_ready, 1)

            def inverse_root(u, tk, half, value):
                pool.wait_ge(stats[half], value)
                G.tensor_tensor(rstd[u][:tk, :], ve[u][:tk, :], roots[:tk, 0:1], ALU.pow).then_inc(rstd_ready[half], 1)

            def keys_by_head(u, tk, i, k, at):
                yield at
                pool.wait_ge(qk_copied[k], nth(i, 1, 3, u))
                G.tensor_tensor(view(kPT[u], 8 * TOK, [TOK, 8], [1, tk]), view(kT[u], TOK, [0, 8], [1, tk]),
                                view(C["headmask"], 0, [1, 8], [0, tk]), ALU.mult).then_inc(km_pool[k], 1)

            def begin(u, i):
                yield 67
                inverse_root(u, TOK, "a", nth(i, 0, 1, u))
                yield from keys_by_head(u, TOK, i, 0, 72.5)

            def front(u, i):
                tk = tokens(u, i)
                for k in (0, 1):
                    z = 35 * k - 7
                    yield (-7, 26)[k]
                    pool.wait_ge(landed["l0"], 16)
                    if k == 0:
                        pool.wait_ge(norm["a"], nth(i, 0, 1, u))
                    else:
                        pool.wait_ge(norm["f"], nth(i, 0, LNF, u))
                    G.tensor_tensor(hb[u][:tk, :], (h, xa)[k][u][:tk, :], C[f"bo{k}"][:tk, :], ALU.add).then_inc(res_ready, 1)
                    if k == 1:
                        yield from keys_by_head(u, tk, i, 1, 32)
                    yield 29.5 + z
                    inverse_root(u, tk, "f", nth(i, k, ROOTS, u))
                yield 74.5
                inverse_root(u, tk, "f", nth(i, 2, ROOTS, u))
                yield 77.5
                inverse_root(u, tk, "f", nth(i, 3, ROOTS, u))

            def back(u, i):
                tk = tokens(u, i)
                own = Steps(pool, own_b["pool"])
                seqs = tk // S
                yield 9
                pool.wait_ge(onehot, nth(i, 0, 1, u))
                G.tensor_tensor(view(OHw[u][:tk], 0, [SLOT, MEM], [1, SLOT]), view(OH[u][:tk], 0, [SLOT, MEM], [1, SLOT]),
                                view(w2[u][:tk], 0, [1, MEM], [0, SLOT]), ALU.mult).then_inc(weighted, 1)
                yield 18
                pool.wait_ge(summed_up, nth(i, 0, 1, u))
                pool.wait_ge(dexped[1 - u], (i + 1) * SP)
                for steps in S_PARTS:
                    for t in steps:
                        if t % 5 == 4:
                            yield 18 + t * 0.5
                        last = G.tensor_tensor(view(Dp[:], DM + t * TOK, [S, seqs], [1, t + 1]),
                                               view(Gc[u][:], 256 + t, [S, seqs], [0, t + 1]),
                                               view(Gc[u][:], 256, [S, seqs], [1, t + 1]), ALU.subtract)
                    last.then_inc(sh_exponents, 1)
                for p, steps in enumerate(S_PARTS):
                    yield (24, 28.5)[p]
                    pool.wait_ge(dexped[u], (i + u) * SP + p + 1)
                    e = view(U[u][:], DM + steps[0] * TOK, [TOK, len(steps)], [1, tk])
                    own.mark(G.tensor_tensor(e, e, view(kS[u][:], 0, [0, len(steps)], [1, tk]), ALU.mult))
                    own.wait()
                    yield (26, 29.5)[p]
                    e = view(U[u][:], DM + steps[0] * TOK, [TOK, len(steps)], [S, seqs], [1, S])
                    G.tensor_tensor(e, e, view(qS[u][:], steps[0], [1, len(steps)], [S, seqs], [0, S]), ALU.mult).then_inc(sh_pairs, 1)
                yield 33
                pool.wait_ge(landed["l1"], 16)
                pool.wait_ge(gs_ready, nth(i, 0, 1, u))
                G.tensor_tensor(gs[u][:tk, :], gs[u][:tk, :], C["norm_w"][:tk, :], ALU.mult).then_inc(gs_scaled, 1)
                yield 52
                pool.wait_ge(rms_ms, nth(i, 0, 1, u))
                G.tensor_tensor(rs4[u][:tk, :], mse[u][:tk, :], roots[:tk, 0:4], ALU.pow).then_inc(rms_ready, 1)
                yield 58.2
                inverse_root(u, tk, "b", nth(i, 0, 1, u))
                own.end()

            all_groups(pool, begin, front, back)

        @block.vector
        def _(dve):
            V = nc.vector
            TT, TS, STT = V.tensor_tensor, V.tensor_scalar, V.scalar_tensor_tensor
            dve.wait_ge(pool_ready, 1)
            dve.wait_ge(landed["route"], 16)

            def statistics(own, u, tk, half, src):
                own.wait()
                own.mark(V.bn_stats(st[u][:tk, :], src[u][:tk, :]))
                own.wait()
                own.mark(V.bn_aggr(mv[u][:tk, :], st[u][:tk, :]))
                own.wait()
                TS(ve[u][:tk, :], mv[u][:tk, 1:2], EPS, None, ALU.add).then_inc(stats[half], 1)

            def normalize(u, tk, half, src, dst):
                TS(dst[u][:tk, :], src[u][:tk, :], mv[u][:tk, 0:1], rstd[u][:tk, :], ALU.subtract, ALU.mult).then_inc(norm[half], 1)

            def weighted_norm(own, u, tk, value, src, dst, w, b):
                own.wait()
                own.mark(STT(src[u][:tk, :], src[u][:tk, :], mv[u][:tk, 0:1], C[w][:tk, :], ALU.subtract, ALU.mult))
                own.wait()
                dve.wait_ge(rstd_ready["f"], value)
                return STT(dst[u][:tk, :], src[u][:tk, :], rstd[u][:tk, :], C[b][:tk, :], ALU.mult, ALU.add)

            def top_two(own, u, tk, half, value, n, p, at):
                own.wait()
                own.mark(V.tensor_reduce(mxs[u][:tk, :], lg[u][:tk, 0:n], AX.X, ALU.max))
                own.wait()
                TS(d8[u][:tk, 0:n], lg[u][:tk, 0:n], mxs[u][:tk, :], None, ALU.subtract).then_inc(logits[half], 1)
                yield at
                dve.wait_ge(softmaxed[half], value)
                own.mark(V.reciprocal(rsum[u][:tk, :], ssum[u][:tk, :]))
                own.wait()
                own.mark(TS(p[u][:tk, 0:n], p[u][:tk, 0:n], rsum[u][:tk, :], None, ALU.mult))
                own.wait()
                own.mark(V.max(mx8[u][:tk, :], p[u][:tk, :]))
                own.wait()
                own.mark(V.max_index(ix[u][:tk, :], mx8[u][:tk, :], p[u][:tk, :]))
                own.wait()
                own.mark(V.tensor_copy(ixf[u][:tk, :], ix[u][:tk, 0:2]))
                own.wait()
                if half == "f" or n == MEM:
                    STT(c0[u][:tk, 0:n], C["eight"][:tk, 0:n], ixf[u][:tk, 0:1], p[u][:tk, 0:n], ALU.is_equal, ALU.mult)
                    own.mark(STT(c1[u][:tk, 0:n], C["eight"][:tk, 0:n], ixf[u][:tk, 1:2], p[u][:tk, 0:n], ALU.is_equal, ALU.mult))

            def keys_by_head(u, tk, i, k, at):
                yield at
                dve.wait_ge(landed["l0"], 16)
                dve.wait_ge(qk_copied[k], nth(i, 0, 3, u))
                TT(view(kPT[u], 0, [TOK, 8], [1, tk]), view(kT[u], 0, [0, 8], [1, tk]),
                   view(C["headmask"], 0, [1, 8], [0, tk]), ALU.mult).then_inc(km_dve[k], 1)

            def copy_v(u, tk, i, k, at):
                yield at
                dve.wait_ge(qkv[k], nth(i, 2 - 2 * k, 3, u))
                TT(view(vS[u][:tk], 0, [D0 + 1, H0], [1, D0]), view(PS[u][:tk, 2, :], 0, [D0, H0], [1, D0]),
                   view(C[f"bv{k}"][:tk], 0, [D0, H0], [1, D0]), ALU.add).then_inc(v_copied[k], 1)

            def begin(u, i):
                own = Steps(dve, own_b["dve"])
                yield 65.5
                dve.wait_ge(tok_used[u], i + 1)
                own.mark(V.tensor_copy(h[u][:TOK, :], PS[u][:TOK, 2, 0:E]))
                statistics(own, u, TOK, "a", h)
                yield 67.5
                dve.wait_ge(rstd_ready["a"], nth(i, 0, 1, u))
                dve.wait_ge(x_stored[u], i * 16 + 16)
                normalize(u, TOK, "a", h, xn)
                own.end()
                yield from keys_by_head(u, TOK, i, 0, 72.5)
                yield from copy_v(u, TOK, i, 0, 73.5)

            def front(u, i):
                tk = tokens(u, i)
                own = Steps(dve, own_f["dve"])
                mark, wait = own.mark, own.wait
                for k in (0, 1):
                    z = 35 * k - 7
                    if k == 1:
                        yield from copy_v(u, tk, i, 1, 29)
                        yield from keys_by_head(u, tk, i, 1, 32.5)
                    for b in range(4):
                        yield 8.5 + z + 1.1 * b
                        dve.wait_ge(scores, nth(i, 4 * k + b, 8, u))
                        m = mxh[u][:tk, 4 * b:4 * b + 4]
                        mark(V.tensor_reduce(m, view(PS[u][:tk, b, :], 0, [TOK, 4], [1, tk]), AX.X, ALU.max))
                        wait()
                        TS(m, m, -float(D0) ** -0.5, None, ALU.mult).then_inc(maxed, 1)
                    yield 16.5 + z
                    dve.wait_ge(p_turned, nth(i, 2 * k + 1, 4, u))
                    V.tensor_copy(view(kPT[u][:tk], 8 * TOK, [4 * TOK, 2], [TOK, 4], [1, tk]),
                                  view(PS[u][:tk, 2, :], 0, [512, 2], [TOK, 4], [1, tk])).then_inc(pt_dve, 1)
                    yield 24.5 + z
                    dve.wait_ge(av, nth(i, k, 2, u))
                    mark(V.reciprocal(rden[u][:tk, :], view(PS[u][:tk, 0, :], D0, [D0 + 1, H0])))
                    wait()
                    TT(view(o[u][:tk], 0, [D0, H0], [1, D0]), view(PS[u][:tk, 0, :], 0, [D0 + 1, H0], [1, D0]),
                       view(rden[u][:tk], 0, [1, H0], [0, D0]), ALU.mult).then_inc(attended, 1)
                    yield 28 + z
                    dve.wait_ge(projected["f"], nth(i, k, 2, u))
                    dve.wait_ge(res_ready, nth(i, k, 2, u))
                    dst = (h, xn)[k]
                    mark(TT(dst[u][:tk, :], PS[u][:tk, 1, 0:E], hb[u][:tk, :], ALU.add))
                    statistics(own, u, tk, "f", dst)
                    if k == 0:
                        yield 23.8
                        dve.wait_ge(rstd_ready["f"], nth(i, 0, ROOTS, u))
                        normalize(u, tk, "f", h, xa)
                        dve.wait_ge(norm["f"], nth(i, 0, LNF, u))
                        TT(rq[u][:tk, :], xa[u][:tk, :], C["rope_cos"][:tk, :], ALU.mult)
                        TT(view(rr[u][:tk], 0, [2, 128]), view(xa[u][:tk], 1, [2, 128]), C["rope_sin"][:tk, :], ALU.mult)
                        mark(TT(view(rr[u][:tk], 1, [2, 128]), view(xa[u][:tk], 0, [2, 128]), C["rope_sin"][:tk, :], ALU.mult))
                        wait()
                        TT(view(rr[u][:tk], 0, [2, 128]), view(rq[u][:tk], 0, [2, 128]), view(rr[u][:tk], 0, [2, 128]), ALU.subtract)
                        TT(view(rr[u][:tk], 1, [2, 128]), view(rq[u][:tk], 1, [2, 128]), view(rr[u][:tk], 1, [2, 128]), ALU.add).then_inc(roped, 1)
                    else:
                        yield 58
                        dve.wait_ge(landed["l0f"], 16)
                        weighted_norm(own, u, tk, nth(i, 1, ROOTS, u), xn, xa, "ln1_w", "ln1_b").then_inc(norm["f"], 1)

                yield 59.5
                dve.wait_ge(gate["f"], nth(i, 0, 1, u))
                mark(TT(lg[u][:tk, :], PS[u][:tk, 0, 0:NE0], C["b_gate0"][:tk, :], ALU.add))
                yield from top_two(own, u, tk, "f", nth(i, 0, 1, u), NE0, pr, 60.5)
                wait()
                TT(cw[u][:tk, :], c0[u][:tk, :], c1[u][:tk, :], ALU.add).then_inc(c_ready, 1)
                for j in range(4):
                    yield (64, 65, 66.5, 71)[j]
                    for e in range(2):
                        if j == 0 and e == 0:
                            dve.wait_ge(c_ready, nth(i, 0, 1, u))
                        elif e == 0:
                            dve.wait_ge(exp_read, nth(i, j - 1, 4, u))
                        else:
                            wait()
                        if e == 0:
                            dve.wait_ge(experts, nth(i, j, 4, u))
                        ins = STT(acc[u][:tk, :], PS[u][:tk, 1 + j % 3, e * E:(e + 1) * E], cw[u][:tk, 2 * j + e:2 * j + e + 1],
                                  (xa if (j, e) == (0, 0) else acc)[u][:tk, :], ALU.mult, ALU.add)
                        if e == 0:
                            mark(ins)
                        else:
                            ins.then_inc(exp_read, 1)
                yield 72
                dve.wait_ge(bias_ready, nth(i, 0, 1, u))
                dve.wait_ge(exp_read, nth(i, 3, 4, u))
                mark(TT(acc[u][:tk, :], acc[u][:tk, :], PS[u][:tk, 0, 256:512], ALU.add))
                statistics(own, u, tk, "f", acc)
                yield 75
                mark(weighted_norm(own, u, tk, nth(i, 2, ROOTS, u), acc, xa, "ln2_w", "ln2_b"))
                wait()
                mark(TT(h[u][:tk, :], h[u][:tk, :], xa[u][:tk, :], ALU.add))
                statistics(own, u, tk, "f", h)
                own.end()

            def back(u, i):
                tk = tokens(u, i)
                own = Steps(dve, own_b["dve"])
                mark, wait = own.mark, own.wait
                seqs = tk // S

                def sigmoid(g, e, at):
                    yield at
                    dve.wait_ge(sig_out, nth(i, 0, 2, u))
                    STT(e, g, 0.0, e, ALU.min, ALU.subtract).then_inc(sig_in, 1)
                    yield at + 1.5
                    dve.wait_ge(sig_out, nth(i, 1, 2, u))

                yield 0
                dve.wait_ge(rstd_ready["f"], nth(i, 3, ROOTS, u))
                normalize(u, tk, "b", h, xn)
                yield 1.5
                dve.wait_ge(gate["b"], nth(i, 0, 2, u))
                mark(V.tensor_copy(lg[u][:tk, 0:MEM], PS[u][:tk, 0, 0:MEM]))
                yield from top_two(own, u, tk, "b", nth(i, 0, 2, u), MEM, pr4, 3)
                mark(TS(t9[u][:tk, :], C["eight"][:tk, 0:MEM], ixf[u][:tk, 0:1], None, ALU.is_equal))
                wait()
                STT(rt[u][:tk, :], C["eight"][:tk, 0:MEM], ixf[u][:tk, 1:2], t9[u][:tk, :], ALU.is_equal, ALU.add).then_inc(routed, 1)
                mark(TT(p12[u][:tk, :], mx8[u][:tk, 0:1], mx8[u][:tk, 1:2], ALU.add))
                wait()
                mark(V.reciprocal(rp[u][:tk, :], p12[u][:tk, :]))
                mark(TT(w2[u][:tk, :], c0[u][:tk, 0:MEM], c1[u][:tk, 0:MEM], ALU.add))
                wait()
                mark(TS(w2[u][:tk, :], w2[u][:tk, :], rp[u][:tk, :], None, ALU.mult))
                yield 6.5
                dve.wait_ge(landed["l1"], 16)
                dve.wait_ge(counted, nth(i, 0, 1, u))
                mark(TS(t9[u][:tk, :], PS[u][:tk, 0, 12:16], -float(CAP), 0.0, ALU.add, ALU.max))
                wait()
                mark(TT(s1[u][:tk, :], PS[u][:tk, 0, 8:12], t9[u][:tk, :], ALU.subtract))
                wait()
                mark(STT(vd[u][:tk, :], s1[u][:tk, :], 1.0, rt[u][:tk, :], ALU.is_ge, ALU.mult))
                wait()
                mark(STT(code[u][:tk, :], s1[u][:tk, :], C["seq9"][:tk, :], vd[u][:tk, :], ALU.add, ALU.mult))
                wait()
                TT(view(OH[u][:tk], 0, [SLOT, MEM], [1, SLOT]), view(C["iota64"][:tk], 0, [0, MEM], [1, SLOT]),
                   view(code[u][:tk], 0, [1, MEM], [0, SLOT]), ALU.is_equal).then_inc(onehot, 1)
                yield from sigmoid(gs[u][:tk, :], egs[u][:tk, :], 6.5)
                TT(gs[u][:tk, :], egs[u][:tk, :], gs[u][:tk, :], ALU.mult).then_inc(gs_ready, 1)
                yield 15
                dve.wait_ge(z2_prod, nth(i, 0, 1, u))
                TT(view(zz[u], 0, [SLOT, MEM], [1, SLOT]), view(PS[u][:, 3, :], 0, [SLOT, MEM], [1, SLOT]),
                   view(C["bgk"], 0, [1, MEM], [0, SLOT]), ALU.add)
                mark(TS(zz[u][:, 256:NZ], PS[u][:, 3, 256:NZ], C["bgk"][:, MEM:MEM + 1], None, ALU.add))
                wait()
                STT(az[u], zz[u], -1.0, zz[u], ALU.mult, ALU.max).then_inc(zabs, 1)
                yield 17.5
                dve.wait_ge(lned, nth(i, 0, 1, u))
                mark(STT(lgz[u], zz[u], 0.0, az[u], ALU.min, ALU.subtract))
                wait()
                V.tensor_tensor_scan(Gc[u][:], C["keep"], lgz[u], 0.0, ALU.mult, ALU.add).then_inc(summed_up, 1)
                dve.wait_ge(summed_up, nth(i, 0, 1, u))
                dve.wait_ge(dexped[1 - u], (i + 1) * SP)
                for p, steps in enumerate(M_PARTS):
                    yield (17.7, 18.5, 18.5)[p]
                    for t in steps:
                        last = TT(view(Dp[:], t * MEM * SLOT, [SLOT, MEM], [CAP, seqs], [1, t + 1]),
                                  view(Gc[u][:], t, [SLOT, MEM], [CAP, seqs], [0, t + 1]),
                                  view(Gc[u][:], 0, [SLOT, MEM], [CAP, seqs], [1, t + 1]), ALU.subtract)
                    last.then_inc(exponents, 1)
                width = SLOT if tk == TOK else seqs * CAP
                for p, steps in enumerate(M_PARTS):
                    yield (22.6, 24, 26.5)[p]
                    dve.wait_ge(dexped_m, nth(i, p, MP, u))
                    if p == 0:
                        dve.wait_ge(qm_copied, nth(i, 0, 2, u))
                    e = view(U[u][:], steps[0] * MEM * SLOT, [MEM * SLOT, len(steps)], [SLOT, MEM], [1, width])
                    mark(TT(e, e, view(kM[u][:], 0, [0, len(steps)], [SLOT, MEM], [1, width]), ALU.mult))
                    wait()
                    yield (23.2, 25.3, 27.8)[p]
                    e = view(U[u][:], steps[0] * MEM * SLOT, [SLOT, MEM * len(steps)], [CAP, seqs], [1, CAP])
                    TT(e, e, view(qP[u][:], steps[0] * MEM * SEQS, [SEQS, MEM * len(steps)], [1, seqs], [0, CAP]), ALU.mult).then_inc(mem_prod, 1)
                yield 37.5
                dve.wait_ge(a_prod, nth(i, 0, 2, u))
                for m in range(MEM):
                    p, mp = (m % 2) * SLOT, m // 2
                    last = TT(view(AbM[u][p:p + SLOT], mp * H1 * 128 + (m % 2) * SLOT, [128, H1], [CAP, SEQS], [1, CAP]),
                              view(PS[u][p:p + SLOT, 0, :], mp * H1, [1, H1], [0, SEQS], [PAIRM * H1, CAP]),
                              view(C["bmask9"][p:p + SLOT], 0, [0, H1], [1, SEQS], [0, CAP]), ALU.mult)
                last.then_inc(a_spread, 1)
                yield 40.5
                dve.wait_ge(a_prod, nth(i, 1, 2, u))
                TT(view(AbS[u][:tk], 0, [TOK, H1], [S, SEQS], [1, S]), view(PS[u][:tk, 3, :], 0, [1, H1], [0, SEQS], [4, S]),
                   view(C["bmask17"][:tk], 0, [0, H1], [1, SEQS], [0, S]), ALU.mult).then_inc(a_spread, 1)
                yield 51
                dve.wait_ge(o_prod, nth(i, 0, 1, u))
                mark(V.tensor_copy(oS[u][:tk, :], PS[u][:tk, 2, 0:E]))
                wait()
                mark(TT(sq[u][:tk, :], oS[u][:tk, :], oS[u][:tk, :], ALU.mult))
                wait()
                mark(V.tensor_reduce(ms[u][:tk, :], view(sq[u][:tk], 0, [DV, H1], [1, DV]), AX.X, ALU.add))
                wait()
                TS(mse[u][:tk, :], ms[u][:tk, :], 1.0 / DV, EPS, ALU.mult, ALU.add).then_inc(rms_ms, 1)
                yield 53.5
                dve.wait_ge(gs_scaled, nth(i, 0, 1, u))
                mark(TT(sq[u][:tk, :], oS[u][:tk, :], gs[u][:tk, :], ALU.mult))
                wait()
                dve.wait_ge(rms_ready, nth(i, 0, 1, u))
                TT(view(oS[u][:tk], 0, [DV, H1], [1, DV]), view(sq[u][:tk], 0, [DV, H1], [1, DV]),
                   view(rs4[u][:tk], 0, [1, H1], [0, DV]), ALU.mult).then_inc(gated, 1)
                yield 57
                dve.wait_ge(projected["b"], nth(i, 0, 1, u))
                TT(view(h_all[:tk], (2 * i + u) * E, [1, E]), h[u][:tk, :], PS[u][:tk, 1, 0:E], ALU.add)
                mark(TT(h[u][:tk, :], h[u][:tk, :], PS[u][:tk, 1, 0:E], ALU.add))
                statistics(own, u, tk, "b", h)
                yield 59
                dve.wait_ge(rstd_ready["b"], nth(i, 0, 1, u))
                normalize(u, tk, "b", h, xn)
                yield 61.8
                dve.wait_ge(gate["b"], nth(i, 1, 2, u))
                mark(V.tensor_copy(lg[u][:tk, :], PS[u][:tk, 0, 0:NE1]))
                yield from top_two(own, u, tk, "b", nth(i, 1, 2, u), NE1, pr, 63)
                V.tensor_copy(view(picked[:tk], (2 * i + u) * 4, [1, 2]), ixf[u][:tk, :])
                V.tensor_copy(view(picked[:tk], (2 * i + u) * 4 + 2, [1, 2]), mx8[u][:tk, 0:2])
                own.end()

            all_groups(dve, begin, front, back)

        block_ctx.close()
        phase1.close()
        expert_phase(nc, ctx, PS, C, arena, w_landed, shared_landed, h_all, picked, out_stored, experts_d, x_d, xs_d, y_d, ysh_d, out_d)


def expert_phase(nc, ctx, PS, C, arena, w_landed, shared_landed, h_all, picked, out_stored, experts_d, x_d, xs_d, y_d, ysh_d, out_d):
    def sb(name, shape, dt=F32):
        return ctx.enter_context(nc.sbuf_tensor(name, shape, dt))

    def sem(name):
        return ctx.enter_context(nc.semaphore(name))

    GE = GROUPS * NE1
    rows = sb("token_rows", [128, 2 * GROUPS * E])
    oh = [sb(f"oh{k}", [128, GE]) for k in (0, 1)]
    both, tot, cum, incl, pos = (sb(n, [128, GE]) for n in ("both", "tot", "cum", "incl", "pos"))
    psum_, wgt = sb("p_sum", [128, GROUPS]), [sb(f"wgt{k}", [128, GROUPS]) for k in (0, 1)]
    over, nt, tend, t128 = sb("over", [128, NE1 * FULL]), sb("nt", [128, NE1]), sb("tend", [128, NE1]), sb("t128", [128, NE1])
    posf, posu = sb("posf", [128, 2 * GROUPS]), sb("posu", [128, 2 * GROUPS], U32)
    past, tef, teu = sb("past", [128, TILES * NE1]), sb("tef", [128, TILES + 1]), sb("teu", [128, TILES + 1], mybir.dt.int32)
    shr = sb("shared_rows", [128, GROUPS * E])
    xs, xsT, eg, hm, hmT, y = ([sb(f"{n}{u}", [128, w]) for u in (0, 1)]
                               for n, w in (("xs", E), ("xsT", E), ("ex", FF), ("hm2", FF), ("hmT2", FF), ("y", E)))
    x_back, rout, counts, placed, scattered, tile_exp = (sem(n) for n in (
        "x_back", "rout", "counts", "placed", "scattered", "tile_exp"))
    row_landed, y_stored = [sem(f"row_landed{u}") for u in (0, 1)], [sem(f"y_stored{u}") for u in (0, 1)]
    (r_turned, r_copied, gated, upped, logged, lowered, sigmoided, inner, i_turned, i_copied, downed, y_copied, dstep,
     astep) = (sem(n) for n in (
        "r_turned", "r_copied", "tile_gated", "upped", "logged", "lowered", "sigmoided", "inner", "i_turned",
        "i_copied", "downed", "y_copied", "dve_link", "act_link"))
    fetched = [sem(f"fetched{g}") for g in range(GROUPS)]
    summed, shared_added, shared_back = sem("summed"), sem("shared_added"), [sem(f"shared_back{k}") for k in (0, 1)]
    UU = (0, 1)
    ALL = SHARED + TILES
    LAST = FIRST + TILES
    EARLY_G = FIRST * 128 // TOK

    def stored(t):
        return (t // 2 + 2) * 16

    def loop_half(q, i):
        return i * (UNROLL // 2) + (FIRST + q) // 2

    def rows_of(g):
        return min(TOK, B * S - g * TOK)

    block = ctx.enter_context(nc.Block())

    @block.sync
    def _(sp):
        def load(t, u, src):
            sp.wait_ge(r_turned, t - 1)
            sp.dma_start(xs[u][:], src).then_inc(row_landed[u], 16)

        def store(t, u, dst):
            sp.wait_ge(y_copied, t + 1)
            sp.dma_start(dst, y[u][:]).then_inc(y_stored[u], 16)

        def shared_rows(t):
            k = t if t < FIRST else t - TILES
            return slice(k * 128, (k + 1) * 128)

        for t in range(3):
            if t < 2:
                sp.dma_start(xs[t][:], x_d[shared_rows(t), :]).then_inc(row_landed[t], 16)
            else:
                load(t, t % 2, x_d[shared_rows(t), :])
        for t in range(FIRST):
            k = t + 3 - FIRST
            if k < 0:
                load(t + 3, (t + 3) % 2, x_d[shared_rows(t + 3), :])
                store(t, t % 2, ysh_d[shared_rows(t), :])
            else:
                if k == 0:
                    store(t, t % 2, ysh_d[shared_rows(t), :])
                    sp.wait_ge(scattered, 2 * GROUPS * 16)
                load(t + 3, (t + 3) % 2, xs_d[k * 128:(k + 1) * 128, :])
                if k:
                    store(t, t % 2, ysh_d[shared_rows(t), :])
        with sp.Fori(0, TILES // UNROLL - 1) as i:
            for q in range(UNROLL):
                t, u = i * UNROLL + (FIRST + q), (FIRST + q) % 2
                load(t + 3, 1 - u, xs_d[bass.ds((i * UNROLL + (q + 3)) * 128, 128), :])
                store(t, u, y_d[bass.ds((i * UNROLL + q) * 128, 128), :])
        for t in range(LAST - UNROLL, ALL):
            k = t + 3 - FIRST
            if t + 3 < ALL:
                load(t + 3, (t + 3) % 2, x_d[shared_rows(t + 3), :] if k >= TILES else xs_d[k * 128:(k + 1) * 128, :])
            k = t - FIRST
            store(t, t % 2, ysh_d[shared_rows(t), :] if k >= TILES else y_d[k * 128:(k + 1) * 128, :])
            if t in (LAST, ALL - 1):
                for n in UU:
                    sp.wait_ge(y_stored[n], stored(LAST - 1 - (LAST - 1 - n) % 2 if t == LAST else ALL - 1 - (ALL - 1 - n) % 2))
                for g in (range(EARLY_G) if t == LAST else range(EARLY_G, GROUPS)):
                    sp.dma_start(shr[:rows_of(g), g * E:(g + 1) * E], ysh_d[g * TOK:g * TOK + rows_of(g), :]).then_inc(shared_back[t != LAST], 16)
        for g in range(GROUPS):
            sp.wait_ge(summed, g + 1)
            sp.dma_start(out_d[g * TOK:g * TOK + rows_of(g), :], h_all[:rows_of(g), g, :]).then_inc(out_stored, 16)
        sp.wait_ge(out_stored, GROUPS * 16)

    @block.tensor
    def _(pe):
        mm, tp = nc.tensor.matmul, nc.tensor.transpose
        pe.wait_ge(rout, 1)
        mm(PS[1][:TOK, 3, 0:GE], C["tri"][:TOK, :], both[:TOK, :], start=True, stop=True)
        mm(PS[1][:TOK, 3, GE:2 * GE], C["ones"][:TOK, :], both[:TOK, :], start=True, stop=True).then_inc(counts, 1)

        def turn_rows(u, landed):
            pe.wait_ge(row_landed[u], landed)
            tp(PS[u][:, 0, 0:128], xs[u][:, 0:128], C["turner"])
            tp(PS[u][:, 0, 128:256], xs[u][:, 128:256], C["turner"]).then_inc(r_turned, 1)

        def up(p, u, n, e_at):
            pe.wait_ge(r_copied, n)
            for c in range(KC):
                last = mm(PS[u][:, 1 + p, :], xsT[u][:, c * 128:(c + 1) * 128],
                          view(arena[:], e_at + (p * KC + c) * FF, [1, FF]), start=(c == 0), stop=(c == KC - 1))
            last.then_inc((gated, upped)[p], 1)

        def turn_inner(u, n):
            pe.wait_ge(inner, n)
            for c in range(4):
                last = tp(PS[u][:, 3, c * 128:(c + 1) * 128], hm[u][:, c * 128:(c + 1) * 128], C["turner"])
            last.then_inc(i_turned, 1)

        def down(u, n, e_at, rows_read=None):
            pe.wait_ge(i_copied, n)
            if rows_read is not None:
                pe.wait_ge(r_copied, rows_read)
            for c in range(4):
                last = mm(PS[u][:, 0, 256:512], hmT[u][:, c * 128:(c + 1) * 128],
                          view(arena[:], e_at + 2 * KC * FF + c * E, [1, E]), start=(c == 0), stop=(c == 3))
            last.then_inc(downed, 1)

        def expert_of(j):
            return pe.value_load(teu[0:1, bass.ds(j, 1)], min_val=0, max_val=NE1 * EW)

        def step(t, half, u, e_this, e_next, more):
            if e_next is not None:
                up(0, 1 - u, t + 2, e_next)
            turn_inner(u, t + 1)
            if more:
                if not isinstance(t, int) or t >= 2:
                    pe.wait_ge(y_copied, t - 1)
                turn_rows(u, half * 16 + 32)
            if e_next is not None:
                up(1, 1 - u, t + 2, e_next)
            if isinstance(e_this, tuple):
                e_this = expert_of(*e_this)
            down(u, t + 1, e_this, t + 3 if more else None)

        turn_rows(0, 16)
        turn_rows(1, 16)
        pe.wait_ge(shared_landed, 16)
        up(0, 0, 1, 0)
        up(1, 0, 1, 0)
        for t in range(FIRST):
            if t == 1:
                pe.wait_ge(placed, 1)
            if t == FIRST - 1:
                pe.wait_ge(tile_exp, 1)
                pe.wait_ge(w_landed, NE1 * 16)
            step(t, t // 2, t % 2, 0, expert_of(0) if t == FIRST - 1 else 0, True)
        with pe.Fori(0, TILES // UNROLL) as i:
            e_this = (i * UNROLL,)
            for q in range(UNROLL):
                e_next = expert_of(i * UNROLL + (q + 1))
                step(i * UNROLL + (FIRST + q), loop_half(q, i), (FIRST + q) % 2, e_this, e_next, True)
                e_this = e_next
        for t in range(LAST, ALL):
            step(t, t // 2, t % 2, 0, 0 if t + 1 < ALL else None, t + 2 < ALL)

    @block.scalar
    def _(act):
        A = nc.scalar.activation

        def abs_part(u, n):
            act.wait_ge(gated, n)
            A(eg[u][:], PS[u][:, 1, :], ACT.Abs).then_inc(astep, 1)

        def log_part(u, n):
            act.wait_ge(astep, 2 * n - 1)
            A(eg[u][:], eg[u][:], ACT.Exp, scale=-1.0).then_inc(astep, 1)
            act.wait_ge(astep, 2 * n)
            A(eg[u][:], eg[u][:], ACT.Ln, bias=1.0).then_inc(logged, 1)

        def sigmoid(u, n):
            act.wait_ge(lowered, n)
            A(eg[u][:], eg[u][:], ACT.Exp).then_inc(sigmoided, 1)

        def copy_inner(u, n):
            act.wait_ge(i_turned, n)
            A(hmT[u][:], PS[u][:, 3, :], ACT.Copy).then_inc(i_copied, 1)

        def copy_y(u, n, stored):
            act.wait_ge(downed, n)
            act.wait_ge(y_stored[u], stored)
            A(y[u][:], PS[u][:, 0, 256:512], ACT.Copy).then_inc(y_copied, 1)

        def step(t, half, u, more=True):
            if more:
                abs_part(1 - u, t + 2)
            copy_inner(u, t + 1)
            if more:
                log_part(1 - u, t + 2)
                sigmoid(1 - u, t + 2)
            copy_y(u, t + 1, half * 16 + 16)

        for g in range(GROUPS):
            act.dma_start(rows[:rows_of(g), g * E:(g + 1) * E], x_d[g * TOK:g * TOK + rows_of(g), :]).then_inc(x_back, 16)
        for e in range(EARLY, SLOTS):
            act.dma_start(arena[:, e * EW:(e + 1) * EW], experts_d[:, e * EW:(e + 1) * EW]).then_inc(w_landed, 16)
        abs_part(0, 1)
        log_part(0, 1)
        sigmoid(0, 1)
        for t in range(FIRST):
            step(t, t // 2, t % 2)
        with act.Fori(0, TILES // UNROLL) as i:
            for q in range(UNROLL):
                step(i * UNROLL + (FIRST + q), loop_half(q, i), (FIRST + q) % 2)
        for t in range(LAST, ALL):
            step(t, t // 2, t % 2, t + 1 < ALL)

    @block.gpsimd
    def _(pool):
        G = nc.gpsimd
        for u in UU:
            pool.sem_inc(y_stored[u], 16)
        pool.wait_ge(placed, 1)
        pool.wait_ge(x_back, GROUPS * 16)
        for k in (0, 1):
            for g in range(GROUPS):
                n = rows_of(g)
                G.indirect_dma_start(xs_d, bass.IndirectOffsetOnAxis(posu[:n, k * GROUPS + g:k * GROUPS + g + 1], 0),
                                     rows[:n, g * E:(g + 1) * E], None).then_inc(scattered, 16)
        for u in UU:
            pool.wait_ge(y_stored[u], stored(LAST - 1 - (LAST - 1 - u) % 2))
        for g in range(GROUPS):
            n = rows_of(g)
            for k in (0, 1):
                at = (2 * g + k) * E
                G.indirect_dma_start(rows[:n, at:at + E], None, y_d,
                                     bass.IndirectOffsetOnAxis(posu[:n, k * GROUPS + g:k * GROUPS + g + 1], 0)).then_inc(fetched[g], 16)

    @block.vector
    def _(dve):
        V = nc.vector
        TT, TS, STT = V.tensor_tensor, V.tensor_scalar, V.scalar_tensor_tensor
        n_steps = [0]

        def link(ins):
            ins.then_inc(dstep, 1)
            n_steps[0] += 1
            dve.wait_ge(dstep, n_steps[0])

        T = slice(0, TOK)
        g_of, e_of = [1, GROUPS], [GROUPS, NE1]
        link(TT(psum_[T, :], view(picked[T], 2, [4, GROUPS]), view(picked[T], 3, [4, GROUPS]), ALU.add))
        link(TS(psum_[T, :], psum_[T, :], 1e-20, None, ALU.add))
        link(V.reciprocal(psum_[T, :], psum_[T, :]))
        for k in (0, 1):
            link(TT(wgt[k][T, :], view(picked[T], 2 + k, [4, GROUPS]), psum_[T, :], ALU.mult))
            link(TT(view(oh[k][T], 0, e_of, g_of), view(C["eight"][T], 0, [1, NE1], [0, GROUPS]),
                    view(picked[T], k, [0, NE1], [4, GROUPS]), ALU.is_equal))
            link(TT(view(oh[k][T], 0, e_of, g_of), view(oh[k][T], 0, e_of, g_of), view(C["valid"][T], 0, [0, NE1], g_of), ALU.mult))
        TT(both[T, :], oh[0][T, :], oh[1][T, :], ALU.add).then_inc(rout, 1)

        def copy_rows(u, n):
            dve.wait_ge(r_turned, n)
            V.tensor_copy(xsT[u][:], PS[u][:, 0, 0:256]).then_inc(r_copied, 1)

        copy_rows(0, 1)
        copy_rows(1, 2)
        dve.wait_ge(counts, 1)
        link(V.tensor_copy(tot[T, :], PS[1][T, 3, GE:2 * GE]))
        link(V.tensor_tensor_scan(incl[T, :], C["step_g"][T, :], tot[T, :], 0.0, ALU.mult, ALU.add))
        link(TT(view(over[T], 0, [FULL, NE1], [1, FULL]), view(incl[T], GROUPS - 1, [GROUPS, NE1], [0, FULL]),
                view(C["fills"][T], 0, [0, NE1], [1, FULL]), ALU.is_gt))
        link(V.tensor_reduce(nt[T, :], view(over[T], 0, [FULL, NE1], [1, FULL]), AX.X, ALU.add))
        link(V.tensor_tensor_scan(tend[T, :], C["step_e"][T, :], nt[T, :], 0.0, ALU.mult, ALU.add))
        link(TT(t128[T, :], tend[T, :], nt[T, :], ALU.subtract))
        link(TS(t128[T, :], t128[T, :], 128.0, -1.0, ALU.mult, ALU.add))
        link(TT(pos[T, :], incl[T, :], tot[T, :], ALU.subtract))
        link(TT(pos[T, :], pos[T, :], PS[1][T, 3, 0:GE], ALU.add))
        link(TT(view(pos[T], 0, e_of, g_of), view(pos[T], 0, e_of, g_of), view(t128[T], 0, [1, NE1], [0, GROUPS]), ALU.add))
        for k in (0, 1):
            link(TT(cum[T, :], pos[T, :], oh[k][T, :], ALU.mult))
            link(V.tensor_reduce(posf[T, k * GROUPS:(k + 1) * GROUPS], view(cum[T], 0, g_of, e_of), AX.X, ALU.add))
        V.tensor_copy(posu[T, :], posf[T, :]).then_inc(placed, 1)
        link(TT(view(past[T], 0, [NE1, TILES], [1, NE1]), view(C["tile_no"][T], 0, [1, TILES], [0, NE1]),
                view(tend[T], 0, [0, TILES], [1, NE1]), ALU.is_ge))
        link(V.tensor_reduce(tef[T, 0:TILES], view(past[T], 0, [NE1, TILES], [1, NE1]), AX.X, ALU.add))
        link(TS(tef[T, 0:TILES], tef[T, 0:TILES], float(NE1 - 1), 1.0, ALU.min, ALU.add))
        link(TS(tef[T, 0:TILES], tef[T, 0:TILES], float(EW), None, ALU.mult))
        link(V.memset(tef[T, TILES:TILES + 1], 0.0))
        V.tensor_copy(teu[T, :], tef[T, :]).then_inc(tile_exp, 1)

        own = n_steps[0]

        def lower(u, n):
            dve.wait_ge(logged, n)
            STT(eg[u][:], PS[u][:, 1, :], 0.0, eg[u][:], ALU.min, ALU.subtract).then_inc(lowered, 1)

        def products(u, n):
            dve.wait_ge(sigmoided, n)
            TT(eg[u][:], eg[u][:], PS[u][:, 1, :], ALU.mult).then_inc(dstep, 1)
            dve.wait_ge(upped, n)
            dve.wait_ge(dstep, n + own)
            TT(hm[u][:], eg[u][:], PS[u][:, 2, :], ALU.mult).then_inc(inner, 1)

        def step(t, u, rows_next, more=True):
            if rows_next:
                copy_rows(u, t + 3)
            if more:
                lower(1 - u, t + 2)
                products(1 - u, t + 2)

        lower(0, 1)
        products(0, 1)
        for t in range(FIRST):
            step(t, t % 2, True)
        with dve.Fori(0, TILES // UNROLL) as i:
            for q in range(UNROLL):
                step(i * UNROLL + (FIRST + q), (FIRST + q) % 2, True)
        n_steps[0] += ALL

        def weigh(g):
            n = rows_of(g)
            dve.wait_ge(fetched[g], 32)
            add = lambda k: STT(h_all[:n, g, :], rows[:n, (2 * g + k) * E:(2 * g + k + 1) * E], wgt[k][:n, g:g + 1], h_all[:n, g, :], ALU.mult, ALU.add)
            link(add(0))
            return add(1)

        for t in range(LAST, ALL):
            step(t, t % 2, t + 2 < ALL, t + 1 < ALL)
            if t == LAST + 1:
                for g in range(EARLY_G):
                    dve.wait_ge(shared_back[0], EARLY_G * 16)
                    TT(h_all[:rows_of(g), g, :], h_all[:rows_of(g), g, :], shr[:rows_of(g), g * E:(g + 1) * E], ALU.add).then_inc(shared_added, 1)
        dve.wait_ge(shared_added, EARLY_G)
        for g in range(EARLY_G):
            weigh(g).then_inc(summed, 1)
        for g in range(EARLY_G, GROUPS):
            last = weigh(g)
        link(last)
        dve.wait_ge(shared_back[1], (GROUPS - EARLY_G) * 16)
        for g in range(EARLY_G, GROUPS):
            TT(h_all[:rows_of(g), g, :], h_all[:rows_of(g), g, :], shr[:rows_of(g), g * E:(g + 1) * E], ALU.add).then_inc(summed, 1)


def _pack_arrays(inp, np):
    f = np.float32

    def rows(w):
        k, n = w.shape
        return w.reshape(k // 128, 128, n).transpose(1, 0, 2).reshape(128, -1)

    def row(v, n=128):
        return np.broadcast_to(v.reshape(1, -1), (n, v.size))

    def col(v):
        return v.reshape(-1, 128).T

    tok = np.arange(TOK)
    seq, pos = tok // S, tok % S
    a = {}
    a["w_tok"] = rows(inp["L0_tok_W"])
    a["cls"] = inp["cls_tok"].reshape(1, E)
    a["is_cls"] = (pos == 0).astype(f)[None]
    w = inp["L0_attn_W_qkv"].reshape(H0, 3, D0, E)
    bq = inp["L0_attn_b_qkv"].reshape(H0, 3, D0)
    q, k, v = (w[:, j].reshape(E, E).T for j in range(3))
    a["wqk0"], a["wv0"] = rows(np.concatenate([q, k], 1)), rows(v)
    a["bqk0"] = np.concatenate([col(bq[:, 0].reshape(-1)), col(bq[:, 1].reshape(-1))], 1)
    a["bv0"] = row(bq[:, 2].reshape(-1))
    a["wo0"], a["bo0"] = rows(inp["L0_attn_W_out"].T), row(inp["L0_attn_b_out"])
    a["headmask"] = (np.arange(128)[:, None] // D0 == np.arange(8)[None]).astype(f)
    w, bb = inp["L0_ffn_in_proj_w"], inp["L0_ffn_in_proj_b"]
    a["wqk1"], a["wv1"] = rows(w[:2 * E].T), rows(w[2 * E:].T)
    a["bqk1"], a["bv1"] = col(bb[:2 * E]), row(bb[2 * E:])
    a["wo1"], a["bo1"] = rows(inp["L0_ffn_out_proj_w"].T), row(inp["L0_ffn_out_proj_b"])
    inv = (1.0 / 10000.0 ** (np.arange(0, D0, 2, dtype=f) / f(D0))).astype(f)
    ang = pos.astype(f)[:, None] * inv[None]
    a["rope_cos"] = np.tile(np.repeat(np.cos(ang), 2, axis=1), (1, H0))
    a["rope_sin"] = np.tile(np.sin(ang), (1, H0))
    a["w_gate0"], a["b_gate0"] = rows(inp["L0_ffn_gate_w"].T), row(inp["L0_ffn_gate_b"])
    a["w_exp0"] = rows(inp["L0_ffn_expert_w"].transpose(2, 0, 1).reshape(E, NE0 * E))
    a["b_exp0"] = inp["L0_ffn_expert_b"]
    for n in ("ln1_w", "ln1_b", "ln2_w", "ln2_b"):
        a[n] = row(inp[f"L0_ffn_{n}"])
    a["w_gate1"], a["w_g"] = rows(inp["L1_attn_w_gate"]), rows(inp["L1_attn_w_g"])
    a["wq"], a["wks"], a["wvs"] = rows(inp["L1_attn_w_q"]), rows(inp["L1_attn_w_ks"]), rows(inp["L1_attn_w_vs"])
    a["wgk1s"], a["wgk2s"] = rows(inp["L1_attn_w_gk1s"]), inp["L1_attn_w_gk2s"]
    a["wk"] = rows(inp["L1_attn_w_k"].transpose(1, 0, 2).reshape(E, -1))
    a["wv"] = rows(inp["L1_attn_w_v"].transpose(1, 0, 2).reshape(E, -1))
    a["wgk1"] = rows(inp["L1_attn_w_gk1"].transpose(1, 0, 2).reshape(E, -1))
    a["wgk2"] = inp["L1_attn_w_gk2"].transpose(1, 0, 2).reshape(LOW, -1)
    a["bgk"] = np.concatenate([inp["L1_attn_b_gk"].T, inp["L1_attn_b_gks"][:, None]], 1)
    a["w_o"], a["norm_w"] = rows(inp["L1_attn_w_o"]), row(np.tile(inp["L1_attn_norm_w"], H1))
    same = seq[:, None] == seq[None]
    a["same"] = same.astype(f)
    a["upto"] = (same & (pos[:, None] <= pos[None])).astype(f)
    a["seq9"] = (seq * CAP).astype(f)[:, None]
    a["iota64"] = row(np.arange(1, SLOT + 1, dtype=f))
    slot = np.arange(SLOT)
    a["keep"] = row(np.concatenate([np.tile((slot % CAP != 0) & (slot < SEQS * CAP), MEM), pos != 0]).astype(f))
    a["hsel"] = (np.arange(128)[:, None] // DK == np.arange(FILL_A)[None] % H1).astype(f)
    a["bmask9"] = ((np.arange(128) % SLOT)[:, None] // CAP == np.arange(SEQS)[None]).astype(f)
    a["bmask17"] = (seq[:, None] == np.arange(SEQS)[None]).astype(f)
    a["w_r"] = rows(inp["L1_ffn_Wr"])
    a["turner"] = np.eye(128, dtype=f)
    a["tri"] = (tok[:, None] <= tok[None]).astype(f)
    a["ones"] = np.ones((TOK, TOK), f)
    a["eight"] = row(np.arange(NE1, dtype=f))
    a["valid"] = (np.arange(GROUPS)[None] * TOK + tok[:, None] < B * S).astype(f)
    a["step_g"] = row(np.tile(np.arange(GROUPS) != 0, NE1).astype(f))
    a["step_e"] = row(np.ones(NE1, f))
    a["fills"] = row(np.arange(FULL, dtype=f) * 128)
    a["tile_no"] = row(np.arange(TILES, dtype=f))
    out = {}
    for k, parts in PACKS.items():
        p = np.zeros((128, WIDTH[k]), f)
        at = 0
        for name, wd in parts:
            assert a[name].shape[1] == wd, (name, a[name].shape, wd)
            p[:a[name].shape[0], at:at + wd] = a[name]
            at += wd
        out[k] = p
    return out


def kernel(**inputs):
    import ml_dtypes
    import numpy as np
    import concourse.bacc as bacc
    from concourse.bass_utils import run_bass_kernel_spmd as run

    inp = {k: np.asarray(v) for k, v in inputs.items()}
    packs = _pack_arrays(inp, np)
    x = inp["x"].reshape(B, 4, 16, 4, 16, 3).transpose(0, 1, 3, 2, 4, 5).reshape(B, PATCHES, FEAT)
    xt = np.zeros((GROUPS * SEQS, S, FEAT), x.dtype)
    xt[:B, 1:] = x
    xt = xt.reshape(GROUPS, TOK, FC, 128).transpose(0, 3, 2, 1).reshape(GROUPS, 128, FC * TOK)
    tok = np.arange(TOK)
    same = tok[:, None] // S == tok[None] // S
    masks = np.zeros((128, 2 * TOK + 128), np.float32)
    masks[:TOK, 0:TOK] = np.where(same, 0.0, FAR)
    masks[:TOK, TOK:2 * TOK] = np.where(same & (tok[None] <= tok[:, None]), 0.0, FAR)
    masks[:, 2 * TOK:] = np.eye(128)
    masks = masks.astype(ml_dtypes.bfloat16)

    ew = np.zeros((128, SLOTS, EW), np.float32)
    for n, (shared, routed) in enumerate((("Sg", "Wg"), ("Su", "Wu"))):
        w = np.concatenate([inp[f"L1_ffn_{shared}"][None], inp[f"L1_ffn_{routed}"]])
        ew[:, :, n * KC * FF:(n + 1) * KC * FF] = w.reshape(SLOTS, KC, 128, FF).transpose(2, 0, 1, 3).reshape(128, SLOTS, KC * FF)
    w = np.concatenate([inp["L1_ffn_Sd"][None], inp["L1_ffn_Wd"]])
    ew[:, :, 2 * KC * FF:] = w.reshape(SLOTS, 4, 128, E).transpose(2, 0, 1, 3).reshape(128, SLOTS, 4 * E)

    nc = bacc.Bacc("TRN2", target_bir_lowering=False, num_devices=1)
    arrays = {"in_patches": np.ascontiguousarray(xt), "in_masks": masks, "in_experts": ew.reshape(128, SLOTS * EW), **{f"in_{k}": v for k, v in packs.items()}}
    aps = {k: nc.dram_tensor(k, a.shape, mybir.dt.from_np(a.dtype), kind="ExternalInput").ap() for k, a in arrays.items()}
    out = nc.dram_tensor("out_0_dram", (B * S, E), F32, kind="ExternalOutput").ap()
    x_d = nc.dram_tensor("expert_in", (GROUPS * TOK, E), F32, kind="Internal").ap()
    xs_d = nc.dram_tensor("expert_rows", (TILES * 128, E), F32, kind="Internal").ap()
    ysh_d = nc.dram_tensor("shared_out", (SHARED * 128, E), F32, kind="Internal").ap()
    y_d = nc.dram_tensor("expert_out", (TILES * 128, E), F32, kind="Internal").ap()
    tower_kernel(nc, aps["in_patches"], {k: aps[f"in_{k}"] for k in PACKS}, aps["in_masks"], aps["in_experts"], x_d, xs_d, y_d, ysh_d, out)
    r = run(nc, [arrays], core_ids=[0])
    return r.results[0]["out_0_dram"].reshape(B, S, E)
```
